# Optimizing a Trainium2 kernel written in Bass

```python
import numpy as np
import jax
import jax.numpy as jnp

def _softmax(x, axis=-1):
    return jax.nn.softmax(x, axis=axis)

def _gelu(x):
    return jax.nn.gelu(x, approximate=True)

def _silu(x):
    return jax.nn.silu(x)

def _sigmoid(x):
    return jax.nn.sigmoid(x)

def _layernorm(x, axis=-1, eps=1e-05):
    m = jnp.mean(x, axis=axis, keepdims=True)
    v = jnp.var(x, axis=axis, keepdims=True)
    return (x - m) / jnp.sqrt(v + eps)

def _scatter_add(tgt, idx, src, axis=0):
    return tgt.at[idx].add(src)

def _segment_sum(src, seg, n):
    return jax.ops.segment_sum(src, seg, n)
kernel_name = 'mk_gps_d1_gnn_r8_c30f04'

def setup_inputs(seed: int=0):
    np.random.seed(seed)
    _w = jnp.asarray

    def _rec_inputs():
        import jax
        import jax.numpy as jnp
        _gk = jax.random.key(seed)
        x = -0.0002117 + 1 * jax.random.normal(jax.random.fold_in(_gk, 1), (1250, 512), jnp.float32)
        src = jax.random.randint(jax.random.fold_in(_gk, 2), (20000,), 0, 1250, jnp.int32)
        dst = jnp.minimum((1250 * jax.random.uniform(jax.random.fold_in(_gk, 3), (20000,)) ** 2.0).astype(jnp.int32), 9999)
        _o = jnp.argsort(dst, stable=True)
        src = src[_o]
        dst = dst[_o]
        return (x, src, dst)
    x, src, dst = _rec_inputs()

    def _L0_gnn_setup():
        import jax, jax.numpy as jnp
        import numpy as np
        BN_EPS = 1e-05

        def batch_norm(h, gamma, beta):
            mu = jnp.mean(h, axis=0)
            var = jnp.var(h, axis=0)
            return (h - mu) * jax.lax.rsqrt(var + BN_EPS) * gamma + beta
        key = jax.random.key(seed)
        ks = jax.random.split(key, 6)
        N, E, dim = (6250, 200000, 512)
        hidden = dim * 2
        x = jax.random.normal(ks[0], (N, dim), dtype=jnp.float32)
        edge_index = jax.random.randint(ks[1], (2, E), 0, N, dtype=jnp.int64)
        s1 = 1.0 / np.sqrt(dim)
        s2 = 1.0 / np.sqrt(hidden)
        return {'x': x, 'edge_index': edge_index, 'eps': jnp.float32(0.0), 'W1': jax.random.uniform(ks[2], (dim, hidden), jnp.float32, -s1, s1), 'b1': jnp.zeros((hidden,), jnp.float32), 'g1': jnp.ones((hidden,), jnp.float32), 'be1': jnp.zeros((hidden,), jnp.float32), 'W2': jax.random.uniform(ks[3], (hidden, dim), jnp.float32, -s2, s2), 'b2': jnp.zeros((dim,), jnp.float32), 'g2': jnp.ones((dim,), jnp.float32), 'be2': jnp.zeros((dim,), jnp.float32)}
    _L0_gnn_all = _L0_gnn_setup()
    _L0_gnn_in = {k: v for k, v in _L0_gnn_all.items() if k in ('eps', 'W1', 'b1', 'g1', 'be1', 'W2', 'b2', 'g2', 'be2')}
    del _L0_gnn_all

    def _L0_mix_setup():
        import jax, jax.numpy as jnp
        import numpy as np
        B, S, DM = (4, 1024, 512)
        H = 8
        D = DM // H

        def _feature_map(t):
            return jax.nn.elu(t) + 1.0
        key = jax.random.key(seed)
        ks = jax.random.split(key, 9)
        s = 1.0 / np.sqrt(DM)
        x = jax.random.normal(ks[0], (B, S, DM), dtype=jnp.float32)
        Wq = jax.random.normal(ks[1], (DM, DM), dtype=jnp.float32) * s
        bq = jnp.zeros((DM,), dtype=jnp.float32)
        Wk = jax.random.normal(ks[2], (DM, DM), dtype=jnp.float32) * s
        bk = jnp.zeros((DM,), dtype=jnp.float32)
        Wv = jax.random.normal(ks[3], (DM, DM), dtype=jnp.float32) * s
        bv = jnp.zeros((DM,), dtype=jnp.float32)
        Wp = jax.random.normal(ks[4], (DM, DM), dtype=jnp.float32) * s
        bp = jnp.zeros((DM,), dtype=jnp.float32)
        return {'x': x, 'Wq': Wq, 'bq': bq, 'Wk': Wk, 'bk': bk, 'Wv': Wv, 'bv': bv, 'Wp': Wp, 'bp': bp}
    _L0_mix_all = _L0_mix_setup()
    _L0_mix_in = {k: v for k, v in _L0_mix_all.items() if k in ('Wq', 'bq', 'Wk', 'bk', 'Wv', 'bv', 'Wp', 'bp')}
    del _L0_mix_all

    def _L0_ffn_setup():
        import jax, jax.numpy as jnp
        import numpy as np
        K_ACTIVE = 2
        CAP_FACTOR = 4

        def _route(x, hash_proj, k):
            logits = jnp.einsum('td,hde->hte', x, hash_proj)
            cand = jnp.argmax(logits, axis=-1)
            scores = jnp.take_along_axis(logits, cand[..., None], axis=-1)[..., 0]
            cand_t = cand.T
            scores_t = scores.T
            top_s, top_i = jax.lax.top_k(scores_t, k)
            sel = jnp.take_along_axis(cand_t, top_i, axis=1)
            return sel

        def _moe(x, sel, W1, W2):
            T, d = x.shape
            E = W1.shape[0]
            k = sel.shape[1]
            C = CAP_FACTOR * T * k // E
            se = sel.reshape(-1)
            oh = jax.nn.one_hot(se, E, dtype=jnp.int32)
            pos = jnp.take_along_axis(jnp.cumsum(oh, axis=0) - 1, se[:, None], axis=1)[:, 0]
            keep = pos < C
            posc = jnp.where(keep, pos, 0)
            xr = jnp.repeat(x, k, axis=0)
            xr = jnp.where(keep[:, None], xr, 0.0)
            buf = jnp.zeros((E, C, d), x.dtype).at[se, posc].add(xr)
            h = jax.nn.gelu(jnp.einsum('ecd,edf->ecf', buf, W1), approximate=False)
            y = jnp.einsum('ecf,efd->ecd', h, W2)
            out = y[se, posc] * keep[:, None].astype(x.dtype)
            return out.reshape(T, k, d)
        key = jax.random.key(seed)
        k1, k2, k3, k4 = jax.random.split(key, 4)
        B, S, D, F, E, H = (4, 256, 512, 256, 64, 4)
        hidden_states = jax.random.normal(k1, (B, S, D), dtype=jnp.float32)
        hash_proj = jax.random.normal(k2, (H, D, E), dtype=jnp.float32)
        W1 = jax.random.normal(k3, (E, D, F), dtype=jnp.float32) * (1.0 / np.sqrt(D))
        W2 = jax.random.normal(k4, (E, F, D), dtype=jnp.float32) * (1.0 / np.sqrt(F))
        return {'hidden_states': hidden_states, 'hash_proj': hash_proj, 'W1': W1, 'W2': W2}
    _L0_ffn_all = _L0_ffn_setup()
    _L0_ffn_in = {k: v for k, v in _L0_ffn_all.items() if k in ('hash_proj', 'W1', 'W2')}
    del _L0_ffn_all
    return {'x': x, 'src': src, 'dst': dst, 'L0_gnn_eps': _L0_gnn_in['eps'], 'L0_gnn_W1': _L0_gnn_in['W1'], 'L0_gnn_b1': _L0_gnn_in['b1'], 'L0_gnn_g1': _L0_gnn_in['g1'], 'L0_gnn_be1': _L0_gnn_in['be1'], 'L0_gnn_W2': _L0_gnn_in['W2'], 'L0_gnn_b2': _L0_gnn_in['b2'], 'L0_gnn_g2': _L0_gnn_in['g2'], 'L0_gnn_be2': _L0_gnn_in['be2'], 'L0_mix_Wq': _L0_mix_in['Wq'], 'L0_mix_bq': _L0_mix_in['bq'], 'L0_mix_Wk': _L0_mix_in['Wk'], 'L0_mix_bk': _L0_mix_in['bk'], 'L0_mix_Wv': _L0_mix_in['Wv'], 'L0_mix_bv': _L0_mix_in['bv'], 'L0_mix_Wp': _L0_mix_in['Wp'], 'L0_mix_bp': _L0_mix_in['bp'], 'L0_ffn_hash_proj': _L0_ffn_in['hash_proj'], 'L0_ffn_W1': _L0_ffn_in['W1'], 'L0_ffn_W2': _L0_ffn_in['W2']}

def reference(x, src, dst, L0_gnn_eps, L0_gnn_W1, L0_gnn_b1, L0_gnn_g1, L0_gnn_be1, L0_gnn_W2, L0_gnn_b2, L0_gnn_g2, L0_gnn_be2, L0_mix_Wq, L0_mix_bq, L0_mix_Wk, L0_mix_bk, L0_mix_Wv, L0_mix_bv, L0_mix_Wp, L0_mix_bp, L0_ffn_hash_proj, L0_ffn_W1, L0_ffn_W2):
    import jax
    import jax.numpy as jnp

    def _L0_gnn_ref(x, edge_index, eps, W1, b1, g1, be1, W2, b2, g2, be2):
        import jax, jax.numpy as jnp
        import numpy as np
        BN_EPS = 1e-05

        def batch_norm(h, gamma, beta):
            mu = jnp.mean(h, axis=0)
            var = jnp.var(h, axis=0)
            return (h - mu) * jax.lax.rsqrt(var + BN_EPS) * gamma + beta
        N = x.shape[0]
        src, dst = (edge_index[0], edge_index[1])
        agg = jax.ops.segment_sum(x[src], dst, num_segments=N)
        h = (1.0 + eps) * x + agg
        h = jax.nn.relu(batch_norm(h @ W1 + b1, g1, be1))
        h = h @ W2 + b2
        h = jax.nn.relu(batch_norm(h, g2, be2))
        return x + h

    def _L0_mix_ref(x, Wq, bq, Wk, bk, Wv, bv, Wp, bp):
        import jax, jax.numpy as jnp
        import numpy as np
        B, S, DM = (4, 1024, 512)
        H = 8
        D = DM // H

        def _feature_map(t):
            return jax.nn.elu(t) + 1.0
        b, s, _ = x.shape
        q = _feature_map(x @ Wq + bq).reshape(b, s, H, D)
        k = _feature_map(x @ Wk + bk).reshape(b, s, H, D)
        v = (x @ Wv + bv).reshape(b, s, H, D)
        kv = jnp.einsum('bshd,bshe->bhde', k, v)
        z = 1.0 / jnp.einsum('bshd,bhd->bsh', q, k.sum(axis=1))
        out = jnp.einsum('bshd,bhde,bsh->bshe', q, kv, z)
        out = out.reshape(b, s, H * D)
        return out @ Wp + bp

    def _L0_ffn_ref(hidden_states, hash_proj, W1, W2):
        import jax, jax.numpy as jnp
        import numpy as np
        K_ACTIVE = 2
        CAP_FACTOR = 4

        def _route(x, hash_proj, k):
            logits = jnp.einsum('td,hde->hte', x, hash_proj)
            cand = jnp.argmax(logits, axis=-1)
            scores = jnp.take_along_axis(logits, cand[..., None], axis=-1)[..., 0]
            cand_t = cand.T
            scores_t = scores.T
            top_s, top_i = jax.lax.top_k(scores_t, k)
            sel = jnp.take_along_axis(cand_t, top_i, axis=1)
            return sel

        def _moe(x, sel, W1, W2):
            T, d = x.shape
            E = W1.shape[0]
            k = sel.shape[1]
            C = CAP_FACTOR * T * k // E
            se = sel.reshape(-1)
            oh = jax.nn.one_hot(se, E, dtype=jnp.int32)
            pos = jnp.take_along_axis(jnp.cumsum(oh, axis=0) - 1, se[:, None], axis=1)[:, 0]
            keep = pos < C
            posc = jnp.where(keep, pos, 0)
            xr = jnp.repeat(x, k, axis=0)
            xr = jnp.where(keep[:, None], xr, 0.0)
            buf = jnp.zeros((E, C, d), x.dtype).at[se, posc].add(xr)
            h = jax.nn.gelu(jnp.einsum('ecd,edf->ecf', buf, W1), approximate=False)
            y = jnp.einsum('ecf,efd->ecd', h, W2)
            out = y[se, posc] * keep[:, None].astype(x.dtype)
            return out.reshape(T, k, d)
        B, S, D = hidden_states.shape
        x = hidden_states.reshape(B * S, D)
        sel = _route(x, hash_proj, K_ACTIVE)
        expert_outputs = _moe(x, sel, W1, W2)
        out = expert_outputs.mean(axis=1)
        return out.reshape(B, S, D)
    edge_index = jnp.stack([src, dst])
    xn = _layernorm(x, axis=-1)
    x = x + _L0_gnn_ref(xn, edge_index, L0_gnn_eps, L0_gnn_W1, L0_gnn_b1, L0_gnn_g1, L0_gnn_be1, L0_gnn_W2, L0_gnn_b2, L0_gnn_g2, L0_gnn_be2) + _L0_mix_ref(xn[None], L0_mix_Wq, L0_mix_bq, L0_mix_Wk, L0_mix_bk, L0_mix_Wv, L0_mix_bv, L0_mix_Wp, L0_mix_bp)[0]
    x = x + _L0_ffn_ref(_layernorm(x, axis=-1)[None], L0_ffn_hash_proj, L0_ffn_W1, L0_ffn_W2)[0]
    return x

_drawn_inputs = setup_inputs


def setup_inputs(seed=0):
    import zlib

    import numpy as np

    out = dict(_drawn_inputs(seed))
    spreads = {'L0_gnn_b1': (0.0, 2.0),
     'L0_gnn_g1': (1.0, 0.2),
     'L0_gnn_be1': (0.0, 0.1),
     'L0_gnn_b2': (0.0, 2.0),
     'L0_gnn_g2': (1.0, 0.2),
     'L0_gnn_be2': (0.0, 0.1),
     'L0_mix_bq': (0.0, 2.0),
     'L0_mix_bk': (0.0, 2.0),
     'L0_mix_bv': (0.0, 0.1),
     'L0_mix_bp': (0.0, 0.1)}
    factors = {'L0_mix_Wq': 12.218, 'L0_mix_Wk': 3.862}
    for name, (base, spread) in spreads.items():
        noise = np.random.default_rng([zlib.crc32(name.encode()), seed]).standard_normal(out[name].shape)
        drawn = base * np.exp(spread * noise) if base else spread * noise
        out[name] = jnp.asarray(drawn.astype(out[name].dtype))
    for name, factor in factors.items():
        out[name] = (out[name] * factor).astype(out[name].dtype)
    return out
```

```python
import concourse.bass as bass
from concourse import mybir
from contextlib import ExitStack

F32 = mybir.dt.float32
I32 = mybir.dt.int32
U32 = mybir.dt.uint32
BF16 = mybir.dt.bfloat16
ALU = mybir.AluOpType
ACT = mybir.ActivationFunctionType
AX = mybir.AxisListType

N = 1250
NT = 10
D = 512
HID = 1024
NE = 20000
GE = 384
NG = 53
WIN = 64
AGW = 1316
CH = [(0, 418), (418, 416), (834, 416)]
NEXP = 64
CAP = 156


def rows(i):
    return min(128, N - 128 * i)


class Program:

    def __init__(self, nc, ctx):
        self.nc = nc
        self.ctx = ctx
        self.queue = {e: [] for e in ("pe", "dve", "act", "pool", "sp")}
        self.count = {}
        self.sems = {}

    def sem(self, name):
        if name not in self.sems:
            self.sems[name] = self.ctx.enter_context(self.nc.semaphore("s_" + name))
            self.count[name] = 0
        return self.sems[name]

    def put(self, eng, call, *args, after=(), signal=True, **kw):
        s = self.sem(eng)
        if signal:
            self.count[eng] += 1
        self.queue[eng].append((call, args, kw, list(after), s if signal else None, 1))
        return (eng, self.count[eng])

    def dma(self, eng, name, *args, after=(), indirect=False, **kw):
        s = self.sem(name)
        self.count[name] += 16
        nc = self.nc
        engine = {"sp": nc.sync, "act": nc.scalar, "pool": nc.gpsimd}[eng]
        call = engine.indirect_dma_start if indirect else engine.dma_start
        self.queue[eng].append((call, args, kw, list(after), s, 16))
        return (name, self.count[name])

    def raw(self, eng, fn, after=()):
        self.queue[eng].append((None, fn, None, list(after), None, 0))

    def replay(self, eng, engine):
        seen = {}
        for call, args, kw, after, s, by in self.queue[eng]:
            for name, value in after:
                if seen.get(name, 0) < value:
                    engine.wait_ge(self.sems[name], value)
                    seen[name] = value
            if call is None:
                args(engine)
                continue
            ins = call(*args, **kw)
            if s is not None:
                ins.then_inc(s, by)


def gnn_mix_moe(nc, x_in, src_in, dst_in, w1g, w2g, wqkvp, hp_in, vec_in, brow_in, cst_in, we_in, out):
    xn_d = nc.dram_tensor("xn_rows", [N, D], F32, kind="Internal").ap()
    xx_d = nc.dram_tensor("xx_rows", [N, D], F32, kind="Internal").ap()
    y_d = nc.dram_tensor("y_rows", [2 * N, D], F32, kind="Internal").ap()

    with ExitStack() as ctx:
        def sb(name, shape, dt=F32):
            return ctx.enter_context(nc.sbuf_tensor(name, shape, dt))

        pr = Program(nc, ctx)
        put, dma = pr.put, pr.dma
        mm = nc.tensor.matmul
        V, A, G = nc.vector, nc.scalar, nc.gpsimd

        XA = sb("XA", [128, NT, D])
        RH = sb("RH", [128, 10280])
        RT = sb("RT", [128, 5000])
        RG = sb("RG", [128, 4, AGW])
        RQ = sb("RQ", [128, 5000])
        RW = sb("RW", [128, 8192])
        GX = sb("GX", [128, 3, 3, D])
        EX = sb("EX", [128, 2048])
        TMP = sb("TMP", [128, 4, D])
        CST = sb("CST", [128, 671])
        VEC = sb("VEC", [128, 41])
        BROW = sb("BROW", [128, 3, D])
        KVB = sb("KVB", [128, 4, 128])
        KSB = sb("KSB", [128, 4, 128])
        RS = RW[0:NG, 6144:6144 + GE].bitcast(I32)
        RD = RW[0:NG, 6656:6656 + GE].bitcast(I32)
        RSF = TMP[0:NG, 0, 0:GE]
        RDF = TMP[0:NG, 1, 0:GE]
        ZERO = KVB[:, :, :].rearrange("p r e -> p (r e)")
        EST = sb("EST", [128, 4])
        EROW = sb("EROW", [1, 64])
        EROWI = sb("EROWI", [1, 64], I32)
        FLAG = sb("FLAG", [1, 4])
        FLAGI = sb("FLAGI", [1, 4], I32)
        SIDX = sb("SIDX", [128, 3, NG], I32)
        DREL = sb("DREL", [128, 3, NG])
        DABS = sb("DABS", [128, 3, NG])
        DC = sb("DC", [128, 2])
        IC = sb("IC", [128, 2], I32)
        OH = sb("OH", [128, 2, 3, WIN])
        ST = sb("ST", [128, NT, 6])
        MV = sb("MV", [128, NT, 2])
        RR = sb("RR", [128, NT])
        BST = sb("BST", [128, 2, 3, 6])
        BMV = sb("BMV", [128, 2, 8])
        NBQ = sb("NBQ", [128, 4])
        OPE = sb("OPE", [128, 1])
        TRIB = sb("TRIB", [128, 128], BF16)
        ONEB = sb("ONEB", [128, 128], BF16)
        TIDX = sb("TIDX", [128, 32], I32)
        SCIDX = sb("SCIDX", [128, 32], I32)
        VIDX = sb("VIDX", [128, 2, 32])

        PS = ctx.enter_context(nc.psum_tensor("PS", [128, 8, 512], F32))

        IDN = CST[:, 0:128]
        TRI = CST[:, 128:256]
        IOTA = CST[:, 256:512]
        BD = CST[:, 512:640]
        VAL = CST[:, 640:650]
        AID = CST[:, 650:670]
        M32 = CST[:, 670:671]
        b1, g1, be1 = VEC[:, 0:8], VEC[:, 8:16], VEC[:, 16:24]
        b2, g2, be2, bq = VEC[:, 24:28], VEC[:, 28:32], VEC[:, 32:36], VEC[:, 36:40]

        XN = RH[:, 0:5120].rearrange("p (i d) -> p i d", i=NT)
        KK = XN
        VA = RH[:, 5120:10280].rearrange("p (i r c) -> p i r c", i=NT, r=4)
        H1 = RH[:, 0:10000].rearrange("p (t n) -> p t n", t=8)
        XT = RT[:, :].rearrange("p (k n) -> p k n", k=4)
        H2 = XT
        QT = RQ[:, :].rearrange("p (k n) -> p k n", k=4)
        WQ = RW[:, 0:2048].rearrange("p (k n) -> p k n", k=4)
        WK = RW[:, 2048:4096].rearrange("p (k n) -> p k n", k=4)
        WV = RW[:, 4096:6144].rearrange("p (k n) -> p k n", k=4)
        WP = RW[:, 6144:8192].rearrange("p (k n) -> p k n", k=4)
        W1 = RW[:, 0:4096].rearrange("p (k n) -> p k n", k=4)
        W2 = RW[:, 4096:8192].rearrange("p (k n) -> p k n", k=8)
        HP = RW[:, 0:1024].rearrange("p (k n) -> p k n", k=4)

        free = {b: [] for b in range(8)}

        t_x = [None] * NT
        t_rd = dma("sp", "rd", RD, dst_in[:, :])
        t_rs = dma("sp", "rs", RS, src_in[:, :])
        t_cst = dma("act", "cst", CST[:, :], cst_in[:, :])
        t_vec = dma("act", "vec", VEC[:, :], vec_in[:, :])
        for i in range(NT):
            t_x[i] = dma("sp", f"x{i}", XA[0:rows(i), i, :], x_in[128 * i:128 * i + rows(i), :])
        t_w = {}

        def load_w(eng, nm, after=()):
            j, w = {"k": (0, WK), "v": (1, WV), "q": (2, WQ), "p": (3, WP)}[nm]
            t_w[nm] = dma(eng, "w" + nm, w, wqkvp[j].rearrange("(k p) n -> p k n", p=128), after=after)

        load_w("sp", "k")
        t_brow = dma("sp", "brow", BROW[:, :, :], brow_in.rearrange("p (a d) -> p a d", a=3))

        t_m1 = put("pool", G.memset, MV[:, :, :], 1.0)
        t_m2 = put("pool", G.memset, VA[:, :, :, 128:129], 1.0)
        t_m3 = put("pool", G.memset, ONEB[:, :], 1.0)
        t_m4 = put("pool", G.memset, ZERO, 0.0)
        t_gz = put("pool", G.memset, RG[:, :, N:AGW], 0.0)
        a = put("dve", V.tensor_copy, RDF, RD, after=[t_rd])
        b = put("dve", V.tensor_copy, RSF, RS, after=[t_rs])
        c = put("dve", V.tensor_reduce, EST[0:NG, 0:1], RDF, AX.X, ALU.min, after=[a])
        d = put("dve", V.tensor_reduce, EST[0:NG, 1:2], RDF, AX.X, ALU.max, after=[a])
        e = put("dve", V.tensor_tensor, EST[0:NG, 2:3], EST[0:NG, 1:2], EST[0:NG, 0:1], ALU.subtract, after=[c, d])
        for j in range(3):
            m = put("pe", nc.tensor.transpose, PS[:, 3, 64 * j:64 * j + NG], RDF[:, 128 * j:128 * j + 128],
                    IDN[0:NG, 0:NG], after=[a, t_cst], signal=(j == 2))
        pv = PS[:, 3, 0:192].rearrange("p (j g) -> p j g", j=3)[:, :, 0:NG]
        t_dabs = put("dve", V.tensor_copy, DABS[:, :, :], pv, after=[m])
        free[3] = [t_dabs]
        f = put("dve", V.tensor_scalar, RDF, RDF, EST[0:NG, 0:1], None, ALU.subtract, after=[c, d, m])
        for j in range(3):
            put("pe", nc.tensor.transpose, PS[:, 0, 64 * j:64 * j + NG], RDF[:, 128 * j:128 * j + 128],
                IDN[0:NG, 0:NG], after=[f, b, t_cst], signal=False)
            put("pe", nc.tensor.transpose, PS[:, 1, 64 * j:64 * j + NG], RSF[:, 128 * j:128 * j + 128],
                IDN[0:NG, 0:NG], signal=False)
        put("pe", nc.tensor.transpose, PS[0:1, 2, 0:NG], EST[0:NG, 0:1], IDN[0:NG, 0:NG], after=[e], signal=False)
        m = put("pe", nc.tensor.transpose, PS[0:1, 2, 64:64 + NG], EST[0:NG, 2:3], IDN[0:NG, 0:NG])
        pv = PS[:, 0, 0:192].rearrange("p (j g) -> p j g", j=3)[:, :, 0:NG]
        t_drel = put("dve", V.tensor_copy, DREL[:, :, :], pv, after=[m])
        pv = PS[:, 1, 0:192].rearrange("p (j g) -> p j g", j=3)[:, :, 0:NG]
        t_sidx = put("dve", V.tensor_copy, SIDX[:, :, :], pv, after=[m])
        t_erow = put("dve", V.tensor_copy, EROWI[0:1, 0:NG], PS[0:1, 2, 0:NG], after=[m])
        s = put("dve", V.tensor_reduce, FLAG[0:1, 0:1], PS[0:1, 2, 64:64 + NG], AX.X, ALU.max, after=[m])
        t_flag = put("dve", V.tensor_copy, FLAGI[0:1, 0:1], FLAG[0:1, 0:1], after=[s])
        free[0] = [t_drel]
        free[1] = [t_sidx]
        free[2] = [t_flag]
        t_edges = [a, b]

        t_xn, t_xns, t_xt, t_acc = [], [], [], []
        ring = 0
        t_r = {}
        for h in range(6):
            if h < 5:
                for i in (2 * h, 2 * h + 1):
                    n = rows(i)
                    s = put("dve", V.bn_stats, ST[0:n, i, :], XA[0:n, i, :], after=[t_x[i], t_m1])
                    s = put("dve", V.bn_aggr, MV[0:n, i, :], ST[0:n, i, :], after=[s])
                hs = slice(2 * h, 2 * h + 2)
                s = put("dve", V.tensor_scalar, RR[:, hs], MV[:, hs, 1], 1e-5, None, ALU.add, after=[s])
                t_r[h] = put("act", A.activation, RR[:, hs], RR[:, hs], ACT.Sqrt, after=[s])
            if h == 0:
                continue
            hs = slice(2 * h - 2, 2 * h)
            s = put("dve", V.reciprocal, RR[:, hs], RR[:, hs], after=[t_r[h - 1]])
            for i in (2 * h - 2, 2 * h - 1):
                n = rows(i)
                t = put("dve", V.tensor_scalar, XN[0:n, i, :], XA[0:n, i, :], MV[0:n, i, 0:1], RR[0:n, i:i + 1],
                        ALU.subtract, ALU.mult, after=[s])
                t_xn.append(t)
                t_xns.append(dma("sp", "xns", xn_d[128 * i:128 * i + n, :], XN[0:n, i, :], after=[t]))
                bk = ring % 4
                ring += 1
                for k in range(4):
                    p = put("pe", nc.tensor.transpose, PS[:, bk, 128 * k:128 * k + n],
                            XN[0:n, i, 128 * k:128 * k + 128], IDN[0:n, 0:n], after=[t, t_cst] + free[bk],
                            signal=(k == 3))
                pv = PS[:, bk, :].rearrange("p (k n) -> p k n", k=4)[:, :, 0:n]
                t = put("act", A.copy, XT[:, :, 128 * i:128 * i + n], pv, after=[p])
                t_xt.append((p, t))
                free[bk] = [t]
        load_w("sp", "v")
        load_w("sp", "q")
        load_w("sp", "p", t_edges)
        t_yz = []
        for i in range(20):
            n = min(128, 2 * N - 128 * i)
            t_yz.append(dma("sp", "yz", y_d[128 * i:128 * i + n, :], ZERO[0:n, :], after=[t_m4]))

        t_ope = put("dve", V.tensor_scalar, OPE[:, :], VEC[:, 40:41], 1.0, None, ALU.add, after=[t_vec])
        t_nbq = put("dve", V.tensor_scalar, NBQ[:, :], bq, -1.0, None, ALU.mult, after=[t_vec])
        t_ag0 = put("dve", V.tensor_scalar, RG[:, :, 0:N], XT[:, :, :], OPE[:, 0:1], None, ALU.mult,
                    after=[t_xt[-1][1], t_ope, t_gz])

        t_gx, t_gdone = [], [None] * NG

        def gather(g):
            for j in range(1 if g == NG - 1 else 3):
                n = 32 if g == NG - 1 else 128
                t = dma("pool", f"gx{g % 3}", out=GX[0:n, g % 3, j, :], out_offset=None, in_=xn_d[:, :],
                        in_offset=bass.IndirectOffsetOnAxis(ap=SIDX[0:n, j, g:g + 1], axis=0), indirect=True,
                        after=([t_xns[-1], t_sidx] if g < 3 else [t_gdone[g - 3]]))
            t_gx.append(t)

        t_ohfree = [None, None]
        t_agg = []
        regs = {}

        def onehot(g):
            o = g % 2
            n = 32 if g == NG - 1 else 128
            nj = 1 if g == NG - 1 else 3
            return put("dve", V.tensor_tensor, OH[0:n, o, 0:nj, :],
                       DREL[0:n, 0:nj, g:g + 1].broadcast_to([n, nj, WIN]),
                       IOTA[0:n, 0:WIN].unsqueeze(1).broadcast_to([n, nj, WIN]), ALU.is_equal,
                       after=[t_drel, t_cst] + ([t_ohfree[o]] if t_ohfree[o] else []))

        t_hot = {}

        def aggregate(g):
            o = g % 2
            n = 32 if g == NG - 1 else 128
            nj = 1 if g == NG - 1 else 3
            t_oh = t_hot.pop(g)
            bk = 4 + o
            for f4 in range(4):
                for j in range(nj):
                    last = f4 == 3 and j == nj - 1
                    p = put("pe", mm, PS[:, bk, WIN * f4:WIN * f4 + WIN], GX[0:n, g % 3, j, 128 * f4:128 * f4 + 128],
                            OH[0:n, o, j, :], start=(j == 0), stop=(j == nj - 1),
                            after=[t_gx[g], t_oh] + free[bk], signal=last)
            t_gdone[g] = p
            t_ohfree[o] = p
            if g + 3 < NG:
                gather(g + 3)
            if g + 2 < NG:
                t_hot[g + 2] = onehot(g + 2)

            if g % 8 == 0:
                def load(eng, g=g):
                    for q in range(g, min(g + 8, NG)):
                        regs[q] = eng.value_load(EROWI[0:1, q:q + 1], min_val=0, max_val=N - 1)
                pr.raw("dve", load, after=[t_erow])

            def add(bk=bk, g=g):
                win = RG[:, :, bass.ds(regs[g], WIN)]
                return V.tensor_tensor(win, PS[:, bk, 0:4 * WIN].rearrange("p (f w) -> p f w", f=4), win, ALU.add)
            t = put("dve", add, after=[p, t_ag0] + t_agg[-1:])
            t_agg.append(t)
            free[bk] = [t]

        for g in range(3):
            gather(g)

        for i in range(NT):
            n = rows(i)
            t = put("dve", V.tensor_tensor, XA[0:n, i, :], XA[0:n, i, :], XN[0:n, i, :], ALU.add, after=[t_xn[i]])
            t = put("dve", V.tensor_tensor, XA[0:n, i, :], XA[0:n, i, :], BROW[0:n, 2, :], ALU.add, after=[t, t_brow])
            t_acc.append(t)

        mix = [0]

        def bank():
            mix[0] += 1
            return (mix[0] - 1) % 4

        t_tmp = [[], []]
        t_k, t_v, t_q = [None] * NT, [None] * NT, {}

        def k_unit(i):
            n, bk, s = rows(i), bank(), i % 2
            for k in range(4):
                p = put("pe", mm, PS[0:n, bk, :], XT[:, k, 128 * i:128 * i + n], WK[:, k, :], start=(k == 0),
                        stop=(k == 3), after=[t_xt[i][1], t_w["k"]] + free[bk], signal=(k == 3))
            u, w = TMP[0:n, 2 * s, :], TMP[0:n, 2 * s + 1, :]
            a1 = put("dve", V.tensor_tensor, u, PS[0:n, bk, :], BROW[0:n, 0, :], ALU.add,
                     after=[p, t_brow] + t_tmp[s])
            free[bk] = [a1]
            a2 = put("act", A.activation, w, u, ACT.Relu, scale=-1.0, after=[a1] + t_tmp[s])
            a3 = put("act", A.activation, w, w, ACT.Exp, scale=-1.0, after=[a2])

            def finish():
                t_k[i] = put("dve", V.scalar_tensor_tensor, KK[0:n, i, :], u, 0.0, w, ALU.max, ALU.add,
                             after=[a3, t_xt[i][0], t_xns[-1], t_acc[i]])
                t_tmp[s] = [t_k[i]]
            return finish

        def v_unit(i):
            n, bk = rows(i), bank()
            for k in range(4):
                p = put("pe", mm, PS[0:n, bk, :], XT[:, k, 128 * i:128 * i + n], WV[:, k, :], start=(k == 0),
                        stop=(k == 3), after=[t_xt[i][1], t_w["v"]] + free[bk], signal=(k == 3))
            t_v[i] = put("dve", V.tensor_tensor, VA[0:n, i, :, 0:128],
                         PS[0:n, bk, :].rearrange("p (r c) -> p r c", r=4),
                         BROW[0:n, 1, :].rearrange("p (r c) -> p r c", r=4), ALU.add, after=[p, t_m2])
            free[bk] = [t_v[i]]

        t_kv = [None] * 4

        def kv_unit(r):
            bk = 6 + r % 2
            o = 129 * (r // 2)
            for i in range(NT):
                n = rows(i)
                p = put("pe", mm, PS[:, bk, o:o + 129], KK[0:n, i, 128 * r:128 * r + 128], VA[0:n, i, r, :],
                        start=(i == 0), stop=(i == NT - 1), after=[t_k[i], t_v[i]] + free[bk], signal=(i == NT - 1))
            a1 = put("dve", V.tensor_tensor, KVB[:, r, :], PS[:, bk, o:o + 128], BD, ALU.mult, after=[p, t_cst, t_yz[-1]])
            a2 = put("dve", V.tensor_copy, EST[:, 3:4], PS[:, bk, o + 128:o + 129], after=[p] + ([t_kv[r - 1]] if r else []))
            free[bk] = [a2]
            t_kv[r] = put("dve", V.tensor_scalar, KSB[:, r, :], BD, EST[:, 3:4], None, ALU.mult, after=[a1, a2])

        def q_unit(r, c):
            o, w = CH[c]
            bk, s = bank(), (3 * r + c) % 2
            for k in range(4):
                p = put("pe", mm, PS[:, bk, 0:w], WQ[:, k, 128 * r:128 * r + 128], XT[:, k, o:o + w], start=(k == 0),
                        stop=(k == 3), after=[t_xt[-1][1], t_w["q"]] + free[bk], signal=(k == 3))
            e1 = TMP[:, 2 * s, 0:w]
            a1 = put("act", A.activation, e1, PS[:, bk, 0:w], ACT.Relu, bias=NBQ[:, r:r + 1], scale=-1.0,
                     after=[p, t_nbq] + t_tmp[s])
            a2 = put("act", A.activation, e1, e1, ACT.Exp, scale=-1.0, after=[a1])
            a3 = put("dve", V.tensor_scalar, QT[:, r, o:o + w], PS[:, bk, 0:w], bq[:, r:r + 1], 0.0, ALU.add,
                     ALU.max, after=[p, a1])
            free[bk] = [a3]

            def finish():
                t_q[r, c] = put("dve", V.tensor_tensor, QT[:, r, o:o + w], QT[:, r, o:o + w], e1, ALU.add,
                                after=[a2, a3])
                t_tmp[s] = [t_q[r, c]]
            return finish

        t_o = {}

        def o_unit(r, c):
            o, w = CH[c]
            bn, bd = bank(), bank()
            put("pe", mm, PS[:, bd, 0:w], KSB[:, r, :], QT[:, r, o:o + w], start=True, stop=True,
                after=[t_kv[r], t_q[r, c]] + free[bd], signal=False)
            p = put("pe", mm, PS[:, bn, 0:w], KVB[:, r, :], QT[:, r, o:o + w], start=True, stop=True, after=free[bn])
            s = c % 2
            z = TMP[:, 2 * s, 0:w]
            a1 = put("dve", V.reciprocal, z, PS[:, bd, 0:w], after=[p] + t_tmp[s])
            t_o[r, c] = put("dve", V.tensor_tensor, QT[:, r, o:o + w], PS[:, bn, 0:w], z, ALU.mult, after=[a1])
            free[bd], free[bn] = [a1], [t_o[r, c]]
            t_tmp[s] = [t_o[r, c]]

        t_p = [None] * NT
        p_last = [None]

        def p_unit(i):
            n, bk = rows(i), bank()
            for k in range(4):
                p = put("pe", mm, PS[0:n, bk, :], QT[:, k, 128 * i:128 * i + n], WP[:, k, :], start=(k == 0),
                        stop=(k == 3), after=[t_w["p"]] + [t_o[k, c] for c in range(3)] + free[bk], signal=(k == 3))
            t_p[i] = put("dve", V.tensor_tensor, XA[0:n, i, :], PS[0:n, bk, :], XA[0:n, i, :], ALU.add,
                         after=[p, t_acc[i]])
            free[bk] = [t_p[i]]
            p_last[0] = p

        units = [(k_unit, (i,)) for i in range(NT)] + [(v_unit, (i,)) for i in range(NT)]
        units += [(q_unit, (r, c)) for r in range(4) for c in range(3)]
        units += [(kv_unit, (r,)) for r in range(4)]
        units += [(o_unit, (r, c)) for r in range(4) for c in range(3)]
        units += [(p_unit, (i,)) for i in range(NT)]
        g, marks, late = 0, {}, None
        for q in range(2):
            t_hot[q] = onehot(q)
        for u, (fn, args) in enumerate(units):
            if late and fn in (kv_unit, o_unit):
                late()
                late = None
            done = fn(*args)
            marks[fn.__name__] = ("pe", pr.count["pe"])
            if late:
                late()
            late = done
            if u >= 3 and g < NG:
                aggregate(g)
                g += 1
        while g < NG:
            aggregate(g)
            g += 1

        ra = {n: pr.sem("ra_" + n) for n in ("idx", "gx", "row", "one", "sum", "dve", "end")}
        OHW = OH[:, :, :, :].rearrange("p a b c -> p (a b c)")[:, 0:256]
        DABSf = DABS[:, :, :].rearrange("p j g -> p (j g)")
        SIDXf = SIDX[:, :, :].rearrange("p j g -> p (j g)")

        def wide(body):
            def run(eng):
                far = eng.value_load(FLAGI[0:1, 0:1], min_val=0, max_val=N)
                with eng.If(far >= WIN):
                    body(eng)
            return run

        def wide_dve(eng):
            n = [0]

            def link(ins):
                n[0] += 1
                ins.then_inc(ra["dve"], 1)
                eng.wait_ge(ra["dve"], n[0])

            link(V.memset(DABS[:, 1:3, NG - 1:NG], -4096.0))
            link(V.tensor_scalar(DABS[:, 0, NG - 1:NG], DABS[:, 0, NG - 1:NG], 4096.0, M32, ALU.add, ALU.mult))
            link(V.tensor_scalar(DABS[:, 0, NG - 1:NG], DABS[:, 0, NG - 1:NG], -4096.0, None, ALU.add))
            link(V.tensor_scalar(RG[:, :, 0:N], XT[:, :, :], OPE[:, 0:1], None, ALU.mult))
            link(V.memset(RG[:, :, N:AGW], 0.0))
            eng.sem_clear(ra["dve"])
            with eng.Fori(0, 3 * NG) as i:
                n[0] = 0
                link(V.tensor_copy(DC[:, 0:1], DABSf[:, bass.ds(i, 1)]))
                V.tensor_copy(IC[:, 0:1], SIDXf[:, bass.ds(i, 1)]).then_inc(ra["idx"], 1)
                for q in range(5):
                    V.tensor_scalar(OHW, IOTA, DC[:, 0:1], None, ALU.is_equal).then_inc(ra["one"], 1)
                    link(V.tensor_scalar(DC[:, 0:1], DC[:, 0:1], -256.0, None, ALU.add))
                    eng.wait_ge(ra["sum"], q + 1)
                    if q == 4:
                        eng.sem_clear(ra["sum"])
                    win = RG[:, :, 256 * q:256 * q + 256]
                    link(V.tensor_tensor(win, PS[:, 4:6, :].rearrange("p b (f w) -> p (b f) w", f=2), win, ALU.add))
                eng.sem_clear(ra["dve"])
            V.memset(DC[:, 1:2], 0.0).then_inc(ra["end"], 1)

        def wide_pool(eng):
            with eng.Fori(0, 3 * NG):
                eng.wait_ge(ra["idx"], 1)
                eng.sem_clear(ra["idx"])
                G.indirect_dma_start(out=GX[:, 0, 0, :], out_offset=None, in_=xn_d[:, :],
                                     in_offset=bass.IndirectOffsetOnAxis(ap=IC[:, 0:1], axis=0)).then_inc(ra["gx"], 16)
                eng.drain().then_inc(ra["row"], 1)

        def wide_pe(eng):
            with eng.Fori(0, 3 * NG):
                eng.wait_ge(ra["row"], 1)
                eng.sem_clear(ra["row"])
                for q in range(5):
                    eng.wait_ge(ra["one"], q + 1)
                    if q == 4:
                        eng.sem_clear(ra["one"])
                    for f4 in range(4):
                        last = mm(PS[:, 4 + f4 // 2, 256 * (f4 % 2):256 * (f4 % 2) + 256],
                                  GX[:, 0, 0, 128 * f4:128 * f4 + 128], OHW, start=True, stop=True)
                    last.then_inc(ra["sum"], 1)
            eng.wait_ge(ra["end"], 1)

        for eng, body in (("dve", wide_dve), ("pool", wide_pool), ("pe", wide_pe)):
            pr.raw(eng, wide(body), after=[t_flag, t_dabs, t_agg[-1], t_ope])

        t_w1 = dma("sp", "w1", W1, w1g.rearrange("(k p) n -> p k n", p=128), after=[marks["q_unit"], marks["k_unit"]])
        t_w2 = dma("sp", "w2", W2, w2g.rearrange("(k p) n -> p k n", p=128), after=[p_last[0], marks["v_unit"]])

        slots, loads = [], []

        def load_expert(buf, after):
            e = len(loads)
            if e < NEXP:
                s = len(slots) if len(slots) > e else None
                loads.append((buf, dma("sp", f"we{e % 24}", buf, we_in[e], after=after)))

        load_expert(EX[:, :], [])

        def norm(t, s, buf, gam, bet, deps):
            for c, (o, w) in enumerate(CH):
                a1 = put("dve", V.bn_stats, BST[:, s, c, :], buf[:, o:o + w], after=[deps[c]])
            m = BMV[:, s, :]
            a1 = put("dve", V.bn_aggr, m[:, 0:2], BST[:, s, :, :].rearrange("p c k -> p (c k)"), after=[a1])
            a1 = put("dve", V.tensor_scalar, m[:, 2:3], m[:, 1:2], 1e-5, None, ALU.add, after=[a1])
            a1 = put("act", A.activation, m[:, 3:4], m[:, 2:3], ACT.Sqrt, after=[a1])
            a1 = put("dve", V.reciprocal, m[:, 4:5], m[:, 3:4], after=[a1])
            a1 = put("dve", V.tensor_tensor, m[:, 5:6], m[:, 4:5], gam, ALU.mult, after=[a1])
            a1 = put("dve", V.tensor_tensor, m[:, 6:7], m[:, 5:6], m[:, 0:1], ALU.mult, after=[a1])
            a1 = put("dve", V.tensor_tensor, m[:, 7:8], bet, m[:, 6:7], ALU.subtract, after=[a1])
            return put("act", A.activation, buf, buf, ACT.Relu, bias=m[:, 7:8], scale=m[:, 5:6], after=[a1])

        t_bmv = [[], []]
        t_h1 = []
        nb = 0
        for t in range(8):
            deps = []
            for c, (o, w) in enumerate(CH):
                bk = nb % 8
                nb += 1
                for k in range(4):
                    p = put("pe", mm, PS[:, bk, 0:w], W1[:, k, 128 * t:128 * t + 128], RG[:, k, o:o + w],
                            start=(k == 0), stop=(k == 3), after=[t_w1, t_agg[-1], t_o[3, 2], t_kv[3]] + free[bk],
                            signal=(k == 3))
                a1 = put("act", A.activation, H1[:, t, o:o + w], PS[:, bk, 0:w], ACT.Identity, bias=b1[:, t:t + 1],
                         after=[p] + t_bmv[t % 2])
                free[bk] = [a1]
                deps.append(a1)
            t_h1.append(norm(t, t % 2, H1[:, t, :], g1[:, t:t + 1], be1[:, t:t + 1], deps))
            t_bmv[t % 2] = [t_h1[-1]]
        pe_w1 = p
        t_hp = dma("sp", "hp", HP, hp_in.rearrange("(k p) n -> p k n", p=128), after=[pe_w1])
        RGf = RG[:, :, :].rearrange("p k n -> p (k n)")
        load_expert(RGf[:, 0:2048], [pe_w1])
        load_expert(RGf[:, 2048:4096], [pe_w1])
        load_expert(RW[:, 2048:4096], [pe_w1])
        load_expert(RQ[:, 0:2048], [p_last[0]])
        load_expert(RQ[:, 2048:4096], [p_last[0]])

        t_h2 = []
        for t in range(4):
            deps = []
            for c, (o, w) in enumerate(CH):
                bk = nb % 8
                nb += 1
                for k in range(8):
                    p = put("pe", mm, PS[:, bk, 0:w], W2[:, k, 128 * t:128 * t + 128], H1[:, k, o:o + w],
                            start=(k == 0), stop=(k == 7), after=[t_w2, t_h1[k]] + free[bk], signal=(k == 7))
                a1 = put("act", A.activation, H2[:, t, o:o + w], PS[:, bk, 0:w], ACT.Identity, bias=b2[:, t:t + 1],
                         after=[p] + t_bmv[t % 2])
                free[bk] = [a1]
                deps.append(a1)
            t_h2.append(norm(t, t % 2, H2[:, t, :], g2[:, t:t + 1], be2[:, t:t + 1], deps))
            t_bmv[t % 2] = [t_h2[-1]]
        pe_w2 = p
        for q in range(3):
            load_expert(RH[:, 2048 * q:2048 * q + 2048], [pe_w2])
        load_expert(RW[:, 4096:6144], [pe_w2])
        load_expert(RW[:, 6144:8192], [pe_w2])

        RB = RH[:, 6144:10280]
        MX = RB[:, 0:320].rearrange("p (i h e) -> p i h e", i=NT, h=4)
        MI = RB[:, 320:640].bitcast(U32).rearrange("p (i h e) -> p i h e", i=NT, h=4)
        LG = RB[:, 640:1152].rearrange("p (s n) -> p s n", s=2)
        t_rb1 = put("dve", V.memset, RB[:, 0:640], 0.0, after=[pe_w2])
        t_m5 = put("dve", V.memset, MV[:, :, :], 1.0)
        t_xx, t_xxs, t_lgf, t_best = [None] * NT, [None] * NT, [[], []], None
        xxr = [None, None]
        xtr = [None, None]
        st = {}

        def step_a(i):
            n, bk = rows(i), nbank()
            for k in range(4):
                p = put("pe", nc.tensor.transpose, PS[0:n, bk, 128 * k:128 * k + 128], H2[:, k, 128 * i:128 * i + n],
                        IDN, after=[t_h2[k]] + free[bk], signal=(k == 3))
            a1 = put("dve", V.tensor_tensor, XA[0:n, i, :], PS[0:n, bk, :], XA[0:n, i, :], ALU.add,
                     after=[p, t_p[i]])
            free[bk] = [a1]
            a1 = put("dve", V.bn_stats, ST[0:n, i, :], XA[0:n, i, :], after=[a1])
            a1 = put("dve", V.bn_aggr, MV[0:n, i, :], ST[0:n, i, :], after=[a1, t_m5])
            a1 = put("dve", V.tensor_scalar, RR[:, i:i + 1], MV[:, i, 1:2], 1e-5, None, ALU.add, after=[a1])
            st[i] = put("act", A.activation, RR[:, i:i + 1], RR[:, i:i + 1], ACT.Sqrt, after=[a1])
            return p

        nbk = [nb]

        def nbank():
            nbk[0] += 1
            return (nbk[0] - 1) % 8

        def step_b(i):
            n, s = rows(i), i % 2
            a1 = put("dve", V.reciprocal, RR[:, i:i + 1], RR[:, i:i + 1], after=[st[i]])
            wait = [a1] + (xxr[s] or [])
            xx = TMP[0:n, s, :]
            a1 = put("dve", V.tensor_scalar, xx, XA[0:n, i, :], MV[0:n, i, 0:1], RR[0:n, i:i + 1], ALU.subtract,
                     ALU.mult, after=wait)
            t_xxs[i] = dma("sp", f"xxs{s}", xx_d[128 * i:128 * i + n, :], xx, after=[a1])
            bk = nbank()
            for k in range(4):
                p = put("pe", nc.tensor.transpose, PS[:, bk, 128 * k:128 * k + n], xx[:, 128 * k:128 * k + 128],
                        IDN[0:n, 0:n], after=[a1] + free[bk], signal=(k == 3))
            xxr[s] = [p, t_xxs[i]]
            xt = TMP[:, 2 + s, :].rearrange("p (k n) -> p k n", k=4)
            a2 = put("act", A.copy, xt[:, :, 0:n], PS[:, bk, :].rearrange("p (k n) -> p k n", k=4)[:, :, 0:n],
                     after=[p] + (xtr[s] or []))
            free[bk] = [a2]
            st["xt", i] = a2

        def step_c(i):
            n, s, bk = rows(i), i % 2, nbank()
            a2 = st["xt", i]
            xt = TMP[:, 2 + s, :].rearrange("p (k n) -> p k n", k=4)
            for k in range(4):
                p = put("pe", mm, PS[0:n, bk, 0:256], xt[:, k, 0:n], HP[:, k, :], start=(k == 0), stop=(k == 3),
                        after=[a2, t_hp] + free[bk], signal=(k == 3))
            xtr[s] = [p]
            a3 = put("act", A.copy, LG[0:n, s, :], PS[0:n, bk, 0:256], after=[p] + t_lgf[s])
            free[bk] = [a3]
            st["lg", i] = a3
            return p

        def step_d(i):
            n, s = rows(i), i % 2
            for h in range(4):
                l = LG[0:n, s, 64 * h:64 * h + 64]
                a1 = put("dve", V.max, MX[0:n, i, h, :], l, after=[st["lg", i], t_rb1])
                a1 = put("dve", V.max_index, MI[0:n, i, h, :], MX[0:n, i, h, :], l, after=[a1])
            t_lgf[s] = [a1]
            return a1

        for i in range(NT + 4):
            if i < NT:
                p_tr = step_a(i)
            if 0 <= i - 2 < NT:
                step_b(i - 2)
            if 0 <= i - 3 < NT:
                p_lg = step_c(i - 3)
            if 0 <= i - 4 < NT:
                t_best = step_d(i - 4)
        nb = nbk[0]
        load_expert(RW[:, 0:2048], [p_lg])

        S1 = RB[:, 1152:4136]
        off = [0]

        def scr(n):
            off[0] += n
            return S1[:, off[0] - n:off[0]]

        SC8 = scr(80).rearrange("p (i e) -> p i e", i=NT)
        T8 = scr(80).rearrange("p (i e) -> p i e", i=NT)
        TI = scr(80).bitcast(U32).rearrange("p (i e) -> p i e", i=NT)
        CAND = scr(40).rearrange("p (i h) -> p i h", i=NT)
        TOP = scr(20).rearrange("p (i k) -> p i k", i=NT)
        SEL = scr(20).rearrange("p (i k) -> p i k", i=NT)
        PR4 = scr(20).rearrange("p (i k) -> p i k", i=NT)
        SELI = scr(20).bitcast(I32)
        ODD = scr(20)
        PAIR = scr(20)
        POS = scr(20).rearrange("p (i k) -> p i k", i=NT)
        QP = scr(20)
        OHE = RT[:, 0:1280].rearrange("p (i k e) -> p i k e", i=NT, k=2)
        OHS = scr(320).bitcast(BF16).rearrange("p (i e) -> p i e", i=NT)
        PRD = RT[:, 1280:1920].rearrange("p (i e) -> p i e", i=NT)
        CC = RT[:, 1920:2560].rearrange("p (i e) -> p i e", i=NT)
        LQ = RT[:, 0:2560].rearrange("p (a q) -> p a q", a=20)
        RP = RT[:, 2560:3200].rearrange("p (a r) -> p a r", a=20)
        SELf = SEL.rearrange("p i k -> p (i k)")
        POSf = POS.rearrange("p i k -> p (i k)")

        w = [t_best]

        def v(call, *args, after=(), **kw):
            w[0] = put("dve", call, *args, after=[w[0], *after], **kw)
            return w[0]

        v(V.memset, SC8[:, :, 4:8], -3.0e38)
        v(V.tensor_copy, SC8[:, :, 0:4], MX[:, :, :, 0])
        v(V.tensor_copy, CAND, MI[:, :, :, 0])
        for i in range(NT):
            v(V.max, T8[:, i, :], SC8[:, i, :])
            v(V.max_index, TI[:, i, :], T8[:, i, :], SC8[:, i, :])
        v(V.tensor_copy, TOP, TI[:, :, 0:2])
        for h in range(4):
            dst = SEL if h == 0 else PR4
            v(V.scalar_tensor_tensor, dst, TOP, float(h), CAND[:, :, h:h + 1].broadcast_to([128, NT, 2]),
              ALU.is_equal, ALU.mult)
            if h:
                v(V.tensor_tensor, SEL, SEL, PR4, ALU.add)
        v(V.scalar_tensor_tensor, SEL, VAL.unsqueeze(2).broadcast_to([128, NT, 2]), -1000.0, SEL, ALU.mult, ALU.add)
        v(V.tensor_tensor, OHE, IOTA[:, 0:NEXP].unsqueeze(1).broadcast_to([128, 20, NEXP]).rearrange(
            "p (i k) e -> p i k e", k=2) if False else IOTA[:, 0:NEXP].unsqueeze(1).unsqueeze(1).broadcast_to(
            [128, NT, 2, NEXP]), SEL.unsqueeze(3).broadcast_to([128, NT, 2, NEXP]), ALU.is_equal,
          after=[p_tr])
        a0 = v(V.tensor_tensor, OHS, OHE[:, :, 0, :], OHE[:, :, 1, :], ALU.add)
        b0 = put("dve", V.tensor_copy, TRIB[:, :], TRI)
        for i in range(NT):
            bk = (nb + i // 5) % 8
            o = 64 * (i % 5)
            for j in range(i):
                put("pe", mm, PS[:, bk, o:o + 64], ONEB[:, :], OHS[:, j, :], start=(j == 0), stop=False,
                    after=[a0, t_m3] + free[bk], signal=False)
            p = put("pe", mm, PS[:, bk, o:o + 64], TRIB[:, :], OHS[:, i, :], start=(i == 0), stop=True,
                    after=[a0, b0] + free[bk])
        c0 = []
        for h in range(2):
            bk = (nb + h) % 8
            c0.append(v(V.tensor_copy, CC[:, 5 * h:5 * h + 5, :],
                        PS[:, bk, 0:320].rearrange("p (i e) -> p i e", i=5), after=[p]))
            free[bk] = [c0[-1]]
        nb += 2
        for k in range(2):
            v(V.tensor_tensor, PRD, OHE[:, :, k, :], CC, ALU.mult)
            v(V.tensor_reduce, POS[:, :, k:k + 1], PRD, AX.X, ALU.add)
        v(V.tensor_tensor, PR4[:, :, 0:1], SEL[:, :, 0:1], SEL[:, :, 1:2], ALU.is_equal)
        v(V.tensor_tensor, POS[:, :, 1:2], POS[:, :, 1:2], PR4[:, :, 0:1], ALU.add)
        a0 = v(V.tensor_reduce, EST[:, 3:4], POSf, AX.X, ALU.max)
        bk = nb % 8
        nb += 1
        p = put("pe", nc.tensor.transpose, PS[0:1, bk, 0:128], EST[:, 3:4], IDN, after=[a0] + free[bk])
        a0 = put("dve", V.tensor_reduce, FLAG[0:1, 1:2], PS[0:1, bk, 0:128], AX.X, ALU.max, after=[p])
        free[bk] = [a0]
        t_full = put("dve", V.tensor_copy, FLAGI[0:1, 1:2], FLAG[0:1, 1:2], after=[a0])
        v(V.tensor_copy, SELI, SELf)
        v(V.tensor_scalar, ODD.bitcast(I32), SELI, 1, None, ALU.bitwise_and)
        v(V.tensor_scalar, PAIR.bitcast(I32), SELI, 1, None, ALU.arith_shift_right)
        v(V.tensor_copy, ODD, ODD.bitcast(I32))
        v(V.tensor_copy, PAIR, PAIR.bitcast(I32))
        v(V.scalar_tensor_tensor, QP, ODD, 64.0, POSf, ALU.mult, ALU.add)
        v(V.tensor_scalar, ODD, POSf, 64.0, 1000.0, ALU.is_ge, ALU.mult)
        v(V.tensor_tensor, QP, QP, ODD, ALU.add)
        bk = nb % 8
        nb += 1
        for h in range(2):
            hs = slice(10 * h, 10 * h + 10)
            v(V.tensor_tensor, RP[:, hs, :], IOTA[:, 0:32].unsqueeze(1).broadcast_to([128, 10, 32]),
              PAIR[:, hs].unsqueeze(2).broadcast_to([128, 10, 32]), ALU.is_equal)
            v(V.tensor_tensor, RP[:, hs, :], RP[:, hs, :], AID[:, hs].unsqueeze(2).broadcast_to([128, 10, 32]),
              ALU.mult)
            v(V.tensor_tensor, LQ[:, hs, :], IOTA[:, 0:128].unsqueeze(1).broadcast_to([128, 10, 128]),
              QP[:, hs].unsqueeze(2).broadcast_to([128, 10, 128]), ALU.is_equal)
            for j in range(10 * h, 10 * h + 10):
                p = put("pe", mm, PS[:, bk, 0:32], LQ[:, j, :], RP[:, j, :], start=(j == 0), stop=(j == 19),
                        after=[w[0]] + free[bk], signal=(j == 19))
        v(V.tensor_copy, VIDX[:, 0, :], PS[:, bk, 0:32], after=[p])
        free[bk] = [w[0]]
        p_idx = p
        v(V.tensor_scalar, VIDX[:, 1, :], VIDX[:, 0, :], 1.0, -1.0, ALU.max, ALU.add)
        v(V.tensor_copy, TIDX[:, :], VIDX[:, 1, :])
        t_tidx = v(V.tensor_scalar, TIDX[:, :], TIDX[:, :], 1, None, ALU.arith_shift_right)
        v(V.tensor_scalar, VIDX[:, 1, :], VIDX[:, 0, :], 0.5, 8192.0, ALU.is_lt, ALU.mult)
        v(V.scalar_tensor_tensor, VIDX[:, 1, :], VIDX[:, 0, :], -1.0, VIDX[:, 1, :], ALU.add, ALU.add)
        t_scidx = v(V.tensor_copy, SCIDX[:, :], VIDX[:, 1, :])
        load_expert(RT[:, 0:2048], [p_idx, w[0]])
        load_expert(RT[:, 2048:4096], [p_idx])

        GXf = GX[:, :, :, :].rearrange("p a b c -> p (a b c)")
        XG = GXf[:, 0:1536].rearrange("p (s d) -> p s d", s=3)
        XTT = GXf[:, 1536:2560].rearrange("p (s d) -> p s d", s=2)
        HT = GXf[:, 2560:3072].rearrange("p (s d) -> p s d", s=2)
        YS = GXf[:, 3072:4608].rearrange("p (s d) -> p s d", s=3)
        t_xg, xg_free = {}, {}

        def gather_pair(r):
            s = r % 3
            t_xg[r] = dma("pool", f"xg{s}", out=XG[:, s, :], out_offset=None, in_=xx_d[:, :],
                          in_offset=bass.IndirectOffsetOnAxis(ap=TIDX[:, r:r + 1], axis=0), indirect=True,
                          after=[t_tidx, t_xxs[-1], t_xxs[-2], t_gdone[-1]] + ([xg_free[r - 3]] if r >= 3 else []))

        for r in range(2):
            gather_pair(r)
        st2 = {}

        def tr(r):
            s, bk = r % 2, r % 2
            for k in range(4):
                p = put("pe", nc.tensor.transpose, PS[:, bk, 128 * k:128 * k + 128], XG[:, r % 3, 128 * k:128 * k + 128],
                        IDN, after=[t_xg[r]] + free[bk], signal=(k == 3))
            xg_free[r] = p
            a1 = put("act" if r % 2 else "dve", A.copy if r % 2 else V.tensor_copy, XTT[:, s, :], PS[:, bk, :],
                     after=[p] + ([st2["h", r - 2][1]] if r >= 2 else []))
            free[bk] = [a1]
            st2["x", r] = a1

        def up(r):
            s, bk = r % 2, 2 + r % 2
            for j in range(2):
                buf, t_e = loads[2 * r + j]
                for f2 in range(2):
                    for k in range(4):
                        p = put("pe", mm, PS[:, bk, 128 * j + 64 * f2:128 * j + 64 * f2 + 64],
                                buf[:, 256 * k + 128 * f2:256 * k + 128 * f2 + 128],
                                XTT[:, s, 128 * k + 64 * j:128 * k + 64 * j + 64], start=(k == 0), stop=(k == 3),
                                after=[t_e, st2["x", r]] + free[bk], signal=(j == 1 and f2 == 1 and k == 3))
            a1 = put("act", A.activation, HT[:, s, :], PS[:, bk, 0:256], ACT.Gelu,
                     after=[p] + ([st2["y", r - 2]] if r >= 2 else []))
            free[bk] = [a1]
            st2["h", r] = (a1, p)

        t_ys = {}
        t_sc = []

        def down(r):
            s, bk = r % 2, 4 + r % 2
            for j in range(2):
                buf, t_e = loads[2 * r + j]
                for f2 in range(2):
                    p = put("pe", mm, PS[64 * j:64 * j + 64, bk, :],
                            HT[:, s, 128 * j + 64 * f2:128 * j + 64 * f2 + 64],
                            buf[:, 1024 + 512 * f2:1024 + 512 * f2 + 512], start=(f2 == 0), stop=(f2 == 1),
                            after=[st2["h", r][0]] + free[bk], signal=(j == 1 and f2 == 1))
            st2["y", r] = p
            a1 = put("dve", V.tensor_copy, YS[:, r % 3, :], PS[:, bk, :],
                     after=[p] + ([t_ys[r - 3]] if r >= 3 else []))
            free[bk] = [a1]
            t_ys[r] = dma("pool", f"ys{r % 3}", out=y_d[:, :], out_offset=bass.IndirectOffsetOnAxis(
                ap=SCIDX[:, r:r + 1], axis=0), in_=YS[:, r % 3, :], in_offset=None, bounds_check=2 * N - 1,
                oob_is_err=False, indirect=True, after=[a1, t_scidx, t_yz[-1]])
            for j in range(2):
                load_expert(loads[2 * r + j][0], [p])

        for r in range(34):
            if r < 32:
                tr(r)
            if 0 <= r - 1 < 32:
                up(r - 1)
            if r + 2 < 32:
                gather_pair(r + 2)
            if 0 <= r - 2 < 32:
                down(r - 2)

        M2 = CAP - 64
        fu = {n: pr.sem("fu_" + n) for n in
              ("load", "idx", "w", "row", "xt", "xc", "up", "gelu", "down", "yc", "sc", "xg", "ys", "hid", "dve", "tab", "end")}
        L2 = RH[:, 0:20 * M2].rearrange("p (a q) -> p a q", a=20)
        R2 = RH[:, 2048:2048 + 20 * NEXP].rearrange("p (a e) -> p a e", a=20)
        V2 = RH[0:M2, 4096:4096 + NEXP]
        V3 = RH[0:M2, 4160:4160 + NEXP]
        T2 = RH[0:M2, 4224:4224 + NEXP].bitcast(I32)
        S2 = RH[0:M2, 4288:4288 + NEXP].bitcast(I32)
        IT, IS = RH[0:M2, 4352:4353].bitcast(I32), RH[0:M2, 4353:4354].bitcast(I32)

        def full(body):
            def run(eng):
                most = eng.value_load(FLAGI[0:1, 1:2], min_val=0, max_val=2 * N)
                with eng.If(most >= 64):
                    body(eng)
            return run

        def take(eng, name, value):
            eng.wait_ge(fu[name], value)
            eng.sem_clear(fu[name])

        def full_dve(eng):
            n = [0]

            def link(ins):
                n[0] += 1
                ins.then_inc(fu["dve"], 1)
                eng.wait_ge(fu["dve"], n[0])

            link(V.tensor_scalar(QP, POSf, -64.0, None, ALU.add))
            link(V.tensor_tensor(L2, IOTA[:, 0:M2].unsqueeze(1).broadcast_to([128, 20, M2]),
                                 QP.unsqueeze(2).broadcast_to([128, 20, M2]), ALU.is_equal))
            link(V.tensor_tensor(R2, IOTA[:, 0:NEXP].unsqueeze(1).broadcast_to([128, 20, NEXP]),
                                 SELf.unsqueeze(2).broadcast_to([128, 20, NEXP]), ALU.is_equal))
            link(V.tensor_tensor(R2, R2, AID.unsqueeze(2).broadcast_to([128, 20, NEXP]), ALU.mult))
            V.memset(DC[:, 0:1], 0.0).then_inc(fu["tab"], 1)
            take(eng, "up", 1)
            link(V.tensor_copy(V2, PS[0:M2, 0, 0:NEXP]))
            link(V.tensor_scalar(V3, V2, 1.0, -1.0, ALU.max, ALU.add))
            link(V.tensor_copy(T2, V3))
            link(V.tensor_scalar(T2, T2, 1, None, ALU.arith_shift_right))
            link(V.tensor_scalar(V3, V2, 0.5, 8192.0, ALU.is_lt, ALU.mult))
            link(V.scalar_tensor_tensor(V3, V2, -1.0, V3, ALU.add, ALU.add))
            link(V.tensor_copy(S2, V3))
            eng.sem_clear(fu["dve"])
            with eng.Fori(0, NEXP) as e:
                n[0] = 0
                link(V.tensor_copy(IT, T2[:, bass.ds(e, 1)]))
                link(V.tensor_copy(IS, S2[:, bass.ds(e, 1)]))
                eng.sem_clear(fu["dve"])
                V.memset(DC[:, 0:1], 0.0).then_inc(fu["load"], 1)
                V.memset(DC[:, 1:2], 0.0).then_inc(fu["idx"], 1)
                take(eng, "xt", 1)
                V.tensor_copy(XTT[:, 0, :].rearrange("p (k n) -> p k n", k=4)[:, :, 0:M2],
                              PS[:, 0, :].rearrange("p (k n) -> p k n", k=4)[:, :, 0:M2]).then_inc(fu["xc"], 1)
                take(eng, "down", 1)
                V.tensor_copy(YS[0:M2, 0, :], PS[0:M2, 4, :]).then_inc(fu["yc"], 1)
                take(eng, "sc", 1)
            V.memset(DC[:, 1:2], 0.0).then_inc(fu["end"], 1)

        def full_pool(eng):
            with eng.Fori(0, NEXP):
                take(eng, "idx", 1)
                G.indirect_dma_start(out=XG[0:M2, 0, :], out_offset=None, in_=xx_d[:, :],
                                     in_offset=bass.IndirectOffsetOnAxis(ap=IT, axis=0)).then_inc(fu["xg"], 16)
                eng.drain().then_inc(fu["row"], 1)
                take(eng, "yc", 1)
                G.indirect_dma_start(out=y_d[:, :], out_offset=bass.IndirectOffsetOnAxis(ap=IS, axis=0),
                                     in_=YS[0:M2, 0, :], in_offset=None, bounds_check=2 * N - 1,
                                     oob_is_err=False).then_inc(fu["ys"], 16)
                eng.drain().then_inc(fu["sc"], 1)

        def full_sp(eng):
            with eng.Fori(0, NEXP) as e:
                take(eng, "load", 1)
                eng.dma_start(EX[:, :], we_in[bass.ds(e, 1), :, :].rearrange("a p n -> (a p) n")).then_inc(fu["w"], 16)
            take(eng, "end", 1)

        def full_act(eng):
            with eng.Fori(0, NEXP):
                take(eng, "gelu", 1)
                A.activation(HT[:, 0, 0:2 * M2], PS[:, 2, 0:2 * M2], ACT.Gelu).then_inc(fu["hid"], 1)

        def full_pe(eng):
            take(eng, "tab", 1)
            for j in range(20):
                last = mm(PS[0:M2, 0, 0:NEXP], L2[:, j, :], R2[:, j, :], start=(j == 0), stop=(j == 19))
            last.then_inc(fu["up"], 1)
            with eng.Fori(0, NEXP):
                take(eng, "row", 1)
                for k in range(4):
                    last = nc.tensor.transpose(PS[:, 0, 128 * k:128 * k + M2], XG[0:M2, 0, 128 * k:128 * k + 128],
                                               IDN[0:M2, 0:M2])
                last.then_inc(fu["xt"], 1)
                take(eng, "xc", 1)
                take(eng, "w", 16)
                for f2 in range(2):
                    for k in range(4):
                        last = mm(PS[:, 2, M2 * f2:M2 * f2 + M2], EX[:, 256 * k + 128 * f2:256 * k + 128 * f2 + 128],
                                  XTT[:, 0, 128 * k:128 * k + M2], start=(k == 0), stop=(k == 3))
                last.then_inc(fu["gelu"], 1)
                take(eng, "hid", 1)
                for f2 in range(2):
                    last = mm(PS[0:M2, 4, :], HT[:, 0, M2 * f2:M2 * f2 + M2],
                              EX[:, 1024 + 512 * f2:1024 + 512 * f2 + 512], start=(f2 == 0), stop=(f2 == 1))
                last.then_inc(fu["down"], 1)

        for eng, body in (("sp", full_sp), ("dve", full_dve), ("act", full_act), ("pool", full_pool), ("pe", full_pe)):
            pr.raw(eng, full(body), after=[t_full, st2["y", 31], t_ys[29], t_ys[30], t_ys[31]])

        YL = RH[:, 0:10240].rearrange("p (i a d) -> p i a d", i=NT, a=2)
        yv = y_d.rearrange("(t a) d -> t a d", a=2)
        t_out = []
        lastp = st2["y", 31]
        for i in range(NT):
            n = rows(i)
            t = dma("sp", f"yl{i}", YL[0:n, i, :, :], yv[128 * i:128 * i + n, :, :],
                    after=[t_ys[29], t_ys[30], t_ys[31], lastp])
            a1 = put("dve", V.tensor_tensor, YL[0:n, i, 0, :], YL[0:n, i, 0, :], YL[0:n, i, 1, :], ALU.add, after=[t])
            a1 = put("dve", V.scalar_tensor_tensor, YL[0:n, i, 0, :], YL[0:n, i, 0, :], 0.5, XA[0:n, i, :], ALU.mult,
                     ALU.add, after=[a1])
            t_out.append(dma("act", "out", out[128 * i:128 * i + n, :], YL[0:n, i, 0, :], after=[a1]))
        pr.raw("act", lambda e: None, after=[t_out[-1], t_xns[-1], t_xxs[-1], t_xxs[-2], t_yz[-1]])

        block = ctx.enter_context(nc.Block())
        block.sync(lambda eng: pr.replay("sp", eng))
        block.gpsimd(lambda eng: pr.replay("pool", eng))
        block.scalar(lambda eng: pr.replay("act", eng))
        block.vector(lambda eng: pr.replay("dve", eng))
        block.tensor(lambda eng: pr.replay("pe", eng))


def constants(np):
    c = np.zeros((128, 671), np.float32)
    p = np.arange(128)
    c[:, 0:128] = np.eye(128)
    c[:, 128:256] = p[:, None] < p[None, :]
    c[:, 256:512] = np.arange(256)[None, :]
    c[:, 512:640] = (p[:, None] // 64) == (p[None, :] // 64)
    c[:, 670] = p < 32
    for i in range(NT):
        c[:, 640 + i] = (128 * i + p) >= N
        for k in range(2):
            c[:, 650 + 2 * i + k] = 2 * (128 * i + p) + k + 1
    return c


def kernel(**inputs):
    import numpy as np
    import concourse.bacc as _bacc
    from concourse import mybir as _mybir
    from concourse.bass_utils import run_bass_kernel_spmd as _run

    g = {k: np.asarray(v) for k, v in inputs.items()}

    def edges(a, mode):
        a = np.pad(a, (0, NG * GE - NE), mode=mode)
        return np.ascontiguousarray(a.reshape(NG, GE))

    def cols(a):
        return a.reshape(-1, 128).T

    vec = np.concatenate([cols(g["L0_gnn_b1"]), cols(g["L0_gnn_g1"]), cols(g["L0_gnn_be1"]), cols(g["L0_gnn_b2"]),
                          cols(g["L0_gnn_g2"]), cols(g["L0_gnn_be2"]), cols(g["L0_mix_bq"]),
                          np.broadcast_to(g["L0_gnn_eps"].reshape(1, 1), (128, 1))], axis=1)
    brow = np.concatenate([np.broadcast_to(g[k][None, :], (128, D)) for k in ("L0_mix_bk", "L0_mix_bv", "L0_mix_bp")],
                          axis=1)
    we = np.concatenate([
        g["L0_ffn_W1"].reshape(NEXP, 4, 128, 256).transpose(0, 2, 1, 3).reshape(NEXP, 128, 1024),
        g["L0_ffn_W2"].reshape(NEXP, 2, 128, 512).transpose(0, 2, 1, 3).reshape(NEXP, 128, 1024)], axis=2)
    arrays = {
        "x": g["x"], "src": edges(g["src"], "constant"), "dst": edges(g["dst"], "edge"),
        "w1g": g["L0_gnn_W1"], "w2g": g["L0_gnn_W2"],
        "wqkvp": np.stack([g["L0_mix_Wk"], g["L0_mix_Wv"], g["L0_mix_Wq"], g["L0_mix_Wp"]]),
        "hp": g["L0_ffn_hash_proj"].transpose(1, 0, 2).reshape(D, 256),
        "vec": vec, "brow": brow, "cst": constants(np), "we": we,
    }
    nc = _bacc.Bacc("TRN2", target_bir_lowering=False, num_devices=1)
    ins, args = {}, []
    for name, a in arrays.items():
        a = np.ascontiguousarray(a)
        ins[f"in_{name}"] = a
        args.append(nc.dram_tensor(f"in_{name}", a.shape, _mybir.dt.from_np(a.dtype), kind="ExternalInput").ap())
    out = nc.dram_tensor("out_0", (N, D), _mybir.dt.float32, kind="ExternalOutput").ap()
    gnn_mix_moe(nc, *args, out)
    r = _run(nc, [ins], core_ids=[0])
    return r.results[0]["out_0"]
```

```python
import concourse.bass as bass
from concourse import mybir
from contextlib import ExitStack

F32 = mybir.dt.float32
I32 = mybir.dt.int32
U32 = mybir.dt.uint32
BF16 = mybir.dt.bfloat16
F32R = mybir.dt.float32r
ALU = mybir.AluOpType
ACT = mybir.ActivationFunctionType
AX = mybir.AxisListType

N = 1250
NT = 10
D = 512
HID = 1024
NE = 20000
GE = 256
NG = 79
RING = 4
WIN = 64
AGW = 1316
CH = [(0, 418), (418, 416), (834, 416)]
NEXP = 64
CAP = 156


def rows(i):
    return min(128, N - 128 * i)


class Program:

    def __init__(self, nc, ctx):
        self.nc = nc
        self.ctx = ctx
        self.queue = {e: [] for e in ("pe", "dve", "act", "pool", "sp")}
        self.count = {}
        self.sems = {}

    def sem(self, name):
        if name not in self.sems:
            self.sems[name] = self.ctx.enter_context(self.nc.semaphore("s_" + name))
            self.count[name] = 0
        return self.sems[name]

    def put(self, eng, call, *args, after=(), signal=True, **kw):
        s = self.sem(eng)
        if signal:
            self.count[eng] += 1
        self.queue[eng].append((call, args, kw, list(after), s if signal else None, 1))
        return (eng, self.count[eng])

    def dma(self, eng, name, *args, after=(), indirect=False, **kw):
        s = self.sem(name)
        self.count[name] += 16
        nc = self.nc
        engine = {"sp": nc.sync, "act": nc.scalar, "pool": nc.gpsimd}[eng]
        call = engine.indirect_dma_start if indirect else engine.dma_start
        self.queue[eng].append((call, args, kw, list(after), s, 16))
        return (name, self.count[name])

    def raw(self, eng, fn, after=()):
        self.queue[eng].append((None, fn, None, list(after), None, 0))

    def replay(self, eng, engine):
        seen = {}
        for call, args, kw, after, s, by in self.queue[eng]:
            for name, value in after:
                if seen.get(name, 0) < value:
                    engine.wait_ge(self.sems[name], value)
                    seen[name] = value
            if call is None:
                args(engine)
                continue
            ins = call(*args, **kw)
            if s is not None:
                ins.then_inc(s, by)


def gnn_mix_moe(nc, x_in, src_in, dst_in, w1g, w2g, wqkvp, hp_in, vec_in, brow_in, cst_in, we_in, out):
    xn_d = nc.dram_tensor("xn_rows", [N, 3 * D], BF16, kind="Internal").ap()
    xx_d = nc.dram_tensor("xx_rows", [N, D], F32, kind="Internal").ap()
    y_d = nc.dram_tensor("y_rows", [2 * N, D], F32, kind="Internal").ap()

    with ExitStack() as ctx:
        def sb(name, shape, dt=F32):
            return ctx.enter_context(nc.sbuf_tensor(name, shape, dt))

        pr = Program(nc, ctx)
        put, dma = pr.put, pr.dma
        mm = nc.tensor.matmul
        V, A, G = nc.vector, nc.scalar, nc.gpsimd

        with nc.sbuf_tensor("ROUND", [128, 44076], F32R) as ROUND:
            pass
        RH = sb("RH", [128, 10280])
        RT = sb("RT", [128, 5000])
        RG = sb("RG", [128, 4, AGW])
        RQ = sb("RQ", [128, 5000])
        RW = sb("RW", [128, 8192])
        GE2 = sb("GE2", [128, 6656])
        GX = GE2[:, 0:6144].bitcast(BF16).rearrange("p (r j d) -> p r j d", r=RING, j=2)
        EX = GE2[:, 4608:6656]
        TMP = sb("TMP", [128, 4, D])
        BROW = sb("BROW", [128, 3, D])
        XA = sb("XA", [128, NT, D])
        CST = sb("CST", [128, 703])
        VEC = sb("VEC", [128, 41])
        KVB = sb("KVB", [128, 4, 128])
        KSB = sb("KSB", [128, 4, 128])
        KS8 = sb("KS8", [128, 4, 8])
        RS = RW[0:NG, 6144:6144 + GE].bitcast(I32)
        RD = RW[0:NG, 6656:6656 + GE].bitcast(I32)
        RSF = TMP[0:NG, 0, 0:GE]
        RDF = TMP[0:NG, 1, 0:GE]
        ZERO = KVB[:, :, :].rearrange("p r e -> p (r e)")
        EST = sb("EST", [128, 4])
        EROWI = sb("EROWI", [1, 80], I32)
        FLAG = sb("FLAG", [1, 4])
        FLAGI = sb("FLAGI", [1, 4], I32)
        SIDX = sb("SIDX", [128, 2, NG], I32)
        DREL = sb("DREL", [128, 2, NG])
        DABS = sb("DABS", [128, 2, NG])
        DC = sb("DC", [128, 2])
        IC = sb("IC", [128, 2], I32)
        OH = sb("OH", [128, 2, 2, WIN], BF16)
        ST = sb("ST", [128, NT, 6])
        MV = sb("MV", [128, NT, 2])
        RR = sb("RR", [128, NT])
        BST = sb("BST", [128, 2, 3, 6])
        BMV = sb("BMV", [128, 2, 8])
        NBQ = sb("NBQ", [128, 4])
        OPE = sb("OPE", [128, 1])
        TRIB = sb("TRIB", [128, 128], BF16)
        ONEB = sb("ONEB", [128, 128], BF16)
        TIDX = sb("TIDX", [128, 32], I32)
        SCIDX = sb("SCIDX", [128, 32], I32)
        VIDX = sb("VIDX", [128, 2, 32])

        PS = ctx.enter_context(nc.psum_tensor("PS", [128, 8, 512], F32))

        IDN = CST[:, 0:128]
        TRI = CST[:, 128:256]
        IOTA = CST[:, 256:512]
        BD = CST[:, 512:640]
        VAL = CST[:, 640:650]
        AID = CST[:, 650:670]
        M32 = CST[:, 670:671]
        M8 = CST[:, 671:703].rearrange("p (r h) -> p r h", r=4)
        b1, g1, be1 = VEC[:, 0:8], VEC[:, 8:16], VEC[:, 16:24]
        b2, g2, be2, bq = VEC[:, 24:28], VEC[:, 28:32], VEC[:, 32:36], VEC[:, 36:40]

        XN = RH[:, 0:5120].rearrange("p (i d) -> p i d", i=NT)
        KK = XN
        VA = RH[:, 5120:10280].rearrange("p (i r c) -> p i r c", i=NT, r=4)
        H1 = RH[:, 0:10000].rearrange("p (t n) -> p t n", t=8)
        XT = RT[:, :].rearrange("p (k n) -> p k n", k=4)
        ZR = RH[0:8, 0:1254].rearrange("p (c n) -> p c n", c=3)
        QT = RQ[:, :].rearrange("p (k n) -> p k n", k=4)
        WQ = RW[:, 0:2048].rearrange("p (k n) -> p k n", k=4)
        WK = RW[:, 2048:4096].rearrange("p (k n) -> p k n", k=4)
        WV = RW[:, 4096:6144].rearrange("p (k n) -> p k n", k=4)
        WP = RW[:, 6144:8192].rearrange("p (k n) -> p k n", k=4)
        W1 = RW[:, 0:4096].rearrange("p (k n) -> p k n", k=4)
        W2 = RW[:, 4096:8192].rearrange("p (k n) -> p k n", k=8)
        HP = RG[:, :, :].rearrange("p k n -> p (k n)")[:, 4096:5120].rearrange("p (k n) -> p k n", k=4)
        H2 = XT
        at, place = 0, {}
        for name, size in (("RH", 10280), ("RT", 5000), ("RG", 4 * AGW), ("RQ", 5000), ("RW", 8192), ("GE2", 6656),
                           ("TMP", 2048), ("BROW", 1536)):
            place[name] = at
            at += size

        def rounded(name, first, size):
            return ROUND[:, place[name] + first:place[name] + first + size]

        HTH = rounded("RT", 0, 5000).rearrange("p (k n) -> p k n", k=4)
        HTL = rounded("RG", 0, 4 * AGW).rearrange("p (k n) -> p k n", k=4)
        W1H = rounded("GE2", 0, 4096).rearrange("p (k n) -> p k n", k=4)
        W1L = rounded("RW", 0, 4096).rearrange("p (k n) -> p k n", k=4)
        W2H = rounded("RQ", 0, 4096).rearrange("p (k n) -> p k n", k=8)
        W2L = rounded("RW", 4096, 4096).rearrange("p (k n) -> p k n", k=8)
        RGf = RG[:, :, :].rearrange("p k n -> p (k n)")
        H1H = []
        for name, first, step in (("GE2", 4096, 416), ("GE2", 4096 + N, 416), ("TMP", 0, 416), ("BROW", 0, 416),
                                  ("GE2", 0, 1024), ("RW", 0, 1024), ("GE2", 420, 1024), ("RW", 420, 1024)):
            more = 2 if step == 416 else 0
            H1H.append([rounded(name, first + (step * c + more if c else 0), w) for c, (_, w) in enumerate(CH)])
        H1L = rounded("RH", 0, 10000).rearrange("p (t n) -> p t n", t=8)

        free = {b: [] for b in range(8)}

        t_x = [None] * NT
        t_rd = dma("sp", "rd", RD, dst_in[:, :])
        t_rs = dma("sp", "rs", RS, src_in[:, :])
        t_cst = dma("act", "cst", CST[:, :], cst_in[:, :])
        t_vec = dma("act", "vec", VEC[:, :], vec_in[:, :])
        for i in range(NT):
            t_x[i] = dma("sp", f"x{i}", XA[0:rows(i), i, :], x_in[128 * i:128 * i + rows(i), :])
        t_w = {}

        def load_w(eng, nm, after=()):
            j, w = {"k": (0, WK), "v": (1, WV), "q": (2, WQ), "p": (3, WP)}[nm]
            t_w[nm] = dma(eng, "w" + nm, w, wqkvp[j].rearrange("(k p) n -> p k n", p=128), after=after)

        load_w("sp", "k")
        t_brow = dma("sp", "brow", BROW[:, :, :], brow_in.rearrange("p (a d) -> p a d", a=3))

        t_m1 = put("pool", G.memset, MV[:, :, :], 1.0)
        t_m2 = put("pool", G.memset, VA[:, :, :, 128:129], 1.0)
        t_m3 = put("pool", G.memset, ONEB[:, :], 1.0)
        t_gz = put("pool", G.memset, RG[:, :, N:AGW], 0.0)
        a = put("dve", V.tensor_copy, RDF, RD, after=[t_rd])
        b = put("dve", V.tensor_copy, RSF, RS, after=[t_rs])
        c = put("dve", V.tensor_reduce, EST[0:NG, 0:1], RDF, AX.X, ALU.min, after=[a])
        d = put("dve", V.tensor_reduce, EST[0:NG, 1:2], RDF, AX.X, ALU.max, after=[a])
        e = put("dve", V.tensor_tensor, EST[0:NG, 2:3], EST[0:NG, 1:2], EST[0:NG, 0:1], ALU.subtract, after=[c, d])
        for j in range(2):
            m = put("pe", nc.tensor.transpose, PS[:, 3, 96 * j:96 * j + NG], RDF[:, 128 * j:128 * j + 128],
                    IDN[0:NG, 0:NG], after=[a, t_cst], signal=(j == 1))
        pv = PS[:, 3, 0:192].rearrange("p (j g) -> p j g", j=2)[:, :, 0:NG]
        t_dabs = put("dve", V.tensor_copy, DABS[:, :, :], pv, after=[m])
        free[3] = [t_dabs]
        f = put("dve", V.tensor_scalar, RDF, RDF, EST[0:NG, 0:1], None, ALU.subtract, after=[c, d, m])
        for j in range(2):
            put("pe", nc.tensor.transpose, PS[:, 0, 96 * j:96 * j + NG], RDF[:, 128 * j:128 * j + 128],
                IDN[0:NG, 0:NG], after=[f, b, t_cst], signal=False)
            put("pe", nc.tensor.transpose, PS[:, 1, 96 * j:96 * j + NG], RSF[:, 128 * j:128 * j + 128],
                IDN[0:NG, 0:NG], signal=False)
        put("pe", nc.tensor.transpose, PS[0:1, 2, 0:NG], EST[0:NG, 0:1], IDN[0:NG, 0:NG], after=[e], signal=False)
        m = put("pe", nc.tensor.transpose, PS[0:1, 2, 128:128 + NG], EST[0:NG, 2:3], IDN[0:NG, 0:NG])
        pv = PS[:, 0, 0:192].rearrange("p (j g) -> p j g", j=2)[:, :, 0:NG]
        t_drel = put("dve", V.tensor_copy, DREL[:, :, :], pv, after=[m])
        pv = PS[:, 1, 0:192].rearrange("p (j g) -> p j g", j=2)[:, :, 0:NG]
        t_sidx = put("dve", V.tensor_copy, SIDX[:, :, :], pv, after=[m])
        t_erow = put("dve", V.tensor_copy, EROWI[0:1, 0:NG], PS[0:1, 2, 0:NG], after=[m])
        s = put("dve", V.tensor_reduce, FLAG[0:1, 0:1], PS[0:1, 2, 128:128 + NG], AX.X, ALU.max, after=[m])
        t_flag = put("dve", V.tensor_copy, FLAGI[0:1, 0:1], FLAG[0:1, 0:1], after=[s])
        free[0] = [t_drel]
        free[1] = [t_sidx]
        free[2] = [t_flag]
        t_edges = [a, b]
        for r in range(4):
            m = put("pe", nc.tensor.transpose, PS[0:8, 5, 128 * r:128 * r + 128], M8[:, r, :], IDN, after=[t_cst],
                    signal=(r == 3))
        t_s8 = put("act", A.copy, KSB[0:8, :, :].rearrange("p r e -> p (r e)"), PS[0:8, 5, :], after=[m])
        free[5] = [t_s8]

        t_xn, t_xns, t_xt, t_acc = [], [], [], []
        t_rem = [[], []]
        XB = RQ[:, 0:4608].bitcast(BF16).rearrange("p (s a d) -> p s a d", s=6, a=3)
        for h in range(2):
            for i in range(5 * h, 5 * h + 5):
                n = rows(i)
                s = put("dve", V.bn_stats, ST[0:n, i, :], XA[0:n, i, :], after=[t_x[i], t_m1])
                s = put("dve", V.bn_aggr, MV[0:n, i, :], ST[0:n, i, :], after=[s])
            hs = slice(5 * h, 5 * h + 5)
            s = put("dve", V.tensor_scalar, RR[:, hs], MV[:, hs, 1], 1e-5, None, ALU.add, after=[s])
            s = put("act", A.activation, RR[:, hs], RR[:, hs], ACT.Sqrt, after=[s])
            t_rr = put("dve", V.reciprocal, RR[:, hs], RR[:, hs], after=[s])
            if h == 0:
                t_rr0 = t_rr
        parts = {}
        for i in range(NT + 2):
            if i < NT:
                n = rows(i)
                t = put("dve", V.tensor_scalar, XN[0:n, i, :], XA[0:n, i, :], MV[0:n, i, 0:1], RR[0:n, i:i + 1],
                        ALU.subtract, ALU.mult, after=[t_rr0 if i < 5 else t_rr])
                t_xn.append(t)
                u = put("act", A.copy, XB[0:n, i % 6, 0, :], XN[0:n, i, :], after=[t] + t_xns[i - 6:i - 5])
                bk = i % 4
                for k in range(4):
                    p = put("pe", nc.tensor.transpose, PS[:, bk, 128 * k:128 * k + n],
                            XN[0:n, i, 128 * k:128 * k + 128], IDN[0:n, 0:n], after=[t, t_cst] + free[bk],
                            signal=(k == 3))
                pv = PS[:, bk, :].rearrange("p (k n) -> p k n", k=4)[:, :, 0:n]
                t = put("act", A.copy, XT[:, :, 128 * i:128 * i + n], pv, after=[p])
                t_xt.append((p, t))
                free[bk] = [t]
                parts[i] = u
            q = i - 1
            if 0 <= q < NT:
                n = rows(q)
                rem = TMP[0:n, 2 + q % 2, :]
                u = put("dve", V.tensor_tensor, rem, XN[0:n, q, :], XB[0:n, q % 6, 0, :], ALU.subtract,
                        after=[parts[q]] + t_rem[q % 2])
                parts[q] = put("act", A.copy, XB[0:n, q % 6, 1, :], rem, after=[u])
            q = i - 2
            if 0 <= q < NT:
                n = rows(q)
                u = put("dve", V.tensor_tensor, XB[0:n, q % 6, 2, :], TMP[0:n, 2 + q % 2, :], XB[0:n, q % 6, 1, :],
                        ALU.subtract, after=[parts[q]])
                t_rem[q % 2] = [u]
                t_xns.append(dma("sp", f"xns{q % 6}", xn_d[128 * q:128 * q + n, :],
                                 XB[0:n, q % 6, :, :].rearrange("p a d -> p (a d)"), after=[u]))
        t_ope = put("dve", V.tensor_scalar, OPE[:, :], VEC[:, 40:41], 1.0, None, ALU.add, after=[t_vec])
        t_nbq = put("dve", V.tensor_scalar, NBQ[:, :], bq, -1.0, None, ALU.mult, after=[t_vec])
        t_ag0 = put("act", A.activation, RG[:, :, 0:N], XT[:, :, :], ACT.Copy, scale=OPE[:, 0:1],
                    after=[t_xt[-1][1], t_ope, t_gz])

        t_gx, t_gdone = [], [None] * NG

        def gather(g):
            for j in range(1 if g == NG - 1 else 2):
                n = 32 if g == NG - 1 else 128
                t = dma("pool", f"gx{g % RING}", out=GX[0:n, g % RING, j, :], out_offset=None, in_=xn_d[:, :],
                        in_offset=bass.IndirectOffsetOnAxis(ap=SIDX[0:n, j, g:g + 1], axis=0), indirect=True,
                        after=(t_xns[-6:] + [t_sidx] if g < RING else [t_gdone[g - RING]]))
            t_gx.append(t)

        t_ohfree = [None, None]
        t_agg = []
        regs = {}

        def onehot(g):
            o = g % 2
            n = 32 if g == NG - 1 else 128
            nj = 1 if g == NG - 1 else 2
            return put("dve", V.tensor_tensor, OH[0:n, o, 0:nj, :],
                       DREL[0:n, 0:nj, g:g + 1].broadcast_to([n, nj, WIN]),
                       IOTA[0:n, 0:WIN].unsqueeze(1).broadcast_to([n, nj, WIN]), ALU.is_equal,
                       after=[t_drel, t_cst] + ([t_ohfree[o]] if t_ohfree[o] else []))

        t_hot = {}

        def aggregate(g):
            o = g % 2
            n = 32 if g == NG - 1 else 128
            nj = 1 if g == NG - 1 else 2
            t_oh = t_hot.pop(g)
            bk = 4 + o
            for f4 in range(4):
                for j in range(nj):
                    for a in range(3):
                        col = D * a + 128 * f4
                        p = put("pe", mm, PS[:, bk, WIN * f4:WIN * f4 + WIN], GX[0:n, g % RING, j, col:col + 128],
                                OH[0:n, o, j, :], start=(j == 0 and a == 0), stop=(j == nj - 1 and a == 2),
                                after=[t_gx[g], t_oh] + free[bk], signal=(f4 == 3 and j == nj - 1 and a == 2))
            t_gdone[g] = p
            t_ohfree[o] = p
            if g + RING < NG:
                gather(g + RING)
            if g == 12:
                load_w("sp", "p", t_edges + [t_gx[g + RING]])
            if g + 2 < NG:
                t_hot[g + 2] = onehot(g + 2)

            def load(eng, g=g):
                regs[g] = eng.value_load(EROWI[0:1, g:g + 1], min_val=0, max_val=N - 1)
            pr.raw("dve", load, after=[t_erow])

            def add(bk=bk, g=g):
                win = RG[:, :, bass.ds(regs[g], WIN)]
                return V.tensor_tensor(win, PS[:, bk, 0:4 * WIN].rearrange("p (f w) -> p f w", f=4), win, ALU.add)
            t = put("dve", add, after=[p, t_ag0] + t_agg[-1:])
            t_agg.append(t)
            free[bk] = [t]

        load_w("sp", "v")
        for g in range(RING):
            gather(g)
        load_w("sp", "q", [t_gx[RING - 1]])

        mix = [0]

        def bank():
            mix[0] += 1
            return (mix[0] - 1) % 4

        t_tmp = [t_rem[0] + t_rem[1], t_rem[0] + t_rem[1]]
        t_k, t_v, t_q = [None] * NT, [None] * NT, {}

        def k_unit(i):
            n, bk, s = rows(i), bank(), i % 2
            for k in range(4):
                p = put("pe", mm, PS[0:n, bk, :], XT[:, k, 128 * i:128 * i + n], WK[:, k, :], start=(k == 0),
                        stop=(k == 3), after=[t_xt[i][1], t_w["k"]] + free[bk], signal=(k == 3))
            u, w = TMP[0:n, 2 * s, :], TMP[0:n, 2 * s + 1, :]
            a1 = put("dve", V.tensor_tensor, u, PS[0:n, bk, :], BROW[0:n, 0, :], ALU.add,
                     after=[p, t_brow] + t_tmp[s])
            free[bk] = [a1]
            a2 = put("act", A.activation, w, u, ACT.Relu, scale=-1.0, after=[a1] + t_tmp[s])
            a3 = put("act", A.activation, w, w, ACT.Exp, scale=-1.0, after=[a2])

            def finish():
                t = put("dve", V.tensor_tensor, XA[0:n, i, :], XA[0:n, i, :], XN[0:n, i, :], ALU.add, after=[t_xn[i]])
                t = put("dve", V.tensor_tensor, XA[0:n, i, :], XA[0:n, i, :], BROW[0:n, 2, :], ALU.add,
                        after=[t, t_brow])
                t_acc.append(t)
                t_k[i] = put("dve", V.scalar_tensor_tensor, KK[0:n, i, :], u, 0.0, w, ALU.max, ALU.add,
                             after=[a3, t_xt[i][0], t_acc[i]])
                t_tmp[s] = [t_k[i]]
            return finish

        def v_unit(i):
            n, bk = rows(i), bank()
            for k in range(4):
                p = put("pe", mm, PS[0:n, bk, :], XT[:, k, 128 * i:128 * i + n], WV[:, k, :], start=(k == 0),
                        stop=(k == 3), after=[t_xt[i][1], t_w["v"]] + free[bk], signal=(k == 3))
            t_v[i] = put("dve", V.tensor_tensor, VA[0:n, i, :, 0:128],
                         PS[0:n, bk, :].rearrange("p (r c) -> p r c", r=4),
                         BROW[0:n, 1, :].rearrange("p (r c) -> p r c", r=4), ALU.add, after=[p, t_m2])
            free[bk] = [t_v[i]]

        t_kv = [None] * 4

        def kv_unit(r):
            bk = 6 + r % 2
            o = 129 * (r // 2)
            for i in range(NT):
                n = rows(i)
                p = put("pe", mm, PS[:, bk, o:o + 129], KK[0:n, i, 128 * r:128 * r + 128], VA[0:n, i, r, :],
                        start=(i == 0), stop=(i == NT - 1), after=[t_k[i], t_v[i]] + free[bk], signal=(i == NT - 1))
            a1 = put("dve", V.tensor_tensor, KVB[:, r, :], PS[:, bk, o:o + 128], BD, ALU.mult, after=[p, t_cst])
            a2 = put("dve", V.tensor_copy, EST[:, 3:4], PS[:, bk, o + 128:o + 129], after=[p] + ([t_kv[r - 1]] if r else []))
            free[bk] = [a2]
            t_kv[r] = put("dve", V.tensor_scalar, KS8[:, r, :], M8[:, r, :], EST[:, 3:4], None, ALU.mult, after=[a1, a2])

        def q_unit(r, c):
            o, w = CH[c]
            bk, s = bank(), r % 2
            for k in range(4):
                p = put("pe", mm, PS[:, bk, 0:w], WQ[:, k, 128 * r:128 * r + 128], XT[:, k, o:o + w], start=(k == 0),
                        stop=(k == 3), after=[t_xt[-1][1], t_w["q"]] + free[bk], signal=(k == 3))
            e1 = TMP[:, 2 * s, 0:w]
            a1 = put("act", A.activation, e1, PS[:, bk, 0:w], ACT.Relu, bias=NBQ[:, r:r + 1], scale=-1.0,
                     after=[p, t_nbq] + t_tmp[s])
            a2 = put("act", A.activation, e1, e1, ACT.Exp, scale=-1.0, after=[a1])
            a3 = put("dve", V.tensor_scalar, QT[:, r, o:o + w], PS[:, bk, 0:w], bq[:, r:r + 1], 0.0, ALU.add,
                     ALU.max, after=[p, a1] + t_xns[-6:])
            free[bk] = [a3]

            def finish():
                t_q[r, c] = put("dve", V.tensor_tensor, QT[:, r, o:o + w], QT[:, r, o:o + w], e1, ALU.add,
                                after=[a2, a3])
                t_tmp[s] = [t_q[r, c]]
            return finish

        t_o = {}

        t_z, t_zt = {}, [[], []]

        def z_unit(c):
            o, w = CH[c]
            bd = bank()
            for r in range(4):
                p = put("pe", mm, PS[0:8, bd, 0:w], KS8[:, r, :], QT[:, r, o:o + w], start=(r == 0), stop=(r == 3),
                        after=[t_kv[r], t_q[r, c]] + free[bd], signal=(r == 3))
            t_z[c] = put("dve", V.reciprocal, ZR[:, c, 0:w], PS[0:8, bd, 0:w], after=[p])
            free[bd] = [t_z[c]]

        def o_unit(r, c):
            o, w = CH[c]
            bn, bd = bank(), bank()
            p = put("pe", mm, PS[:, bn, 0:w], KVB[:, r, :], QT[:, r, o:o + w], start=True, stop=True, after=free[bn])
            p = put("pe", mm, PS[:, bd, 0:w], KSB[0:8, r, :], ZR[:, c, 0:w], start=True, stop=True,
                    after=[t_z[c], t_s8] + free[bd])
            z = TMP[:, 1 + 2 * (r % 2), 0:w]
            a1 = put("act", A.copy, z, PS[:, bd, 0:w], after=[p] + t_zt[r % 2])
            t_o[r, c] = put("dve", V.tensor_tensor, QT[:, r, o:o + w], PS[:, bn, 0:w], z, ALU.mult, after=[a1])
            t_zt[r % 2] = [t_o[r, c]]
            free[bd], free[bn] = [a1], [t_o[r, c]]

        t_p = [None] * NT
        p_last = [None]

        def p_unit(i):
            n, bk = rows(i), bank()
            for k in range(4):
                p = put("pe", mm, PS[0:n, bk, :], QT[:, k, 128 * i:128 * i + n], WP[:, k, :], start=(k == 0),
                        stop=(k == 3), after=[t_w["p"]] + [t_o[k, c] for c in range(3)] + free[bk], signal=(k == 3))
            t_p[i] = put("dve", V.tensor_tensor, XA[0:n, i, :], PS[0:n, bk, :], XA[0:n, i, :], ALU.add,
                         after=[p, t_acc[i]])
            free[bk] = [t_p[i]]
            p_last[0] = p

        units = [(k_unit, (i,)) for i in range(NT)] + [(v_unit, (i,)) for i in range(NT)]
        units += [(kv_unit, (r,)) for r in range(4)]
        units += [(q_unit, (r, 0)) for r in range(4)]
        for c in range(3):
            nxt = [(q_unit, (r, c + 1)) for r in range(4)] if c < 2 else []
            units += nxt[0:1] + [(z_unit, (c,))] + nxt[1:2]
            for r in range(4):
                units += [(o_unit, (r, c))] + nxt[r + 2:r + 3]
        units += [(p_unit, (i,)) for i in range(NT)]

        ra = {n: pr.sem("ra_" + n) for n in ("idx", "gx", "row", "one", "sum", "dve", "end")}
        OHW = OH[:, :, :, :].rearrange("p a b c -> p (a b c)")
        DABSf = DABS[:, :, :].rearrange("p j g -> p (j g)")
        SIDXf = SIDX[:, :, :].rearrange("p j g -> p (j g)")

        def wide(body):
            def run(eng):
                far = eng.value_load(FLAGI[0:1, 0:1], min_val=0, max_val=N)
                with eng.If(far >= WIN):
                    body(eng)
            return run

        def wide_dve(eng):
            n = [0]

            def link(ins):
                n[0] += 1
                ins.then_inc(ra["dve"], 1)
                eng.wait_ge(ra["dve"], n[0])

            link(V.memset(DABS[:, 1:2, NG - 1:NG], -4096.0))
            link(V.tensor_scalar(DABS[:, 0, NG - 1:NG], DABS[:, 0, NG - 1:NG], 4096.0, M32, ALU.add, ALU.mult))
            link(V.tensor_scalar(DABS[:, 0, NG - 1:NG], DABS[:, 0, NG - 1:NG], -4096.0, None, ALU.add))
            link(V.tensor_scalar(RG[:, :, 0:N], XT[:, :, :], OPE[:, 0:1], None, ALU.mult))
            link(V.memset(RG[:, :, N:AGW], 0.0))
            eng.sem_clear(ra["dve"])
            with eng.Fori(0, 2 * NG) as i:
                n[0] = 0
                link(V.tensor_copy(DC[:, 0:1], DABSf[:, bass.ds(i, 1)]))
                V.tensor_copy(IC[:, 0:1], SIDXf[:, bass.ds(i, 1)]).then_inc(ra["idx"], 1)
                for q in range(5):
                    V.tensor_scalar(OHW, IOTA, DC[:, 0:1], None, ALU.is_equal).then_inc(ra["one"], 1)
                    link(V.tensor_scalar(DC[:, 0:1], DC[:, 0:1], -256.0, None, ALU.add))
                    eng.wait_ge(ra["sum"], q + 1)
                    if q == 4:
                        eng.sem_clear(ra["sum"])
                    win = RG[:, :, 256 * q:256 * q + 256]
                    link(V.tensor_tensor(win, PS[:, 4:6, :].rearrange("p b (f w) -> p (b f) w", f=2), win, ALU.add))
                eng.sem_clear(ra["dve"])
            V.memset(DC[:, 1:2], 0.0).then_inc(ra["end"], 1)

        def wide_pool(eng):
            with eng.Fori(0, 2 * NG):
                eng.wait_ge(ra["idx"], 1)
                eng.sem_clear(ra["idx"])
                G.indirect_dma_start(out=GX[:, 0, 0, :], out_offset=None, in_=xn_d[:, :],
                                     in_offset=bass.IndirectOffsetOnAxis(ap=IC[:, 0:1], axis=0)).then_inc(ra["gx"], 16)
                eng.drain().then_inc(ra["row"], 1)

        def wide_pe(eng):
            with eng.Fori(0, 2 * NG):
                eng.wait_ge(ra["row"], 1)
                eng.sem_clear(ra["row"])
                for q in range(5):
                    eng.wait_ge(ra["one"], q + 1)
                    if q == 4:
                        eng.sem_clear(ra["one"])
                    for f4 in range(4):
                        for a in range(3):
                            col = D * a + 128 * f4
                            last = mm(PS[:, 4 + f4 // 2, 256 * (f4 % 2):256 * (f4 % 2) + 256],
                                      GX[:, 0, 0, col:col + 128], OHW, start=(a == 0), stop=(a == 2))
                    last.then_inc(ra["sum"], 1)
            eng.wait_ge(ra["end"], 1)

        t_w1 = []
        pieces = []

        def aggregated():
            for eng, body in (("dve", wide_dve), ("pool", wide_pool), ("pe", wide_pe)):
                pr.raw(eng, wide(body), after=[t_flag, t_dabs, t_agg[-1], t_ope])
            for k in range(4):
                t_w1.append(dma("sp", f"w1{k}", W1[:, k, :], w1g[128 * k:128 * k + 128, :],
                                after=[marks["q_unit"], marks["k_unit"], t_gx[-1]]))
            pieces.extend([(split_ht, k) for k in range(4)] + [(split_w1, k) for k in range(4)])

        t_ht, t_w1s, t_w2s = [], [], []

        def split_ht(k):
            a1 = put("dve", V.tensor_copy, HTH[:, k, :], RG[:, k, 0:N], after=[t_agg[-1], marks["q_unit"], t_ag0])
            t_ht.append(put("dve", V.tensor_tensor, HTL[:, k, 0:N], RG[:, k, 0:N], HTH[:, k, :].bitcast(F32),
                            ALU.subtract, after=[a1]))

        def split_w1(k):
            a1 = put("dve", V.tensor_copy, W1H[:, k, :], W1[:, k, :], after=[t_w1[k], t_gdone[-1]])
            t_w1s.append(put("dve", V.tensor_tensor, W1L[:, k, :], W1[:, k, :], W1H[:, k, :].bitcast(F32),
                             ALU.subtract, after=[a1]))

        g, marks, late = 0, {}, None
        RATE = 1.6
        for q in range(2):
            t_hot[q] = onehot(q)
        for u, (fn, args) in enumerate(units):
            if late and fn in (kv_unit, z_unit, o_unit):
                late()
                late = None
            done = fn(*args)
            marks[fn.__name__] = ("pe", pr.count["pe"])
            if late:
                late()
            late = done
            if pieces:
                fn, k = pieces.pop(0)
                fn(k)
            while u >= 3 and g < min(NG, (u - 2) * RATE):
                aggregate(g)
                g += 1
                if g == NG:
                    aggregated()
        while g < NG:
            aggregate(g)
            g += 1
            if g == NG:
                aggregated()
        for fn, k in pieces:
            fn(k)

        t_m4 = put("pool", G.memset, ZERO, 0.0, after=[p_last[0]])

        t_w2 = dma("sp", "w2", W2, w2g.rearrange("(k p) n -> p k n", p=128), after=[p_last[0], marks["v_unit"]])

        t_yz = []
        for i in range(20):
            n = min(128, 2 * N - 128 * i)
            t_yz.append(dma("sp", "yz", y_d[128 * i:128 * i + n, :], ZERO[0:n, :], after=[t_m4]))

        slots, loads = [], []

        def load_expert(buf, after):
            e = len(loads)
            if e < NEXP:
                s = len(slots) if len(slots) > e else None
                loads.append((buf, dma("sp", f"we{e % 24}", buf, we_in[e], after=after)))

        def split_w2(k):
            a1 = put("dve", V.tensor_copy, W2H[:, k, :], W2[:, k, :], after=[t_w2, p_last[0]])
            t_w2s.append(put("dve", V.tensor_tensor, W2L[:, k, :], W2[:, k, :], W2H[:, k, :].bitcast(F32),
                             ALU.subtract, after=[a1]))

        def products(out, ah, al, bh, bl, first, last, after, signal):
            put("pe", mm, out, ah, bh, start=first, stop=False, after=after, signal=False)
            put("pe", mm, out, ah, bl, start=False, stop=False, signal=False)
            return put("pe", mm, out, al, bh, start=False, stop=last, signal=signal)

        def norm(t, s, buf, gam, bet, deps):
            for c, (o, w) in enumerate(CH):
                a1 = put("dve", V.bn_stats, BST[:, s, c, :], buf[:, o:o + w], after=[deps[c]])
            m = BMV[:, s, :]
            a1 = put("dve", V.bn_aggr, m[:, 0:2], BST[:, s, :, :].rearrange("p c k -> p (c k)"), after=[a1])
            a1 = put("dve", V.tensor_scalar, m[:, 2:3], m[:, 1:2], 1e-5, None, ALU.add, after=[a1])
            a1 = put("act", A.activation, m[:, 3:4], m[:, 2:3], ACT.Sqrt, after=[a1])
            a1 = put("dve", V.reciprocal, m[:, 4:5], m[:, 3:4], after=[a1])
            a1 = put("dve", V.tensor_tensor, m[:, 5:6], m[:, 4:5], gam, ALU.mult, after=[a1])
            a1 = put("dve", V.tensor_tensor, m[:, 6:7], m[:, 5:6], m[:, 0:1], ALU.mult, after=[a1])
            a1 = put("dve", V.tensor_tensor, m[:, 7:8], bet, m[:, 6:7], ALU.subtract, after=[a1])
            return put("act", A.activation, buf, buf, ACT.Relu, bias=m[:, 7:8], scale=m[:, 5:6], after=[a1])

        t_bmv = [[], []]
        t_h1, t_h1s, pe_h1 = [], [], []

        def split_h1(t):
            wait = [t_h1[t], t_gdone[-1], marks["p_unit"], t_k[NT - 1]]
            if t >= 4:
                wait.append(pe_h1[3 if t < 6 else 6])
            for c, (o, w) in enumerate(CH):
                a1 = put("act", A.copy, H1H[t][c], H1[:, t, o:o + w], after=wait)
                a1 = put("dve", V.tensor_tensor, H1L[:, t, o:o + w], H1[:, t, o:o + w], H1H[t][c].bitcast(F32),
                         ALU.subtract, after=[a1])
            t_h1s.append(a1)

        nb = 0
        for t in range(8):
            deps = []
            for c, (o, w) in enumerate(CH):
                bk = nb % 8
                nb += 1
                for k in range(4):
                    f = slice(128 * t, 128 * t + 128)
                    p = products(PS[:, bk, 0:w], W1H[:, k, f], W1L[:, k, f], HTH[:, k, o:o + w], HTL[:, k, o:o + w],
                                 k == 0, k == 3, [t_w1s[k], t_ht[k], t_o[3, 2], t_kv[3]] + free[bk], k == 3)
                a1 = put("act", A.activation, H1[:, t, o:o + w], PS[:, bk, 0:w], ACT.Identity, bias=b1[:, t:t + 1],
                         after=[p] + t_bmv[t % 2])
                free[bk] = [a1]
                deps.append(a1)
            t_h1.append(norm(t, t % 2, H1[:, t, :], g1[:, t:t + 1], be1[:, t:t + 1], deps))
            t_bmv[t % 2] = [t_h1[-1]]
            pe_h1.append(p)
            split_w2(t)
            if t >= 1:
                split_h1(t - 1)
        pe_w1 = p
        split_h1(7)
        t_hp = dma("sp", "hp", HP, hp_in.rearrange("(k p) n -> p k n", p=128), after=[pe_w1])
        load_expert(RGf[:, 0:2048], [pe_w1])
        load_expert(RGf[:, 2048:4096], [pe_w1])

        t_h2 = []
        for t in range(4):
            deps = []
            f = slice(128 * t, 128 * t + 128)
            pw = {}
            for ks in (range(4), range(4, 8)):
                for c, (o, w) in enumerate(CH):
                    bk = (nb + c) % 8
                    for k in ks:
                        pw[c] = products(PS[:, bk, 0:w], W2H[:, k, f], W2L[:, k, f], H1H[k][c],
                                         H1L[:, k, o:o + w], k == 0, k == 7, [t_w2s[k], t_h1s[k]] + free[bk], k == 7)
            for c, (o, w) in enumerate(CH):
                bk = nb % 8
                nb += 1
                p = pw[c]
                a1 = put("act", A.activation, H2[:, t, o:o + w], PS[:, bk, 0:w], ACT.Identity, bias=b2[:, t:t + 1],
                         after=[p] + t_bmv[t % 2])
                free[bk] = [a1]
                deps.append(a1)
            t_h2.append(norm(t, t % 2, H2[:, t, :], g2[:, t:t + 1], be2[:, t:t + 1], deps))
            t_bmv[t % 2] = [t_h2[-1]]
        pe_w2 = p
        waiting = [EX] + [RH[:, 2048 * q:2048 * q + 2048] for q in range(3)]
        waiting += [RW[:, 2048 * q:2048 * q + 2048] for q in range(4)] + [RQ[:, 0:2048], RQ[:, 2048:4096]]

        RB = RH[:, 6144:10280]
        MX = RB[:, 0:320].rearrange("p (i h e) -> p i h e", i=NT, h=4)
        MI = RB[:, 320:640].bitcast(U32).rearrange("p (i h e) -> p i h e", i=NT, h=4)
        LG = RB[:, 640:1152].rearrange("p (s n) -> p s n", s=2)
        t_rb1 = put("dve", V.memset, RB[:, 0:640], 0.0, after=[pe_w2])
        t_m5 = put("dve", V.memset, MV[:, :, :], 1.0)
        t_xx, t_xxs, t_lgf, t_best = [None] * NT, [None] * NT, [[], []], None
        xxr = [None, None]
        xtr = [None, None]
        st = {}

        def step_t(i):
            n, bk = rows(i), nbank()
            for k in range(4):
                p = put("pe", nc.tensor.transpose, PS[0:n, bk, 128 * k:128 * k + 128], H2[:, k, 128 * i:128 * i + n],
                        IDN, after=[t_h2[k]] + free[bk], signal=(k == 3))
            st["t", i] = (bk, p)
            return p

        def step_a(i):
            n, (bk, p) = rows(i), st["t", i]
            a1 = put("dve", V.tensor_tensor, XA[0:n, i, :], PS[0:n, bk, :], XA[0:n, i, :], ALU.add,
                     after=[p, t_p[i]])
            free[bk] = [a1]
            a1 = put("dve", V.bn_stats, ST[0:n, i, :], XA[0:n, i, :], after=[a1])
            a1 = put("dve", V.bn_aggr, MV[0:n, i, :], ST[0:n, i, :], after=[a1, t_m5])
            a1 = put("dve", V.tensor_scalar, RR[:, i:i + 1], MV[:, i, 1:2], 1e-5, None, ALU.add, after=[a1])
            st[i] = put("act", A.activation, RR[:, i:i + 1], RR[:, i:i + 1], ACT.Sqrt, after=[a1])

        nbk = [nb]

        def nbank():
            nbk[0] += 1
            return (nbk[0] - 1) % 8

        def step_b(i):
            n, s = rows(i), i % 2
            a1 = put("dve", V.reciprocal, RR[:, i:i + 1], RR[:, i:i + 1], after=[st[i]])
            wait = [a1] + (xxr[s] or [])
            xx = TMP[0:n, s, :]
            a1 = put("dve", V.tensor_scalar, xx, XA[0:n, i, :], MV[0:n, i, 0:1], RR[0:n, i:i + 1], ALU.subtract,
                     ALU.mult, after=wait)
            t_xxs[i] = dma("sp", f"xxs{s}", xx_d[128 * i:128 * i + n, :], xx, after=[a1])
            bk = nbank()
            for k in range(4):
                p = put("pe", nc.tensor.transpose, PS[:, bk, 128 * k:128 * k + n], xx[:, 128 * k:128 * k + 128],
                        IDN[0:n, 0:n], after=[a1] + free[bk], signal=(k == 3))
            xxr[s] = [p, t_xxs[i]]
            xt = TMP[:, 2 + s, :].rearrange("p (k n) -> p k n", k=4)
            a2 = put("act", A.copy, xt[:, :, 0:n], PS[:, bk, :].rearrange("p (k n) -> p k n", k=4)[:, :, 0:n],
                     after=[p] + (xtr[s] or []))
            free[bk] = [a2]
            st["xt", i] = a2

        def step_c(i):
            n, s, bk = rows(i), i % 2, nbank()
            a2 = st["xt", i]
            xt = TMP[:, 2 + s, :].rearrange("p (k n) -> p k n", k=4)
            for k in range(4):
                p = put("pe", mm, PS[0:n, bk, 0:256], xt[:, k, 0:n], HP[:, k, :], start=(k == 0), stop=(k == 3),
                        after=[a2, t_hp] + free[bk], signal=(k == 3))
            xtr[s] = [p]
            a3 = put("act", A.copy, LG[0:n, s, :], PS[0:n, bk, 0:256], after=[p] + t_lgf[s])
            free[bk] = [a3]
            st["lg", i] = a3
            return p

        def step_d(i):
            n, s = rows(i), i % 2
            for h in range(4):
                l = LG[0:n, s, 64 * h:64 * h + 64]
                a1 = put("dve", V.max, MX[0:n, i, h, :], l, after=[st["lg", i], t_rb1])
                a1 = put("dve", V.max_index, MI[0:n, i, h, :], MX[0:n, i, h, :], l, after=[a1])
            t_lgf[s] = [a1]
            return a1

        for i in range(-2, NT + 3):
            if i + 2 < NT:
                p_tr = step_t(i + 2)
            if 0 <= i - 2 < NT:
                p_lg = step_c(i - 2)
            if 0 <= i < NT:
                step_a(i)
            if 0 <= i - 1 < NT:
                step_b(i - 1)
                load_expert(waiting.pop(0), [p_tr])
            if 0 <= i - 3 < NT:
                t_best = step_d(i - 3)
        nb = nbk[0]

        S1 = RB[:, 1152:4136]
        off = [0]

        def scr(n):
            off[0] += n
            return S1[:, off[0] - n:off[0]]

        SC8 = scr(80).rearrange("p (i e) -> p i e", i=NT)
        T8 = scr(80).rearrange("p (i e) -> p i e", i=NT)
        TI = scr(80).bitcast(U32).rearrange("p (i e) -> p i e", i=NT)
        CAND = scr(40).rearrange("p (i h) -> p i h", i=NT)
        TOP = scr(20).rearrange("p (i k) -> p i k", i=NT)
        SEL = scr(20).rearrange("p (i k) -> p i k", i=NT)
        PR4 = scr(20).rearrange("p (i k) -> p i k", i=NT)
        SELI = scr(20).bitcast(I32)
        ODD = scr(20)
        PAIR = scr(20)
        POS = scr(20).rearrange("p (i k) -> p i k", i=NT)
        QP = scr(20)
        OHE = RT[:, 0:1280].rearrange("p (i k e) -> p i k e", i=NT, k=2)
        OHS = scr(320).bitcast(BF16).rearrange("p (i e) -> p i e", i=NT)
        PRD = RT[:, 1280:1920].rearrange("p (i e) -> p i e", i=NT)
        CC = RT[:, 1920:2560].rearrange("p (i e) -> p i e", i=NT)
        LQ = RT[:, 0:2560].rearrange("p (a q) -> p a q", a=20)
        RP = RT[:, 2560:3200].rearrange("p (a r) -> p a r", a=20)
        SELf = SEL.rearrange("p i k -> p (i k)")
        POSf = POS.rearrange("p i k -> p (i k)")

        w = [t_best]

        def v(call, *args, after=(), **kw):
            w[0] = put("dve", call, *args, after=[w[0], *after], **kw)
            return w[0]

        v(V.memset, SC8[:, :, 4:8], -3.0e38)
        v(V.tensor_copy, SC8[:, :, 0:4], MX[:, :, :, 0])
        v(V.tensor_copy, CAND, MI[:, :, :, 0])
        top = [put("dve", V.max, T8[:, i, :], SC8[:, i, :], after=[w[0]]) for i in range(NT)]
        for i in range(NT):
            w[0] = put("dve", V.max_index, TI[:, i, :], T8[:, i, :], SC8[:, i, :], after=[top[i]])
        v(V.tensor_copy, TOP, TI[:, :, 0:2])
        for h in range(4):
            dst = SEL if h == 0 else PR4
            v(V.scalar_tensor_tensor, dst, TOP, float(h), CAND[:, :, h:h + 1].broadcast_to([128, NT, 2]),
              ALU.is_equal, ALU.mult)
            if h:
                v(V.tensor_tensor, SEL, SEL, PR4, ALU.add)
        v(V.scalar_tensor_tensor, SEL, VAL.unsqueeze(2).broadcast_to([128, NT, 2]), -1000.0, SEL, ALU.mult, ALU.add)
        v(V.tensor_tensor, OHE, IOTA[:, 0:NEXP].unsqueeze(1).broadcast_to([128, 20, NEXP]).rearrange(
            "p (i k) e -> p i k e", k=2) if False else IOTA[:, 0:NEXP].unsqueeze(1).unsqueeze(1).broadcast_to(
            [128, NT, 2, NEXP]), SEL.unsqueeze(3).broadcast_to([128, NT, 2, NEXP]), ALU.is_equal,
          after=[p_tr])
        a0 = v(V.tensor_tensor, OHS, OHE[:, :, 0, :], OHE[:, :, 1, :], ALU.add)
        b0 = put("dve", V.tensor_copy, TRIB[:, :], TRI)
        for i in range(NT):
            bk = (nb + i // 5) % 8
            o = 64 * (i % 5)
            for j in range(i):
                put("pe", mm, PS[:, bk, o:o + 64], ONEB[:, :], OHS[:, j, :], start=(j == 0), stop=False,
                    after=[a0, t_m3] + free[bk], signal=False)
            p = put("pe", mm, PS[:, bk, o:o + 64], TRIB[:, :], OHS[:, i, :], start=(i == 0), stop=True,
                    after=[a0, b0] + free[bk])
        c0 = []
        for h in range(2):
            bk = (nb + h) % 8
            c0.append(v(V.tensor_copy, CC[:, 5 * h:5 * h + 5, :],
                        PS[:, bk, 0:320].rearrange("p (i e) -> p i e", i=5), after=[p]))
            free[bk] = [c0[-1]]
        nb += 2
        for k in range(2):
            v(V.tensor_tensor, PRD, OHE[:, :, k, :], CC, ALU.mult)
            v(V.tensor_reduce, POS[:, :, k:k + 1], PRD, AX.X, ALU.add)
        v(V.tensor_tensor, PR4[:, :, 0:1], SEL[:, :, 0:1], SEL[:, :, 1:2], ALU.is_equal)
        v(V.tensor_tensor, POS[:, :, 1:2], POS[:, :, 1:2], PR4[:, :, 0:1], ALU.add)
        a0 = v(V.tensor_reduce, EST[:, 3:4], POSf, AX.X, ALU.max)
        bk = nb % 8
        nb += 1
        p = put("pe", nc.tensor.transpose, PS[0:1, bk, 0:128], EST[:, 3:4], IDN, after=[a0] + free[bk])
        a0 = put("dve", V.tensor_reduce, FLAG[0:1, 1:2], PS[0:1, bk, 0:128], AX.X, ALU.max, after=[p])
        free[bk] = [a0]
        t_full = put("dve", V.tensor_copy, FLAGI[0:1, 1:2], FLAG[0:1, 1:2], after=[a0])
        v(V.tensor_copy, SELI, SELf)
        v(V.tensor_scalar, ODD.bitcast(I32), SELI, 1, None, ALU.bitwise_and)
        v(V.tensor_scalar, PAIR.bitcast(I32), SELI, 1, None, ALU.arith_shift_right)
        v(V.tensor_copy, ODD, ODD.bitcast(I32))
        v(V.tensor_copy, PAIR, PAIR.bitcast(I32))
        v(V.scalar_tensor_tensor, QP, ODD, 64.0, POSf, ALU.mult, ALU.add)
        v(V.tensor_scalar, ODD, POSf, 64.0, 1000.0, ALU.is_ge, ALU.mult)
        v(V.tensor_tensor, QP, QP, ODD, ALU.add)
        bk = nb % 8
        nb += 1
        for h in range(2):
            hs = slice(10 * h, 10 * h + 10)
            v(V.tensor_tensor, RP[:, hs, :], IOTA[:, 0:32].unsqueeze(1).broadcast_to([128, 10, 32]),
              PAIR[:, hs].unsqueeze(2).broadcast_to([128, 10, 32]), ALU.is_equal)
            v(V.tensor_tensor, RP[:, hs, :], RP[:, hs, :], AID[:, hs].unsqueeze(2).broadcast_to([128, 10, 32]),
              ALU.mult)
            v(V.tensor_tensor, LQ[:, hs, :], IOTA[:, 0:128].unsqueeze(1).broadcast_to([128, 10, 128]),
              QP[:, hs].unsqueeze(2).broadcast_to([128, 10, 128]), ALU.is_equal)
            for j in range(10 * h, 10 * h + 10):
                p = put("pe", mm, PS[:, bk, 0:32], LQ[:, j, :], RP[:, j, :], start=(j == 0), stop=(j == 19),
                        after=[w[0]] + free[bk], signal=(j == 19))
        v(V.tensor_copy, VIDX[:, 0, :], PS[:, bk, 0:32], after=[p])
        free[bk] = [w[0]]
        p_idx = p
        v(V.tensor_scalar, VIDX[:, 1, :], VIDX[:, 0, :], 1.0, -1.0, ALU.max, ALU.add)
        v(V.tensor_copy, TIDX[:, :], VIDX[:, 1, :])
        t_tidx = v(V.tensor_scalar, TIDX[:, :], TIDX[:, :], 1, None, ALU.arith_shift_right)
        v(V.tensor_scalar, VIDX[:, 1, :], VIDX[:, 0, :], 0.5, 8192.0, ALU.is_lt, ALU.mult)
        v(V.scalar_tensor_tensor, VIDX[:, 1, :], VIDX[:, 0, :], -1.0, VIDX[:, 1, :], ALU.add, ALU.add)
        t_scidx = v(V.tensor_copy, SCIDX[:, :], VIDX[:, 1, :])
        load_expert(RT[:, 0:2048], [p_idx, w[0]])
        load_expert(RT[:, 2048:4096], [p_idx])

        GXf = GE2[:, 0:4608]
        XG = GXf[:, 0:1536].rearrange("p (s d) -> p s d", s=3)
        XTT = GXf[:, 1536:2560].rearrange("p (s d) -> p s d", s=2)
        HT = GXf[:, 2560:3072].rearrange("p (s d) -> p s d", s=2)
        YS = GXf[:, 3072:4608].rearrange("p (s d) -> p s d", s=3)
        t_xg, xg_free = {}, {}

        def gather_pair(r):
            s = r % 3
            t_xg[r] = dma("pool", f"xg{s}", out=XG[:, s, :], out_offset=None, in_=xx_d[:, :],
                          in_offset=bass.IndirectOffsetOnAxis(ap=TIDX[:, r:r + 1], axis=0), indirect=True,
                          after=[t_tidx, t_xxs[-1], t_xxs[-2], p_lg, p_tr] + ([xg_free[r - 3]] if r >= 3 else []))

        for r in range(2):
            gather_pair(r)
        st2 = {}

        def tr(r):
            s, bk = r % 2, r % 2
            for k in range(4):
                p = put("pe", nc.tensor.transpose, PS[:, bk, 128 * k:128 * k + 128], XG[:, r % 3, 128 * k:128 * k + 128],
                        IDN, after=[t_xg[r]] + free[bk], signal=(k == 3))
            xg_free[r] = p
            a1 = put("act" if r % 2 else "dve", A.copy if r % 2 else V.tensor_copy, XTT[:, s, :], PS[:, bk, :],
                     after=[p] + ([st2["h", r - 2][1]] if r >= 2 else []))
            free[bk] = [a1]
            st2["x", r] = a1

        def up(r):
            s, bk = r % 2, 2 + r % 2
            for j in range(2):
                buf, t_e = loads[2 * r + j]
                for f2 in range(2):
                    for k in range(4):
                        p = put("pe", mm, PS[:, bk, 128 * j + 64 * f2:128 * j + 64 * f2 + 64],
                                buf[:, 256 * k + 128 * f2:256 * k + 128 * f2 + 128],
                                XTT[:, s, 128 * k + 64 * j:128 * k + 64 * j + 64], start=(k == 0), stop=(k == 3),
                                after=[t_e, st2["x", r]] + free[bk], signal=(j == 1 and f2 == 1 and k == 3))
            a1 = put("act", A.activation, HT[:, s, :], PS[:, bk, 0:256], ACT.Gelu,
                     after=[p] + ([st2["y", r - 2]] if r >= 2 else []))
            free[bk] = [a1]
            st2["h", r] = (a1, p)

        t_ys = {}
        t_sc = []

        def down(r):
            s, bk = r % 2, 4 + r % 2
            for j in range(2):
                buf, t_e = loads[2 * r + j]
                for f2 in range(2):
                    p = put("pe", mm, PS[64 * j:64 * j + 64, bk, :],
                            HT[:, s, 128 * j + 64 * f2:128 * j + 64 * f2 + 64],
                            buf[:, 1024 + 512 * f2:1024 + 512 * f2 + 512], start=(f2 == 0), stop=(f2 == 1),
                            after=[st2["h", r][0]] + free[bk], signal=(j == 1 and f2 == 1))
            st2["y", r] = p
            a1 = put("dve", V.tensor_copy, YS[:, r % 3, :], PS[:, bk, :],
                     after=[p] + ([t_ys[r - 3]] if r >= 3 else []))
            free[bk] = [a1]
            t_ys[r] = dma("pool", f"ys{r % 3}", out=y_d[:, :], out_offset=bass.IndirectOffsetOnAxis(
                ap=SCIDX[:, r:r + 1], axis=0), in_=YS[:, r % 3, :], in_offset=None, bounds_check=2 * N - 1,
                oob_is_err=False, indirect=True, after=[a1, t_scidx, t_yz[-1]])
            for j in range(2):
                load_expert(loads[2 * r + j][0], [p])

        for r in range(34):
            if r < 32:
                tr(r)
            if 0 <= r - 1 < 32:
                up(r - 1)
            if r + 2 < 32:
                gather_pair(r + 2)
            if 0 <= r - 2 < 32:
                down(r - 2)

        M2 = CAP - 64
        fu = {n: pr.sem("fu_" + n) for n in
              ("load", "idx", "w", "row", "xt", "xc", "up", "gelu", "down", "yc", "sc", "xg", "ys", "hid", "dve", "tab", "end")}
        L2 = RH[:, 0:20 * M2].rearrange("p (a q) -> p a q", a=20)
        R2 = RH[:, 2048:2048 + 20 * NEXP].rearrange("p (a e) -> p a e", a=20)
        V2 = RH[0:M2, 4096:4096 + NEXP]
        V3 = RH[0:M2, 4160:4160 + NEXP]
        T2 = RH[0:M2, 4224:4224 + NEXP].bitcast(I32)
        S2 = RH[0:M2, 4288:4288 + NEXP].bitcast(I32)
        IT, IS = RH[0:M2, 4352:4353].bitcast(I32), RH[0:M2, 4353:4354].bitcast(I32)

        def full(body):
            def run(eng):
                most = eng.value_load(FLAGI[0:1, 1:2], min_val=0, max_val=2 * N)
                with eng.If(most >= 64):
                    body(eng)
            return run

        def take(eng, name, value):
            eng.wait_ge(fu[name], value)
            eng.sem_clear(fu[name])

        def full_dve(eng):
            n = [0]

            def link(ins):
                n[0] += 1
                ins.then_inc(fu["dve"], 1)
                eng.wait_ge(fu["dve"], n[0])

            link(V.tensor_scalar(QP, POSf, -64.0, None, ALU.add))
            link(V.tensor_tensor(L2, IOTA[:, 0:M2].unsqueeze(1).broadcast_to([128, 20, M2]),
                                 QP.unsqueeze(2).broadcast_to([128, 20, M2]), ALU.is_equal))
            link(V.tensor_tensor(R2, IOTA[:, 0:NEXP].unsqueeze(1).broadcast_to([128, 20, NEXP]),
                                 SELf.unsqueeze(2).broadcast_to([128, 20, NEXP]), ALU.is_equal))
            link(V.tensor_tensor(R2, R2, AID.unsqueeze(2).broadcast_to([128, 20, NEXP]), ALU.mult))
            V.memset(DC[:, 0:1], 0.0).then_inc(fu["tab"], 1)
            take(eng, "up", 1)
            link(V.tensor_copy(V2, PS[0:M2, 0, 0:NEXP]))
            link(V.tensor_scalar(V3, V2, 1.0, -1.0, ALU.max, ALU.add))
            link(V.tensor_copy(T2, V3))
            link(V.tensor_scalar(T2, T2, 1, None, ALU.arith_shift_right))
            link(V.tensor_scalar(V3, V2, 0.5, 8192.0, ALU.is_lt, ALU.mult))
            link(V.scalar_tensor_tensor(V3, V2, -1.0, V3, ALU.add, ALU.add))
            link(V.tensor_copy(S2, V3))
            eng.sem_clear(fu["dve"])
            with eng.Fori(0, NEXP) as e:
                n[0] = 0
                link(V.tensor_copy(IT, T2[:, bass.ds(e, 1)]))
                link(V.tensor_copy(IS, S2[:, bass.ds(e, 1)]))
                eng.sem_clear(fu["dve"])
                V.memset(DC[:, 0:1], 0.0).then_inc(fu["load"], 1)
                V.memset(DC[:, 1:2], 0.0).then_inc(fu["idx"], 1)
                take(eng, "xt", 1)
                V.tensor_copy(XTT[:, 0, :].rearrange("p (k n) -> p k n", k=4)[:, :, 0:M2],
                              PS[:, 0, :].rearrange("p (k n) -> p k n", k=4)[:, :, 0:M2]).then_inc(fu["xc"], 1)
                take(eng, "down", 1)
                V.tensor_copy(YS[0:M2, 0, :], PS[0:M2, 4, :]).then_inc(fu["yc"], 1)
                take(eng, "sc", 1)
            V.memset(DC[:, 1:2], 0.0).then_inc(fu["end"], 1)

        def full_pool(eng):
            with eng.Fori(0, NEXP):
                take(eng, "idx", 1)
                G.indirect_dma_start(out=XG[0:M2, 0, :], out_offset=None, in_=xx_d[:, :],
                                     in_offset=bass.IndirectOffsetOnAxis(ap=IT, axis=0)).then_inc(fu["xg"], 16)
                eng.drain().then_inc(fu["row"], 1)
                take(eng, "yc", 1)
                G.indirect_dma_start(out=y_d[:, :], out_offset=bass.IndirectOffsetOnAxis(ap=IS, axis=0),
                                     in_=YS[0:M2, 0, :], in_offset=None, bounds_check=2 * N - 1,
                                     oob_is_err=False).then_inc(fu["ys"], 16)
                eng.drain().then_inc(fu["sc"], 1)

        def full_sp(eng):
            with eng.Fori(0, NEXP) as e:
                take(eng, "load", 1)
                eng.dma_start(EX[:, :], we_in[bass.ds(e, 1), :, :].rearrange("a p n -> (a p) n")).then_inc(fu["w"], 16)
            take(eng, "end", 1)

        def full_act(eng):
            with eng.Fori(0, NEXP):
                take(eng, "gelu", 1)
                A.activation(HT[:, 0, 0:2 * M2], PS[:, 2, 0:2 * M2], ACT.Gelu).then_inc(fu["hid"], 1)

        def full_pe(eng):
            take(eng, "tab", 1)
            for j in range(20):
                last = mm(PS[0:M2, 0, 0:NEXP], L2[:, j, :], R2[:, j, :], start=(j == 0), stop=(j == 19))
            last.then_inc(fu["up"], 1)
            with eng.Fori(0, NEXP):
                take(eng, "row", 1)
                for k in range(4):
                    last = nc.tensor.transpose(PS[:, 0, 128 * k:128 * k + M2], XG[0:M2, 0, 128 * k:128 * k + 128],
                                               IDN[0:M2, 0:M2])
                last.then_inc(fu["xt"], 1)
                take(eng, "xc", 1)
                take(eng, "w", 16)
                for f2 in range(2):
                    for k in range(4):
                        last = mm(PS[:, 2, M2 * f2:M2 * f2 + M2], EX[:, 256 * k + 128 * f2:256 * k + 128 * f2 + 128],
                                  XTT[:, 0, 128 * k:128 * k + M2], start=(k == 0), stop=(k == 3))
                last.then_inc(fu["gelu"], 1)
                take(eng, "hid", 1)
                for f2 in range(2):
                    last = mm(PS[0:M2, 4, :], HT[:, 0, M2 * f2:M2 * f2 + M2],
                              EX[:, 1024 + 512 * f2:1024 + 512 * f2 + 512], start=(f2 == 0), stop=(f2 == 1))
                last.then_inc(fu["down"], 1)

        for eng, body in (("sp", full_sp), ("dve", full_dve), ("act", full_act), ("pool", full_pool), ("pe", full_pe)):
            pr.raw(eng, full(body), after=[t_full, st2["y", 31], t_ys[29], t_ys[30], t_ys[31]])

        YL = RH[:, 0:10240].rearrange("p (i a d) -> p i a d", i=NT, a=2)
        yv = y_d.rearrange("(t a) d -> t a d", a=2)
        t_out = []
        lastp = st2["y", 31]
        for i in range(NT):
            n = rows(i)
            t = dma("sp", f"yl{i}", YL[0:n, i, :, :], yv[128 * i:128 * i + n, :, :],
                    after=[t_ys[29], t_ys[30], t_ys[31], lastp])
            a1 = put("dve", V.tensor_tensor, YL[0:n, i, 0, :], YL[0:n, i, 0, :], YL[0:n, i, 1, :], ALU.add, after=[t])
            a1 = put("dve", V.scalar_tensor_tensor, YL[0:n, i, 0, :], YL[0:n, i, 0, :], 0.5, XA[0:n, i, :], ALU.mult,
                     ALU.add, after=[a1])
            t_out.append(dma("act", "out", out[128 * i:128 * i + n, :], YL[0:n, i, 0, :], after=[a1]))
        pr.raw("act", lambda e: None, after=[t_out[-1], *t_xns[-6:], t_xxs[-1], t_xxs[-2], t_yz[-1]])

        block = ctx.enter_context(nc.Block())
        block.sync(lambda eng: pr.replay("sp", eng))
        block.gpsimd(lambda eng: pr.replay("pool", eng))
        block.scalar(lambda eng: pr.replay("act", eng))
        block.vector(lambda eng: pr.replay("dve", eng))
        block.tensor(lambda eng: pr.replay("pe", eng))


def constants(np):
    c = np.zeros((128, 703), np.float32)
    p = np.arange(128)
    c[:, 0:128] = np.eye(128)
    c[:, 128:256] = p[:, None] < p[None, :]
    c[:, 256:512] = np.arange(256)[None, :]
    c[:, 512:640] = (p[:, None] // 64) == (p[None, :] // 64)
    c[:, 670] = p < 32
    for q in range(128):
        for r in range(4):
            c[q, 671 + 8 * r + 2 * r + q // 64] = 1
    for i in range(NT):
        c[:, 640 + i] = (128 * i + p) >= N
        for k in range(2):
            c[:, 650 + 2 * i + k] = 2 * (128 * i + p) + k + 1
    return c


def kernel(**inputs):
    import numpy as np
    import concourse.bacc as _bacc
    from concourse import mybir as _mybir
    from concourse.bass_utils import run_bass_kernel_spmd as _run

    g = {k: np.asarray(v) for k, v in inputs.items()}

    def edges(a, mode):
        a = np.pad(a, (0, NG * GE - NE), mode=mode)
        return np.ascontiguousarray(a.reshape(NG, GE))

    def cols(a):
        return a.reshape(-1, 128).T

    vec = np.concatenate([cols(g["L0_gnn_b1"]), cols(g["L0_gnn_g1"]), cols(g["L0_gnn_be1"]), cols(g["L0_gnn_b2"]),
                          cols(g["L0_gnn_g2"]), cols(g["L0_gnn_be2"]), cols(g["L0_mix_bq"]),
                          np.broadcast_to(g["L0_gnn_eps"].reshape(1, 1), (128, 1))], axis=1)
    brow = np.concatenate([np.broadcast_to(g[k][None, :], (128, D)) for k in ("L0_mix_bk", "L0_mix_bv", "L0_mix_bp")],
                          axis=1)
    we = np.concatenate([
        g["L0_ffn_W1"].reshape(NEXP, 4, 128, 256).transpose(0, 2, 1, 3).reshape(NEXP, 128, 1024),
        g["L0_ffn_W2"].reshape(NEXP, 2, 128, 512).transpose(0, 2, 1, 3).reshape(NEXP, 128, 1024)], axis=2)
    arrays = {
        "x": g["x"], "src": edges(g["src"], "constant"), "dst": edges(g["dst"], "edge"),
        "w1g": g["L0_gnn_W1"], "w2g": g["L0_gnn_W2"],
        "wqkvp": np.stack([g["L0_mix_Wk"], g["L0_mix_Wv"], g["L0_mix_Wq"], g["L0_mix_Wp"]]),
        "hp": g["L0_ffn_hash_proj"].transpose(1, 0, 2).reshape(D, 256),
        "vec": vec, "brow": brow, "cst": constants(np), "we": we,
    }
    nc = _bacc.Bacc("TRN2", target_bir_lowering=False, num_devices=1)
    ins, args = {}, []
    for name, a in arrays.items():
        a = np.ascontiguousarray(a)
        ins[f"in_{name}"] = a
        args.append(nc.dram_tensor(f"in_{name}", a.shape, _mybir.dt.from_np(a.dtype), kind="ExternalInput").ap())
    out = nc.dram_tensor("out_0", (N, D), _mybir.dt.float32, kind="ExternalOutput").ap()
    gnn_mix_moe(nc, *args, out)
    r = _run(nc, [ins], core_ids=[0])
    return r.results[0]["out_0"]
```

```python
import concourse.bass as bass
from concourse import mybir
from contextlib import ExitStack

F32 = mybir.dt.float32
I32 = mybir.dt.int32
U32 = mybir.dt.uint32
BF16 = mybir.dt.bfloat16
F32R = mybir.dt.float32r
ALU = mybir.AluOpType
ACT = mybir.ActivationFunctionType
AX = mybir.AxisListType

N = 1250
NT = 10
D = 512
HID = 1024
NE = 20000
GE = 256
NG = 79
RING = 4
WIN = 64
AGW = 1316
NX, NY = 9, 6
CH = [(0, 418), (418, 416), (834, 416)]
NEXP = 64
CAP = 156


def rows(i):
    return min(128, N - 128 * i)


class Program:

    def __init__(self, nc, ctx):
        self.nc = nc
        self.ctx = ctx
        self.queue = {e: [] for e in ("pe", "dve", "act", "pool", "sp")}
        self.count = {}
        self.sems = {}

    def sem(self, name):
        if name not in self.sems:
            self.sems[name] = self.ctx.enter_context(self.nc.semaphore("s_" + name))
            self.count[name] = 0
        return self.sems[name]

    def put(self, eng, call, *args, after=(), signal=True, **kw):
        s = self.sem(eng)
        if signal:
            self.count[eng] += 1
        self.queue[eng].append((call, args, kw, list(after), s if signal else None, 1))
        return (eng, self.count[eng])

    def dma(self, eng, name, *args, after=(), indirect=False, **kw):
        s = self.sem(name)
        self.count[name] += 16
        nc = self.nc
        engine = {"sp": nc.sync, "act": nc.scalar, "pool": nc.gpsimd}[eng]
        call = engine.indirect_dma_start if indirect else engine.dma_start
        self.queue[eng].append((call, args, kw, list(after), s, 16))
        return (name, self.count[name])

    def raw(self, eng, fn, after=()):
        self.queue[eng].append((None, fn, None, list(after), None, 0))

    def replay(self, eng, engine):
        seen = {}
        for call, args, kw, after, s, by in self.queue[eng]:
            for name, value in after:
                if seen.get(name, 0) < value:
                    engine.wait_ge(self.sems[name], value)
                    seen[name] = value
            if call is None:
                args(engine)
                continue
            ins = call(*args, **kw)
            if s is not None:
                ins.then_inc(s, by)


def gnn_mix_moe(nc, x_in, src_in, dst_in, w1g, w2g, wqkvp, hp_in, vec_in, brow_in, cst_in, we_in, out):
    xn_d = nc.dram_tensor("xn_rows", [N, 3 * D], BF16, kind="Internal").ap()
    xx_d = nc.dram_tensor("xx_rows", [N, D], F32, kind="Internal").ap()
    y_d = nc.dram_tensor("y_rows", [2 * N, D], F32, kind="Internal").ap()

    with ExitStack() as ctx:
        def sb(name, shape, dt=F32):
            return ctx.enter_context(nc.sbuf_tensor(name, shape, dt))

        pr = Program(nc, ctx)
        put, dma = pr.put, pr.dma
        mm = nc.tensor.matmul
        V, A, G = nc.vector, nc.scalar, nc.gpsimd

        at, place, ROUND = 0, {}, {}
        with ExitStack() as names:
            for name, size in (("RH", 10280), ("RT", 5000), ("RG", 4 * AGW), ("RQ", 5000), ("RW", 8192), ("GE2", 6656),
                               ("TMP", 2048), ("BROW", 1536)):
                place[name] = (at, at + size)
                at += size
                ROUND[name] = names.enter_context(nc.sbuf_tensor("ROUND_" + name, [128, size], F32R))
        BIG1 = sb("BIG1", [128, 20544])
        BIG2 = sb("BIG2", [128, 43976 - 20544])

        def big(first, size):
            return BIG1[:, first:first + size] if first < 20544 else BIG2[:, first - 20544:first - 20544 + size]

        def region(name):
            return big(place[name][0], place[name][1] - place[name][0])

        def rounded(name, first, size):
            return ROUND[name][:, first:first + size]

        RH, RT, RQ, RW, GE2, RGf = (region(n) for n in ("RH", "RT", "RQ", "RW", "GE2", "RG"))
        RG = RGf.rearrange("p (k n) -> p k n", k=4)
        GX = GE2[:, 0:6144].bitcast(BF16).rearrange("p (r j d) -> p r j d", r=RING, j=2)
        EX = GE2[:, 0:2048]
        TMP = region("TMP").rearrange("p (a d) -> p a d", a=4)
        BROW = region("BROW").rearrange("p (a d) -> p a d", a=3)
        XA = sb("XA", [128, NT, D])
        CST = sb("CST", [128, 743])
        VEC = sb("VEC", [128, 41])
        XG4 = sb("XG4", [128, D])
        KVB = sb("KVB", [128, 4, 128])
        KSB = sb("KSB", [128, 4, 128])
        KS8 = sb("KS8", [128, 4, 8])
        RS = RW[0:NG, 6144:6144 + GE].bitcast(I32)
        RD = RW[0:NG, 6656:6656 + GE].bitcast(I32)
        RSF = TMP[0:NG, 0, 0:GE]
        RDF = TMP[0:NG, 1, 0:GE]
        ZERO = KVB[:, :, :].rearrange("p r e -> p (r e)")
        EST = sb("EST", [128, 4])
        EROWI = sb("EROWI", [1, 80], I32)
        FLAG = sb("FLAG", [1, 4])
        FLAGI = sb("FLAGI", [1, 4], I32)
        SIDX = sb("SIDX", [128, 2, NG], I32)
        DREL = sb("DREL", [128, 2, NG])
        DABS = sb("DABS", [128, 2, NG])
        DC = sb("DC", [128, 2])
        IC = sb("IC", [128, 2], I32)
        OH = sb("OH", [128, 2, 2, WIN], BF16)
        ST = sb("ST", [128, NT, 6])
        MV = sb("MV", [128, NT, 2])
        RR = sb("RR", [128, NT])
        BST = sb("BST", [128, 2, 3, 6])
        BMV = sb("BMV", [128, 2, 8])
        NBQ = sb("NBQ", [128, 4])
        OPE = sb("OPE", [128, 1])
        TRIB = sb("TRIB", [128, 128], BF16)
        ONEB = sb("ONEB", [128, 128], BF16)
        TIDX = sb("TIDX", [128, 32], I32)
        SCIDX = sb("SCIDX", [128, 32], I32)
        VIDX = sb("VIDX", [128, 2, 32])

        PS = ctx.enter_context(nc.psum_tensor("PS", [128, 8, 512], F32))

        IDN = CST[:, 0:128]
        TRI = CST[:, 128:256]
        IOTA = CST[:, 256:512]
        BD = CST[:, 512:640]
        VAL = CST[:, 640:650]
        AID = CST[:, 650:670]
        M32 = CST[:, 670:671]
        AHI, ALO = CST[:, 703:723], CST[:, 723:743]
        M8 = CST[:, 671:703].rearrange("p (r h) -> p r h", r=4)
        b1, g1, be1 = VEC[:, 0:8], VEC[:, 8:16], VEC[:, 16:24]
        b2, g2, be2, bq = VEC[:, 24:28], VEC[:, 28:32], VEC[:, 32:36], VEC[:, 36:40]

        XN = RH[:, 0:5120].rearrange("p (i d) -> p i d", i=NT)
        KK = XN
        VA = RH[:, 5120:10280].rearrange("p (i r c) -> p i r c", i=NT, r=4)
        H1 = RH[:, 0:10000].rearrange("p (t n) -> p t n", t=8)
        XT = RT[:, :].rearrange("p (k n) -> p k n", k=4)
        ZR = XG4[0:8, 0:418]
        QT = RH[:, 0:5000].rearrange("p (k n) -> p k n", k=4)
        WQ = RW[:, 0:2048].rearrange("p (k n) -> p k n", k=4)
        WK = RW[:, 2048:4096].rearrange("p (k n) -> p k n", k=4)
        WV = RW[:, 4096:6144].rearrange("p (k n) -> p k n", k=4)
        WP = RW[:, 6144:8192].rearrange("p (k n) -> p k n", k=4)
        W1 = RW[:, 0:4096].rearrange("p (k n) -> p k n", k=4)
        W2 = RW[:, 4096:8192].rearrange("p (k n) -> p k n", k=8)
        HP = RGf[:, 0:1024].rearrange("p (k n) -> p k n", k=4)
        H2 = XT
        XTH = rounded("RQ", 0, 5000).rearrange("p (k n) -> p k n", k=4)
        XTL = rounded("RT", 0, 5000).rearrange("p (k n) -> p k n", k=4)
        OUH = rounded("RH", 5120, 5000).rearrange("p (k n) -> p k n", k=4)
        OUL = rounded("RH", 0, 5000).rearrange("p (k n) -> p k n", k=4)
        WH, WL = {}, {}
        for nm, hi, lo in (("k", 6144, 2048), ("v", 0, 4096), ("q", 2048, 0), ("p", 4096, 6144)):
            WH[nm] = rounded("RW", hi, 2048).rearrange("p (k n) -> p k n", k=4)
            WL[nm] = rounded("RW", lo, 2048).rearrange("p (k n) -> p k n", k=4)
        HTH = rounded("RT", 0, 5000).rearrange("p (k n) -> p k n", k=4)
        HTL = rounded("RG", 0, 4 * AGW).rearrange("p (k n) -> p k n", k=4)
        W1H = rounded("GE2", 0, 4096).rearrange("p (k n) -> p k n", k=4)
        W1L = rounded("RW", 0, 4096).rearrange("p (k n) -> p k n", k=4)
        W2H = rounded("RQ", 0, 4096).rearrange("p (k n) -> p k n", k=8)
        W2L = rounded("RW", 4096, 4096).rearrange("p (k n) -> p k n", k=8)
        H1H = []
        for name, first, step in (("GE2", 4096, 416), ("GE2", 4096 + N, 416), ("TMP", 0, 416), ("BROW", 0, 416),
                                  ("GE2", 0, 1024), ("RW", 0, 1024), ("GE2", 420, 1024), ("RW", 420, 1024)):
            more = 2 if step == 416 else 0
            H1H.append([rounded(name, first + (step * c + more if c else 0), w) for c, (_, w) in enumerate(CH)])
        H1L = rounded("RH", 0, 10000).rearrange("p (t n) -> p t n", t=8)

        free = {b: [] for b in range(8)}

        t_x = [None] * NT
        t_rd = dma("sp", "rd", RD, dst_in[:, :])
        t_rs = dma("sp", "rs", RS, src_in[:, :])
        t_cst = dma("act", "cst", CST[:, :], cst_in[:, :])
        t_vec = dma("act", "vec", VEC[:, :], vec_in[:, :])
        for i in range(NT):
            t_x[i] = dma("sp", f"x{i}", XA[0:rows(i), i, :], x_in[128 * i:128 * i + rows(i), :])
        t_w = {}

        def load_w(eng, nm, after=()):
            j, w = {"k": (0, WK), "v": (1, WV), "q": (2, WQ), "p": (3, WP)}[nm]
            t_w[nm] = dma(eng, "w" + nm, w, wqkvp[j].rearrange("(k p) n -> p k n", p=128), after=after)

        t_ws = {}

        def split_w(nm, after):
            raw = {"k": WK, "v": WV, "q": WQ, "p": WP}[nm]
            for k in range(4):
                a1 = put("dve", V.tensor_copy, WH[nm][:, k, :], raw[:, k, :], after=[t_w[nm]] + after)
                t_ws[nm, k] = put("dve", V.tensor_tensor, WL[nm][:, k, :], raw[:, k, :], WH[nm][:, k, :].bitcast(F32),
                                  ALU.subtract, after=[a1])

        def products(out, ah, al, bh, bl, first, last, after, signal):
            put("pe", mm, out, ah, bh, start=first, stop=False, after=after, signal=False)
            put("pe", mm, out, ah, bl, start=False, stop=False, signal=False)
            return put("pe", mm, out, al, bh, start=False, stop=last, signal=signal)

        load_w("sp", "k")
        t_brow = dma("sp", "brow", BROW[:, :, :], brow_in.rearrange("p (a d) -> p a d", a=3))

        t_m1 = put("pool", G.memset, MV[:, :, :], 1.0)
        t_m2 = put("pool", G.memset, VA[:, :, :, 128:129], 1.0)
        t_m3 = put("pool", G.memset, ONEB[:, :], 1.0)
        t_gz = put("pool", G.memset, RG[:, :, N:AGW], 0.0)
        t_st = {}

        def stats(i):
            n = rows(i)
            s = put("dve", V.bn_stats, ST[0:n, i, :], XA[0:n, i, :], after=[t_x[i], t_m1])
            t_st[i] = put("dve", V.bn_aggr, MV[0:n, i, :], ST[0:n, i, :], after=[s])

        def root(h):
            hs = slice(5 * h, 5 * h + 5)
            s = put("dve", V.tensor_scalar, RR[:, hs], MV[:, hs, 1], 1e-5, None, ALU.add, after=[t_st[5 * h + 4]])
            s = put("act", A.activation, RR[:, hs], RR[:, hs], ACT.Sqrt, after=[s])
            return put("dve", V.reciprocal, RR[:, hs], RR[:, hs], after=[s])

        a = put("dve", V.tensor_copy, RDF, RD, after=[t_rd])
        b = put("dve", V.tensor_copy, RSF, RS, after=[t_rs])
        c = put("dve", V.tensor_reduce, EST[0:NG, 0:1], RDF, AX.X, ALU.min, after=[a])
        d = put("dve", V.tensor_reduce, EST[0:NG, 1:2], RDF, AX.X, ALU.max, after=[a])
        e = put("dve", V.tensor_tensor, EST[0:NG, 2:3], EST[0:NG, 1:2], EST[0:NG, 0:1], ALU.subtract, after=[c, d])
        for j in range(2):
            m = put("pe", nc.tensor.transpose, PS[:, 3, 96 * j:96 * j + NG], RDF[:, 128 * j:128 * j + 128],
                    IDN[0:NG, 0:NG], after=[a, t_cst], signal=(j == 1))
        stats(0)
        pv = PS[:, 3, 0:192].rearrange("p (j g) -> p j g", j=2)[:, :, 0:NG]
        t_dabs = put("dve", V.tensor_copy, DABS[:, :, :], pv, after=[m])
        free[3] = [t_dabs]
        f = put("dve", V.tensor_scalar, RDF, RDF, EST[0:NG, 0:1], None, ALU.subtract, after=[c, d, m])
        for j in range(2):
            put("pe", nc.tensor.transpose, PS[:, 0, 96 * j:96 * j + NG], RDF[:, 128 * j:128 * j + 128],
                IDN[0:NG, 0:NG], after=[f, b, t_cst], signal=False)
            put("pe", nc.tensor.transpose, PS[:, 1, 96 * j:96 * j + NG], RSF[:, 128 * j:128 * j + 128],
                IDN[0:NG, 0:NG], signal=False)
        put("pe", nc.tensor.transpose, PS[0:1, 2, 0:NG], EST[0:NG, 0:1], IDN[0:NG, 0:NG], after=[e], signal=False)
        m = put("pe", nc.tensor.transpose, PS[0:1, 2, 128:128 + NG], EST[0:NG, 2:3], IDN[0:NG, 0:NG])
        stats(1)
        stats(2)
        pv = PS[:, 0, 0:192].rearrange("p (j g) -> p j g", j=2)[:, :, 0:NG]
        t_drel = put("dve", V.tensor_copy, DREL[:, :, :], pv, after=[m])
        pv = PS[:, 1, 0:192].rearrange("p (j g) -> p j g", j=2)[:, :, 0:NG]
        t_sidx = put("dve", V.tensor_copy, SIDX[:, :, :], pv, after=[m])
        t_erow = put("dve", V.tensor_copy, EROWI[0:1, 0:NG], PS[0:1, 2, 0:NG], after=[m])
        s = put("dve", V.tensor_reduce, FLAG[0:1, 0:1], PS[0:1, 2, 128:128 + NG], AX.X, ALU.max, after=[m])
        t_flag = put("dve", V.tensor_copy, FLAGI[0:1, 0:1], FLAG[0:1, 0:1], after=[s])
        free[0] = [t_drel]
        free[1] = [t_sidx]
        free[2] = [t_flag]
        t_edges = [a, b]
        for r in range(4):
            m = put("pe", nc.tensor.transpose, PS[0:8, 5, 128 * r:128 * r + 128], M8[:, r, :], IDN, after=[t_cst],
                    signal=(r == 3))
        t_s8 = put("act", A.copy, KSB[0:8, :, :].rearrange("p r e -> p (r e)"), PS[0:8, 5, :], after=[m])
        free[5] = [t_s8]

        t_xn, t_xns, t_xt, t_acc = [], [], [], []
        t_rem = [[], []]
        XB = GE2[:, 0:4608].bitcast(BF16).rearrange("p (s a d) -> p s a d", s=6, a=3)
        stats(3)
        stats(4)
        t_rr = [root(0)]
        t_ope = put("dve", V.tensor_scalar, OPE[:, :], VEC[:, 40:41], 1.0, None, ALU.add, after=[t_vec])
        parts, tail = {}, {}
        for i in range(NT + 2):
            if i < 5:
                stats(5 + i)
            if i == 5:
                t_rr.append(root(1))
            if i < NT:
                n = rows(i)
                t = put("dve", V.tensor_scalar, XN[0:n, i, :], XA[0:n, i, :], MV[0:n, i, 0:1], RR[0:n, i:i + 1],
                        ALU.subtract, ALU.mult, after=[t_rr[i // 5]])
                t_xn.append(t)
                u = put("act", A.copy, XB[0:n, i % 6, 0, :], XN[0:n, i, :], after=[t] + t_xns[i - 6:i - 5])
                bk = i % 4
                for k in range(4):
                    p = put("pe", nc.tensor.transpose, PS[:, bk, 128 * k:128 * k + n],
                            XN[0:n, i, 128 * k:128 * k + 128], IDN[0:n, 0:n], after=[t, t_cst] + free[bk],
                            signal=(k == 3))
                pv = PS[:, bk, :].rearrange("p (k n) -> p k n", k=4)[:, :, 0:n]
                cs = slice(128 * i, 128 * i + n)
                h = put("act", A.copy, XTH[:, :, cs], pv, after=[p])
                t_ag0 = put("act", A.activation, RG[:, :, cs], pv, ACT.Copy, scale=OPE[:, 0:1], after=[p, t_ope])
                tail[i] = (bk, p, t_ag0, cs, pv)
                parts[i] = u
            q = i - 1
            if 0 <= q < NT:
                n = rows(q)
                rem = TMP[0:n, 2 + q % 2, :]
                u = put("dve", V.tensor_tensor, rem, XN[0:n, q, :], XB[0:n, q % 6, 0, :], ALU.subtract,
                        after=[parts[q]] + t_rem[q % 2])
                parts[q] = put("act", A.copy, XB[0:n, q % 6, 1, :], rem, after=[u])
                bk, p, h, cs, pv = tail[q]
                t = put("dve", V.tensor_tensor, XTL[:, :, cs], pv, XTH[:, :, cs].bitcast(F32), ALU.subtract, after=[h])
                t_xt.append((p, t))
                free[bk] = [t, t_ag0]
            q = i - 2
            if 0 <= q < NT:
                n = rows(q)
                u = put("pool", G.tensor_tensor, XB[0:n, q % 6, 2, :], TMP[0:n, 2 + q % 2, :], XB[0:n, q % 6, 1, :],
                        ALU.subtract, after=[parts[q]])
                t_rem[q % 2] = [u]
                t_xns.append(dma("sp", f"xns{q % 6}", xn_d[128 * q:128 * q + n, :],
                                 XB[0:n, q % 6, :, :].rearrange("p a d -> p (a d)"), after=[u]))
        t_nbq = put("dve", V.tensor_scalar, NBQ[:, :], bq, -1.0, None, ALU.mult, after=[t_vec])
        split_w("k", t_edges)

        t_gx, t_gdone = [], [None] * NG

        def gather(g):
            for j in range(1 if g == NG - 1 else 2):
                n = 32 if g == NG - 1 else 128
                t = dma("pool", f"gx{g % RING}", out=GX[0:n, g % RING, j, :], out_offset=None, in_=xn_d[:, :],
                        in_offset=bass.IndirectOffsetOnAxis(ap=SIDX[0:n, j, g:g + 1], axis=0), indirect=True,
                        after=(t_xns[-6:] + [t_sidx] if g < RING else [t_gdone[g - RING]]))
            t_gx.append(t)

        t_ohfree = [None, None]
        t_agg = []
        regs = {}

        def onehot(g):
            o = g % 2
            n = 32 if g == NG - 1 else 128
            nj = 1 if g == NG - 1 else 2
            return put("dve", V.tensor_tensor, OH[0:n, o, 0:nj, :],
                       DREL[0:n, 0:nj, g:g + 1].broadcast_to([n, nj, WIN]),
                       IOTA[0:n, 0:WIN].unsqueeze(1).broadcast_to([n, nj, WIN]), ALU.is_equal,
                       after=[t_drel, t_cst] + ([t_ohfree[o]] if t_ohfree[o] else []))

        t_hot = {}

        def aggregate(g):
            o = g % 2
            n = 32 if g == NG - 1 else 128
            nj = 1 if g == NG - 1 else 2
            t_oh = t_hot.pop(g)
            bk = 4 + o
            for f4 in range(4):
                for j in range(nj):
                    for a in range(3):
                        col = D * a + 128 * f4
                        p = put("pe", mm, PS[:, bk, WIN * f4:WIN * f4 + WIN], GX[0:n, g % RING, j, col:col + 128],
                                OH[0:n, o, j, :], start=(j == 0 and a == 0), stop=(j == nj - 1 and a == 2),
                                after=[t_gx[g], t_oh] + free[bk], signal=(f4 == 3 and j == nj - 1 and a == 2))
            t_gdone[g] = p
            t_ohfree[o] = p
            if g + RING < NG:
                gather(g + RING)
            if g + 2 < NG:
                t_hot[g + 2] = onehot(g + 2)

            def load(eng, g=g):
                regs[g] = eng.value_load(EROWI[0:1, g:g + 1], min_val=0, max_val=N - 1)
            pr.raw("dve", load, after=[t_erow])

            def add(bk=bk, g=g):
                win = RG[:, :, bass.ds(regs[g], WIN)]
                return V.tensor_tensor(win, PS[:, bk, 0:4 * WIN].rearrange("p (f w) -> p f w", f=4), win, ALU.add)
            t = put("dve", add, after=[p, t_ag0, t_gz] + t_agg[-1:])
            t_agg.append(t)
            free[bk] = [t]

        load_w("sp", "v")
        for g in range(RING):
            gather(g)

        mix = [0]

        def bank():
            mix[0] += 1
            return (mix[0] - 1) % 4

        t_tmp = [t_rem[0] + t_rem[1], t_rem[0] + t_rem[1]]
        t_k, t_v, t_q = [None] * NT, [None] * NT, {}

        def k_unit(i):
            n, bk, s = rows(i), bank(), i % 2
            for k in range(4):
                cs = slice(128 * i, 128 * i + n)
                p = products(PS[0:n, bk, :], XTH[:, k, cs], XTL[:, k, cs], WH["k"][:, k, :], WL["k"][:, k, :], k == 0,
                             k == 3, [t_xt[i][1], t_ws["k", k]] + free[bk], k == 3)
            u, w = TMP[0:n, 2 * s, :], TMP[0:n, 2 * s + 1, :]
            a1 = put("dve", V.tensor_tensor, u, PS[0:n, bk, :], BROW[0:n, 0, :], ALU.add,
                     after=[p, t_brow] + t_tmp[s])
            free[bk] = [a1]
            a2 = put("act", A.activation, w, u, ACT.Relu, scale=-1.0, after=[a1] + t_tmp[s])
            a3 = put("act", A.activation, w, w, ACT.Exp, scale=-1.0, after=[a2])

            def finish():
                t = put("dve", V.tensor_tensor, XA[0:n, i, :], XA[0:n, i, :], XN[0:n, i, :], ALU.add, after=[t_xn[i]])
                t = put("dve", V.tensor_tensor, XA[0:n, i, :], XA[0:n, i, :], BROW[0:n, 2, :], ALU.add,
                        after=[t, t_brow])
                t_acc.append(t)
                t_k[i] = put("dve", V.scalar_tensor_tensor, KK[0:n, i, :], u, 0.0, w, ALU.max, ALU.add,
                             after=[a3, t_xt[i][0], t_acc[i]])
                t_tmp[s] = [t_k[i]]
            return finish

        def v_unit(i):
            n, bk = rows(i), bank()
            for k in range(4):
                cs = slice(128 * i, 128 * i + n)
                p = products(PS[0:n, bk, :], XTH[:, k, cs], XTL[:, k, cs], WH["v"][:, k, :], WL["v"][:, k, :], k == 0,
                             k == 3, [t_xt[i][1], t_ws["v", k]] + free[bk], k == 3)
            t_v[i] = put("dve", V.tensor_tensor, VA[0:n, i, :, 0:128],
                         PS[0:n, bk, :].rearrange("p (r c) -> p r c", r=4),
                         BROW[0:n, 1, :].rearrange("p (r c) -> p r c", r=4), ALU.add, after=[p, t_m2])
            free[bk] = [t_v[i]]

        t_kv = [None] * 4

        def kv_unit(r):
            bk = 6 + r % 2
            o = 129 * (r // 2)
            for i in range(NT):
                n = rows(i)
                p = put("pe", mm, PS[:, bk, o:o + 129], KK[0:n, i, 128 * r:128 * r + 128], VA[0:n, i, r, :],
                        start=(i == 0), stop=(i == NT - 1), after=[t_k[i], t_v[i]] + free[bk], signal=(i == NT - 1))
            a1 = put("dve", V.tensor_tensor, KVB[:, r, :], PS[:, bk, o:o + 128], BD, ALU.mult, after=[p, t_cst])
            a2 = put("dve", V.tensor_copy, EST[:, 3:4], PS[:, bk, o + 128:o + 129], after=[p] + ([t_kv[r - 1]] if r else []))
            free[bk] = [a2]
            t_kv[r] = put("dve", V.tensor_scalar, KS8[:, r, :], M8[:, r, :], EST[:, 3:4], None, ALU.mult, after=[a1, a2])

        def q_unit(r, c):
            o, w = CH[c]
            bk, s = bank(), r % 2
            for k in range(4):
                f = slice(128 * r, 128 * r + 128)
                p = products(PS[:, bk, 0:w], WH["q"][:, k, f], WL["q"][:, k, f], XTH[:, k, o:o + w], XTL[:, k, o:o + w],
                             k == 0, k == 3, [t_xt[-1][1], t_ws["q", k]] + free[bk], k == 3)
            e1 = TMP[:, 2 * s, 0:w]
            a1 = put("act", A.activation, e1, PS[:, bk, 0:w], ACT.Relu, bias=NBQ[:, r:r + 1], scale=-1.0,
                     after=[p, t_nbq] + t_tmp[s])
            a2 = put("act", A.activation, e1, e1, ACT.Exp, scale=-1.0, after=[a1])
            a3 = put("dve", V.tensor_scalar, QT[:, r, o:o + w], PS[:, bk, 0:w], bq[:, r:r + 1], 0.0, ALU.add,
                     ALU.max, after=[p, a1] + t_kv)
            free[bk] = [a3]

            def finish():
                t_q[r, c] = put("dve", V.tensor_tensor, QT[:, r, o:o + w], QT[:, r, o:o + w], e1, ALU.add,
                                after=[a2, a3])
                t_tmp[s] = [t_q[r, c]]
            return finish

        t_o = {}

        zread = []
        t_z, t_zt = {}, [[], []]

        def z_unit(c):
            o, w = CH[c]
            bd = bank()
            for r in range(4):
                p = put("pe", mm, PS[0:8, bd, 0:w], KS8[:, r, :], QT[:, r, o:o + w], start=(r == 0), stop=(r == 3),
                        after=[t_kv[r], t_q[r, c]] + free[bd], signal=(r == 3))
            t_z[c] = put("dve", V.reciprocal, ZR[:, 0:w], PS[0:8, bd, 0:w], after=[p] + zread)
            free[bd] = [t_z[c]]

        def o_unit(r, c):
            o, w = CH[c]
            bn, bd = bank(), bank()
            p = put("pe", mm, PS[:, bn, 0:w], KVB[:, r, :], QT[:, r, o:o + w], start=True, stop=True, after=free[bn])
            p = put("pe", mm, PS[:, bd, 0:w], KSB[0:8, r, :], ZR[:, 0:w], start=True, stop=True,
                    after=[t_z[c], t_s8] + free[bd])
            zread[:] = [p]
            z = TMP[:, 1 + 2 * (r % 2), 0:w]
            a1 = put("act", A.copy, z, PS[:, bd, 0:w], after=[p] + t_zt[r % 2])
            a2 = put("dve", V.tensor_tensor, QT[:, r, o:o + w], PS[:, bn, 0:w], z, ALU.mult, after=[a1])
            t_zt[r % 2] = [a2]
            free[bd], free[bn] = [a1], [a2]
            a2 = put("dve", V.tensor_copy, OUH[:, r, o:o + w], QT[:, r, o:o + w], after=[a2])
            t_o[r, c] = put("dve", V.tensor_tensor, OUL[:, r, o:o + w], QT[:, r, o:o + w],
                            OUH[:, r, o:o + w].bitcast(F32), ALU.subtract, after=[a2])

        t_p = [None] * NT
        p_last = [None]

        def p_unit(i):
            n, bk = rows(i), bank()
            for k in range(4):
                cs = slice(128 * i, 128 * i + n)
                p = products(PS[0:n, bk, :], OUH[:, k, cs], OUL[:, k, cs], WH["p"][:, k, :], WL["p"][:, k, :], k == 0,
                             k == 3, [t_ws["p", k]] + [t_o[k, c] for c in range(3)] + free[bk], k == 3)
            t_p[i] = put("dve", V.tensor_tensor, XA[0:n, i, :], PS[0:n, bk, :], XA[0:n, i, :], ALU.add,
                         after=[p, t_acc[i]])
            free[bk] = [t_p[i]]
            p_last[0] = p

        units = [(k_unit, (i,)) for i in range(NT)] + [(v_unit, (i,)) for i in range(NT)]
        units += [(kv_unit, (r,)) for r in range(4)]
        units += [(q_unit, (r, 0)) for r in range(4)]
        for c in range(3):
            nxt = [(q_unit, (r, c + 1)) for r in range(4)] if c < 2 else []
            units += nxt[0:1] + [(z_unit, (c,))] + nxt[1:2]
            for r in range(4):
                units += [(o_unit, (r, c))] + nxt[r + 2:r + 3]
        units += [(p_unit, (i,)) for i in range(NT)]

        ra = {n: pr.sem("ra_" + n) for n in ("idx", "gx", "row", "one", "sum", "dve", "end")}
        OHW = OH[:, :, :, :].rearrange("p a b c -> p (a b c)")
        DABSf = DABS[:, :, :].rearrange("p j g -> p (j g)")
        SIDXf = SIDX[:, :, :].rearrange("p j g -> p (j g)")

        def wide(body):
            def run(eng):
                far = eng.value_load(FLAGI[0:1, 0:1], min_val=0, max_val=N)
                with eng.If(far >= WIN):
                    body(eng)
            return run

        def wide_dve(eng):
            n = [0]

            def link(ins):
                n[0] += 1
                ins.then_inc(ra["dve"], 1)
                eng.wait_ge(ra["dve"], n[0])

            link(V.memset(DABS[:, 1:2, NG - 1:NG], -4096.0))
            link(V.tensor_scalar(DABS[:, 0, NG - 1:NG], DABS[:, 0, NG - 1:NG], 4096.0, M32, ALU.add, ALU.mult))
            link(V.tensor_scalar(DABS[:, 0, NG - 1:NG], DABS[:, 0, NG - 1:NG], -4096.0, None, ALU.add))
            link(V.tensor_tensor(RG[:, :, 0:N], XTH.bitcast(F32), XTL.bitcast(F32), ALU.add))
            link(V.tensor_scalar(RG[:, :, 0:N], RG[:, :, 0:N], OPE[:, 0:1], None, ALU.mult))
            link(V.memset(RG[:, :, N:AGW], 0.0))
            eng.sem_clear(ra["dve"])
            with eng.Fori(0, 2 * NG) as i:
                n[0] = 0
                link(V.tensor_copy(DC[:, 0:1], DABSf[:, bass.ds(i, 1)]))
                V.tensor_copy(IC[:, 0:1], SIDXf[:, bass.ds(i, 1)]).then_inc(ra["idx"], 1)
                for q in range(5):
                    V.tensor_scalar(OHW, IOTA, DC[:, 0:1], None, ALU.is_equal).then_inc(ra["one"], 1)
                    link(V.tensor_scalar(DC[:, 0:1], DC[:, 0:1], -256.0, None, ALU.add))
                    eng.wait_ge(ra["sum"], q + 1)
                    if q == 4:
                        eng.sem_clear(ra["sum"])
                    win = RG[:, :, 256 * q:256 * q + 256]
                    link(V.tensor_tensor(win, PS[:, 4:6, :].rearrange("p b (f w) -> p (b f) w", f=2), win, ALU.add))
                eng.sem_clear(ra["dve"])
            V.memset(DC[:, 1:2], 0.0).then_inc(ra["end"], 1)

        def wide_pool(eng):
            with eng.Fori(0, 2 * NG):
                eng.wait_ge(ra["idx"], 1)
                eng.sem_clear(ra["idx"])
                G.indirect_dma_start(out=GX[:, 0, 0, :], out_offset=None, in_=xn_d[:, :],
                                     in_offset=bass.IndirectOffsetOnAxis(ap=IC[:, 0:1], axis=0)).then_inc(ra["gx"], 16)
                eng.drain().then_inc(ra["row"], 1)

        def wide_pe(eng):
            with eng.Fori(0, 2 * NG):
                eng.wait_ge(ra["row"], 1)
                eng.sem_clear(ra["row"])
                for q in range(5):
                    eng.wait_ge(ra["one"], q + 1)
                    if q == 4:
                        eng.sem_clear(ra["one"])
                    for f4 in range(4):
                        for a in range(3):
                            col = D * a + 128 * f4
                            last = mm(PS[:, 4 + f4 // 2, 256 * (f4 % 2):256 * (f4 % 2) + 256],
                                      GX[:, 0, 0, col:col + 128], OHW, start=(a == 0), stop=(a == 2))
                    last.then_inc(ra["sum"], 1)
            eng.wait_ge(ra["end"], 1)

        t_w1 = []
        pieces = []

        def aggregated():
            for eng, body in (("dve", wide_dve), ("pool", wide_pool), ("pe", wide_pe)):
                pr.raw(eng, wide(body), after=[t_flag, t_dabs, t_agg[-1], t_ope])
            for k in range(4):
                t_w1.append(dma("sp", f"w1{k}", W1[:, k, :], w1g[128 * k:128 * k + 128, :],
                                after=[marks["q_unit"], marks["k_unit"], t_gx[-1]]))
            pieces.extend([(split_ht, k) for k in range(4)] + [(split_w1, k) for k in range(4)])

        t_ht, t_w1s, t_w2s = [], [], []

        def split_ht(k):
            a1 = put("dve", V.tensor_copy, HTH[:, k, :], RG[:, k, 0:N], after=[t_agg[-1], marks["q_unit"], t_ag0])
            t_ht.append(put("dve", V.tensor_tensor, HTL[:, k, 0:N], RG[:, k, 0:N], HTH[:, k, :].bitcast(F32),
                            ALU.subtract, after=[a1]))

        def split_w1(k):
            a1 = put("dve", V.tensor_copy, W1H[:, k, :], W1[:, k, :], after=[t_w1[k], t_gdone[-1]])
            t_w1s.append(put("dve", V.tensor_tensor, W1L[:, k, :], W1[:, k, :], W1H[:, k, :].bitcast(F32),
                             ALU.subtract, after=[a1]))

        g, marks, late = 0, {}, None
        RATE = 1.6
        for q in range(2):
            t_hot[q] = onehot(q)
        for u, (fn, args) in enumerate(units):
            if u == 7:
                split_w("v", [])
            if u == 10:
                load_w("sp", "p", [marks["k_unit"]])
            if u == 20:
                load_w("sp", "q", [marks["v_unit"]])
            if u == 22:
                split_w("q", [marks["k_unit"]])
            if u == 34:
                split_w("p", [marks["v_unit"]])
            if late and fn in (kv_unit, z_unit, o_unit):
                late()
                late = None
            done = fn(*args)
            marks[fn.__name__] = ("pe", pr.count["pe"])
            if late:
                late()
            late = done
            if pieces:
                split, k = pieces.pop(0)
                split(k)
            while u >= 3 and g < min(NG, (u - 2) * RATE):
                aggregate(g)
                g += 1
                if g == NG:
                    aggregated()
        while g < NG:
            aggregate(g)
            g += 1
            if g == NG:
                aggregated()
        for fn, k in pieces:
            fn(k)

        t_m4 = put("pool", G.memset, ZERO, 0.0, after=[p_last[0]])

        t_w2 = dma("sp", "w2", W2, w2g.rearrange("(k p) n -> p k n", p=128), after=[p_last[0], marks["v_unit"]])

        t_yz = []
        for i in range(20):
            n = min(128, 2 * N - 128 * i)
            t_yz.append(dma("sp", "yz", y_d[128 * i:128 * i + n, :], ZERO[0:n, :], after=[t_m4]))

        loads = []

        def load_expert(buf, after):
            e = len(loads)
            if e < NEXP:
                loads.append((buf, dma("sp", f"we{e % 24}", buf, we_in[e], after=after)))

        def split_w2(k):
            a1 = put("dve", V.tensor_copy, W2H[:, k, :], W2[:, k, :], after=[t_w2, p_last[0]])
            t_w2s.append(put("dve", V.tensor_tensor, W2L[:, k, :], W2[:, k, :], W2H[:, k, :].bitcast(F32),
                             ALU.subtract, after=[a1]))

        def norm(t, s, buf, gam, bet, deps):
            for c, (o, w) in enumerate(CH):
                a1 = put("dve", V.bn_stats, BST[:, s, c, :], buf[:, o:o + w], after=[deps[c]])
            m = BMV[:, s, :]
            a1 = put("dve", V.bn_aggr, m[:, 0:2], BST[:, s, :, :].rearrange("p c k -> p (c k)"), after=[a1])
            a1 = put("dve", V.tensor_scalar, m[:, 2:3], m[:, 1:2], 1e-5, None, ALU.add, after=[a1])
            a1 = put("act", A.activation, m[:, 3:4], m[:, 2:3], ACT.Sqrt, after=[a1])
            a1 = put("dve", V.reciprocal, m[:, 4:5], m[:, 3:4], after=[a1])
            a1 = put("dve", V.tensor_tensor, m[:, 5:6], m[:, 4:5], gam, ALU.mult, after=[a1])
            a1 = put("dve", V.tensor_tensor, m[:, 6:7], m[:, 5:6], m[:, 0:1], ALU.mult, after=[a1])
            a1 = put("dve", V.tensor_tensor, m[:, 7:8], bet, m[:, 6:7], ALU.subtract, after=[a1])
            return put("act", A.activation, buf, buf, ACT.Relu, bias=m[:, 7:8], scale=m[:, 5:6], after=[a1])

        t_bmv = [[], []]
        t_h1, t_h1s, pe_h1 = [], [], []

        def split_h1(t):
            wait = [t_h1[t], t_gdone[-1], marks["p_unit"], t_k[NT - 1]]
            if t >= 4:
                wait.append(pe_h1[3 if t < 6 else 6])
            for c, (o, w) in enumerate(CH):
                a1 = put("act", A.copy, H1H[t][c], H1[:, t, o:o + w], after=wait)
                a1 = put("dve", V.tensor_tensor, H1L[:, t, o:o + w], H1[:, t, o:o + w], H1H[t][c].bitcast(F32),
                         ALU.subtract, after=[a1])
            t_h1s.append(a1)

        nb = 0
        for t in range(8):
            deps = []
            for c, (o, w) in enumerate(CH):
                bk = nb % 8
                nb += 1
                for k in range(4):
                    f = slice(128 * t, 128 * t + 128)
                    p = products(PS[:, bk, 0:w], W1H[:, k, f], W1L[:, k, f], HTH[:, k, o:o + w], HTL[:, k, o:o + w],
                                 k == 0, k == 3, [t_w1s[k], t_ht[k], t_o[3, 2], t_kv[3]] + free[bk], k == 3)
                a1 = put("act", A.activation, H1[:, t, o:o + w], PS[:, bk, 0:w], ACT.Identity, bias=b1[:, t:t + 1],
                         after=[p] + t_bmv[t % 2])
                free[bk] = [a1]
                deps.append(a1)
            t_h1.append(norm(t, t % 2, H1[:, t, :], g1[:, t:t + 1], be1[:, t:t + 1], deps))
            t_bmv[t % 2] = [t_h1[-1]]
            pe_h1.append(p)
            split_w2(t)
            if t >= 1:
                split_h1(t - 1)
        pe_w1 = p
        split_h1(7)
        t_hp = dma("sp", "hp", HP, hp_in.rearrange("(k p) n -> p k n", p=128), after=[pe_w1])
        load_expert(big(16424, 2048), [pe_w1])
        load_expert(big(18472, 2048), [pe_w1])

        t_h2 = []
        for t in range(4):
            deps = []
            f = slice(128 * t, 128 * t + 128)
            pw = {}
            for ks in (range(4), range(4, 8)):
                for c, (o, w) in enumerate(CH):
                    bk = (nb + c) % 8
                    for k in ks:
                        pw[c] = products(PS[:, bk, 0:w], W2H[:, k, f], W2L[:, k, f], H1H[k][c],
                                         H1L[:, k, o:o + w], k == 0, k == 7, [t_w2s[k], t_h1s[k]] + free[bk], k == 7)
            for c, (o, w) in enumerate(CH):
                bk = nb % 8
                nb += 1
                p = pw[c]
                a1 = put("act", A.activation, H2[:, t, o:o + w], PS[:, bk, 0:w], ACT.Identity, bias=b2[:, t:t + 1],
                         after=[p] + t_bmv[t % 2])
                free[bk] = [a1]
                deps.append(a1)
            t_h2.append(norm(t, t % 2, H2[:, t, :], g2[:, t:t + 1], be2[:, t:t + 1], deps))
            t_bmv[t % 2] = [t_h2[-1]]
        pe_w2 = p
        waiting = [big(q, 2048) for q in [*range(20544, 38976, 2048), *range(0, 10240, 2048), 14376]]

        RB = region("BROW")
        MX = RB[:, 0:320].rearrange("p (i h e) -> p i h e", i=NT, h=4)
        MI = RB[:, 320:640].bitcast(U32).rearrange("p (i h e) -> p i h e", i=NT, h=4)
        LG = RB[:, 640:1152].rearrange("p (s n) -> p s n", s=2)
        b0 = put("dve", V.tensor_copy, TRIB[:, :], TRI)
        t_rb1 = put("dve", V.memset, RB[:, 0:640], 0.0, after=[pe_w2])
        t_m5 = put("dve", V.memset, MV[:, :, :], 1.0)
        t_xx, t_xxs, t_lgf, t_best = [None] * NT, [None] * NT, [[], []], [None]
        xxr = [None] * 4
        XX = [TMP[:, 0, :], TMP[:, 1, :], XG4[:, :], KSB[:, :, :].rearrange("p r e -> p (r e)")]
        xtr = [None, None]
        st = {}

        def step_t(i):
            n, bk = rows(i), nbank()
            for k in range(4):
                p = put("pe", nc.tensor.transpose, PS[0:n, bk, 128 * k:128 * k + 128], H2[:, k, 128 * i:128 * i + n],
                        IDN, after=[t_h2[k]] + free[bk], signal=(k == 3))
            st["t", i] = (bk, p)
            return p

        def step_a(i):
            n, (bk, p) = rows(i), st["t", i]
            a1 = put("dve", V.tensor_tensor, XA[0:n, i, :], PS[0:n, bk, :], XA[0:n, i, :], ALU.add,
                     after=[p, t_p[i]])
            free[bk] = [a1]
            yield
            a1 = put("dve", V.bn_stats, ST[0:n, i, :], XA[0:n, i, :], after=[a1])
            yield
            a1 = put("dve", V.bn_aggr, MV[0:n, i, :], ST[0:n, i, :], after=[a1, t_m5])
            yield
            a1 = put("dve", V.tensor_scalar, RR[:, i:i + 1], MV[:, i, 1:2], 1e-5, None, ALU.add, after=[a1])
            st[i] = put("act", A.activation, RR[:, i:i + 1], RR[:, i:i + 1], ACT.Sqrt, after=[a1])

        nbk = [nb]

        def nbank():
            nbk[0] += 1
            return (nbk[0] - 1) % 8

        def step_b(i):
            n, s = rows(i), i % 2
            a1 = put("dve", V.reciprocal, RR[:, i:i + 1], RR[:, i:i + 1], after=[st[i]])
            wait = [a1] + (xxr[i % 4] or [])
            xx = XX[i % 4][0:n, :]
            a1 = put("dve", V.tensor_scalar, xx, XA[0:n, i, :], MV[0:n, i, 0:1], RR[0:n, i:i + 1], ALU.subtract,
                     ALU.mult, after=wait)
            t_xxs[i] = dma("sp", f"xxs{i % 4}", xx_d[128 * i:128 * i + n, :], xx, after=[a1])
            bk = nbank()
            for k in range(4):
                p = put("pe", nc.tensor.transpose, PS[:, bk, 128 * k:128 * k + n], xx[:, 128 * k:128 * k + 128],
                        IDN[0:n, 0:n], after=[a1] + free[bk], signal=(k == 3))
            xxr[i % 4] = [p, t_xxs[i]]
            xt = TMP[:, 2 + s, :].rearrange("p (k n) -> p k n", k=4)
            a2 = put("act", A.copy, xt[:, :, 0:n], PS[:, bk, :].rearrange("p (k n) -> p k n", k=4)[:, :, 0:n],
                     after=[p] + (xtr[s] or []))
            free[bk] = [a2]
            st["xt", i] = a2

        def step_c(i):
            n, s, bk = rows(i), i % 2, nbank()
            a2 = st["xt", i]
            xt = TMP[:, 2 + s, :].rearrange("p (k n) -> p k n", k=4)
            for k in range(4):
                p = put("pe", mm, PS[0:n, bk, 0:256], xt[:, k, 0:n], HP[:, k, :], start=(k == 0), stop=(k == 3),
                        after=[a2, t_hp] + free[bk], signal=(k == 3))
            xtr[s] = [p]
            a3 = put("act", A.copy, LG[0:n, s, :], PS[0:n, bk, 0:256], after=[p] + t_lgf[s])
            free[bk] = [a3]
            st["lg", i] = a3
            return p

        def step_d(i):
            n, s = rows(i), i % 2
            l = [LG[0:n, s, 64 * h:64 * h + 64] for h in range(4)]
            for h in range(4):
                a1 = put("dve", V.max, MX[0:n, i, h, :], l[h], after=[st["lg", i], t_rb1])
            yield
            for h in range(4):
                t_best[0] = put("dve", V.max_index, MI[0:n, i, h, :], MX[0:n, i, h, :], l[h], after=[a1])
                if h in (1, 2):
                    yield
            t_lgf[s] = [t_best[0]]

        for i in range(-2, NT + 3):
            if i + 2 < NT:
                p_tr = step_t(i + 2)
            if 0 <= i - 2 < NT:
                p_lg = step_c(i - 2)
            work = [step_a(i)] if 0 <= i < NT else []
            work += [step_d(i - 3)] if 0 <= i - 3 < NT else []
            while work:
                for w in list(work):
                    if next(w, "end") == "end":
                        work.remove(w)
            if 0 <= i - 1 < NT:
                step_b(i - 1)
                load_expert(waiting.pop(0), [p_tr])
        nb = nbk[0]
        for buf in waiting:
            load_expert(buf, [p_tr, p_lg])

        S1 = GE2[:, 5240:6656]
        off = [0]

        def scr(n):
            off[0] += n
            return S1[:, off[0] - n:off[0]]

        SC8 = scr(80).rearrange("p (i e) -> p i e", i=NT)
        T8 = scr(80).rearrange("p (i e) -> p i e", i=NT)
        TI = scr(80).bitcast(U32).rearrange("p (i e) -> p i e", i=NT)
        CAND = scr(40).rearrange("p (i h) -> p i h", i=NT)
        TOP = scr(20).rearrange("p (i k) -> p i k", i=NT)
        SEL = scr(20).rearrange("p (i k) -> p i k", i=NT)
        SELI = scr(20).bitcast(I32)
        ODD = scr(20)
        PAIR = scr(20)
        POS = scr(20).rearrange("p (i k) -> p i k", i=NT)
        QP = scr(20)
        OHE = RT[:, 0:640].bitcast(BF16).rearrange("p (i k e) -> p i k e", i=NT, k=2)
        OHS = scr(320).bitcast(BF16).rearrange("p (i e) -> p i e", i=NT)
        PRD = RT[:, 640:1920].rearrange("p (i k e) -> p i k e", i=NT, k=2)
        LQ = RT[:, 1920:3200].bitcast(BF16).rearrange("p (a q) -> p a q", a=20)
        RP = RT[:, 3200:3520].bitcast(BF16).rearrange("p (a r) -> p a r", a=20)
        RPH = RT[:, 3520:3840].bitcast(BF16).rearrange("p (a r) -> p a r", a=20)
        RPL = scr(320).bitcast(BF16).rearrange("p (a r) -> p a r", a=20)
        SAME = scr(10).rearrange("p (i k) -> p i k", i=NT)
        SELf = SEL.rearrange("p i k -> p (i k)")
        POSf = POS.rearrange("p i k -> p (i k)")

        w = [t_best[0]]

        def v(call, *args, after=(), **kw):
            w[0] = put("dve", call, *args, after=[w[0], *after], **kw)
            return w[0]

        v(V.memset, SC8[:, :, 4:8], -3.0e38)
        v(V.tensor_copy, SC8[:, :, 0:4], MX[:, :, :, 0])
        v(V.tensor_copy, CAND, MI[:, :, :, 0])
        top = [put("dve", V.max, T8[:, i, :], SC8[:, i, :], after=[w[0]]) for i in range(NT)]
        for i in range(NT):
            w[0] = put("dve", V.max_index, TI[:, i, :], T8[:, i, :], SC8[:, i, :], after=[top[i]])
        v(V.tensor_copy, TOP, TI[:, :, 0:2])
        EQ = T8.rearrange("p i (k h) -> p i k h", k=2)
        v(V.tensor_tensor, EQ, IOTA[:, 0:4].unsqueeze(1).unsqueeze(1).broadcast_to([128, NT, 2, 4]),
          TOP.unsqueeze(3).broadcast_to([128, NT, 2, 4]), ALU.is_equal)
        v(V.tensor_tensor, EQ, EQ, CAND.unsqueeze(2).broadcast_to([128, NT, 2, 4]), ALU.mult)
        v(V.tensor_reduce, SEL.rearrange("p i k -> p (i k)").unsqueeze(2), EQ.rearrange("p i k h -> p (i k) h"), AX.X,
          ALU.add)
        v(V.scalar_tensor_tensor, SEL, VAL.unsqueeze(2).broadcast_to([128, NT, 2]), -1000.0, SEL, ALU.mult, ALU.add)
        v(V.tensor_tensor, OHE, IOTA[:, 0:NEXP].unsqueeze(1).unsqueeze(1).broadcast_to([128, NT, 2, NEXP]),
          SEL.unsqueeze(3).broadcast_to([128, NT, 2, NEXP]), ALU.is_equal, after=[p_tr])
        a0 = v(V.tensor_tensor, OHS, OHE[:, :, 0, :], OHE[:, :, 1, :], ALU.add)
        v(V.tensor_copy, SELI, SELf)
        v(V.tensor_scalar, PAIR.bitcast(I32), SELI, 1, None, ALU.arith_shift_right)
        v(V.tensor_copy, PAIR, PAIR.bitcast(I32))
        v(V.tensor_tensor, RP, IOTA[:, 0:32].unsqueeze(1).broadcast_to([128, 20, 32]),
          PAIR.unsqueeze(2).broadcast_to([128, 20, 32]), ALU.is_equal)
        put("dve", V.tensor_scalar, ODD.bitcast(I32), SELI, 1, None, ALU.bitwise_and, after=[w[0]])
        v(V.tensor_tensor, RPH, RP, AHI.unsqueeze(2).broadcast_to([128, 20, 32]), ALU.mult)
        v(V.tensor_copy, ODD, ODD.bitcast(I32))
        v(V.tensor_tensor, RPL, RP, ALO.unsqueeze(2).broadcast_to([128, 20, 32]), ALU.mult)
        v(V.tensor_tensor, SAME, SEL[:, :, 0:1], SEL[:, :, 1:2], ALU.is_equal)
        for i in range(NT):
            bk = (nb + i // 5) % 8
            o = 64 * (i % 5)
            for j in range(i):
                put("pe", mm, PS[:, bk, o:o + 64], ONEB[:, :], OHS[:, j, :], start=(j == 0), stop=False,
                    after=[a0, t_m3] + free[bk], signal=False)
            p = put("pe", mm, PS[:, bk, o:o + 64], TRIB[:, :], OHS[:, i, :], start=(i == 0), stop=True,
                    after=[a0, b0] + free[bk])
        for h in range(2):
            bk = (nb + h) % 8
            hs = slice(5 * h, 5 * h + 5)
            before = PS[:, bk, 0:320].rearrange("p (i e) -> p i e", i=5).unsqueeze(2).broadcast_to([128, 5, 2, NEXP])
            v(V.tensor_tensor, PRD[:, hs, :, :], OHE[:, hs, :, :], before, ALU.mult, after=[p])
            free[bk] = [w[0]]
        nb += 2
        v(V.tensor_reduce, POSf.unsqueeze(2), PRD.rearrange("p i k e -> p (i k) e"), AX.X, ALU.add)
        v(V.tensor_tensor, POS[:, :, 1:2], POS[:, :, 1:2], SAME, ALU.add)
        v(V.scalar_tensor_tensor, QP, ODD, 64.0, POSf, ALU.mult, ALU.add)
        v(V.tensor_scalar, ODD, POSf, 64.0, 1000.0, ALU.is_ge, ALU.mult)
        v(V.tensor_tensor, QP, QP, ODD, ALU.add)
        bk = nb % 8
        nb += 1
        for h in range(2):
            hs = slice(10 * h, 10 * h + 10)
            v(V.tensor_tensor, LQ[:, hs, :], IOTA[:, 0:128].unsqueeze(1).broadcast_to([128, 10, 128]),
              QP[:, hs].unsqueeze(2).broadcast_to([128, 10, 128]), ALU.is_equal)
            for j in range(10 * h, 10 * h + 10):
                put("pe", mm, PS[:, bk, 0:32], LQ[:, j, :], RPH[:, j, :], start=(j == 0), stop=False,
                    after=[w[0]] + free[bk], signal=False)
                p = put("pe", mm, PS[:, bk, 0:32], LQ[:, j, :], RPL[:, j, :], start=False, stop=(j == 19))
        v(V.tensor_scalar, TIDX[:, :], PS[:, bk, 0:32], 1.0, -1.0, ALU.max, ALU.add, after=[p])
        t_tidx = v(V.tensor_scalar, TIDX[:, :], TIDX[:, :], 1, None, ALU.arith_shift_right)
        v(V.tensor_scalar, VIDX[:, 1, :], PS[:, bk, 0:32], 0.5, 8192.0, ALU.is_lt, ALU.mult)
        t_scidx = v(V.scalar_tensor_tensor, SCIDX[:, :], PS[:, bk, 0:32], -1.0, VIDX[:, 1, :], ALU.add, ALU.add)
        free[bk] = [t_scidx]
        p_idx = p
        a0 = v(V.tensor_reduce, EST[:, 3:4], POSf, AX.X, ALU.max)
        bk = nb % 8
        nb += 1
        p = put("pe", nc.tensor.transpose, PS[0:1, bk, 0:128], EST[:, 3:4], IDN, after=[a0] + free[bk])
        a0 = put("dve", V.tensor_reduce, FLAG[0:1, 1:2], PS[0:1, bk, 0:128], AX.X, ALU.max, after=[p])
        free[bk] = [a0]
        t_full = put("dve", V.tensor_copy, FLAGI[0:1, 1:2], FLAG[0:1, 1:2], after=[a0])

        RT5 = [RT[:, q:q + D] for q in range(0, 4096, D)]
        XG = [TMP[:, 0, :], TMP[:, 1, :], TMP[:, 2, :], XG4[:, :], *RT5[0:NX - 4]]
        HG = S1[:, 900:1412].rearrange("p (s d) -> p s d", s=2)
        HT = TMP[:, 3, :].rearrange("p (s d) -> p s d", s=2)
        XTT = [a[:, :, :].rearrange("p r e -> p (r e)") for a in (KSB, KVB)]
        YS = [BROW[:, 0, :], BROW[:, 1, :], BROW[:, 2, :], *RT5[NX - 4:NX + NY - 7]]
        t_xg, xg_free = {}, {}

        def gather_pair(r):
            s = r % NX
            t_xg[r] = dma("pool", f"xg{s}", out=XG[s], out_offset=None, in_=xx_d[:, :],
                          in_offset=bass.IndirectOffsetOnAxis(ap=TIDX[:, r:r + 1], axis=0), indirect=True,
                          after=[t_tidx, *t_xxs[-4:], p_lg, p_tr, p_idx] + ([xg_free[r - NX]] if r >= NX else []))

        for r in range(NX):
            gather_pair(r)
        st2 = {}

        def tr(r):
            s, bk = r % 2, r % 2
            for k in range(4):
                p = put("pe", nc.tensor.transpose, PS[:, bk, 128 * k:128 * k + 128], XG[r % NX][:, 128 * k:128 * k + 128],
                        IDN, after=[t_xg[r]] + free[bk], signal=(k == 3))
            xg_free[r] = p
            a1 = put("act", A.copy, XTT[s][:, :], PS[:, bk, :],
                     after=[p] + ([st2["h", r - 2][1]] if r >= 2 else [t_yz[-1]]))
            free[bk] = [a1]
            st2["x", r] = a1

        def up(r):
            s, bk = r % 2, 2 + r % 2
            for k in range(4):
                for j in range(2):
                    buf, t_e = loads[2 * r + j]
                    p = put("pe", mm, PS[64 * j:64 * j + 64, bk, 0:256], XTT[s][:, 128 * k + 64 * j:128 * k + 64 * j + 64],
                            buf[:, 256 * k:256 * k + 256], start=(k == 0), stop=(k == 3),
                            after=[t_e, st2["x", r]] + free[bk], signal=(j == 1 and k == 3))
            a1 = put("act", A.activation, HG[:, s, :], PS[:, bk, 0:256], ACT.Gelu,
                     after=[p] + ([st2["g", r - 2][1]] if r >= 2 else []))
            free[bk] = [a1]
            st2["h", r] = (a1, p)

        def hidden(r):
            s, bk = r % 2, 6 + r % 2
            for f2 in range(2):
                p = put("pe", nc.tensor.transpose, PS[:, bk, 128 * f2:128 * f2 + 128], HG[:, s, 128 * f2:128 * f2 + 128],
                        IDN, after=[st2["h", r][0]] + free[bk], signal=(f2 == 1))
            a1 = put("dve", V.tensor_copy, HT[:, s, :], PS[:, bk, 0:256],
                     after=[p] + ([st2["y", r - 2]] if r >= 2 else []))
            free[bk] = [a1]
            st2["g", r] = (a1, p)

        t_ys = {}
        t_sc = []

        def down(r):
            s, bk = r % 2, 4 + r % 2
            for f2 in range(2):
                for j in range(2):
                    buf, t_e = loads[2 * r + j]
                    p = put("pe", mm, PS[64 * j:64 * j + 64, bk, :],
                            HT[:, s, 128 * f2 + 64 * j:128 * f2 + 64 * j + 64],
                            buf[:, 1024 + 512 * f2:1024 + 512 * f2 + 512], start=(f2 == 0), stop=(f2 == 1),
                            after=[st2["g", r][0]] + free[bk], signal=(j == 1 and f2 == 1))
            st2["y", r] = p
            a1 = put("dve", V.tensor_copy, YS[r % NY], PS[:, bk, :],
                     after=[p] + ([t_ys[r - NY]] if r >= NY else []))
            free[bk] = [a1]
            t_ys[r] = dma("pool", f"ys{r % NY}", out=y_d[:, :], out_offset=bass.IndirectOffsetOnAxis(
                ap=SCIDX[:, r:r + 1], axis=0), in_=YS[r % NY], in_offset=None, bounds_check=2 * N - 1,
                oob_is_err=False, indirect=True, after=[a1, t_scidx, t_yz[-1]])
            for j in range(2):
                load_expert(loads[2 * r + j][0], [p])

        tr(0)
        for r in range(32):
            if r + 1 < 32:
                tr(r + 1)
            up(r)
            if r + NX < 32:
                gather_pair(r + NX)
            if r >= 2:
                down(r - 1)
            hidden(r)
            if r == 0:
                down(0)
        down(31)

        M2 = CAP - 64
        fu = {n: pr.sem("fu_" + n) for n in
              ("load", "idx", "w", "row", "xt", "xc", "up", "gelu", "down", "yc", "sc", "xg", "ys", "hid", "dve", "tab", "end")}
        L2 = RH[:, 0:20 * M2].rearrange("p (a q) -> p a q", a=20)
        R2 = RH[:, 2048:2048 + 20 * NEXP].rearrange("p (a e) -> p a e", a=20)
        V2 = RH[0:M2, 4096:4096 + NEXP]
        V3 = RH[0:M2, 4160:4160 + NEXP]
        T2 = RH[0:M2, 4224:4224 + NEXP].bitcast(I32)
        S2 = RH[0:M2, 4288:4288 + NEXP].bitcast(I32)
        IT, IS = RH[0:M2, 4352:4353].bitcast(I32), RH[0:M2, 4353:4354].bitcast(I32)

        def full(body):
            def run(eng):
                most = eng.value_load(FLAGI[0:1, 1:2], min_val=0, max_val=2 * N)
                with eng.If(most >= 64):
                    body(eng)
            return run

        def take(eng, name, value):
            eng.wait_ge(fu[name], value)
            eng.sem_clear(fu[name])

        def full_dve(eng):
            n = [0]

            def link(ins):
                n[0] += 1
                ins.then_inc(fu["dve"], 1)
                eng.wait_ge(fu["dve"], n[0])

            link(V.tensor_scalar(QP, POSf, -64.0, None, ALU.add))
            link(V.tensor_tensor(L2, IOTA[:, 0:M2].unsqueeze(1).broadcast_to([128, 20, M2]),
                                 QP.unsqueeze(2).broadcast_to([128, 20, M2]), ALU.is_equal))
            link(V.tensor_tensor(R2, IOTA[:, 0:NEXP].unsqueeze(1).broadcast_to([128, 20, NEXP]),
                                 SELf.unsqueeze(2).broadcast_to([128, 20, NEXP]), ALU.is_equal))
            link(V.tensor_tensor(R2, R2, AID.unsqueeze(2).broadcast_to([128, 20, NEXP]), ALU.mult))
            V.memset(DC[:, 0:1], 0.0).then_inc(fu["tab"], 1)
            take(eng, "up", 1)
            link(V.tensor_copy(V2, PS[0:M2, 0, 0:NEXP]))
            link(V.tensor_scalar(V3, V2, 1.0, -1.0, ALU.max, ALU.add))
            link(V.tensor_copy(T2, V3))
            link(V.tensor_scalar(T2, T2, 1, None, ALU.arith_shift_right))
            link(V.tensor_scalar(V3, V2, 0.5, 8192.0, ALU.is_lt, ALU.mult))
            link(V.scalar_tensor_tensor(V3, V2, -1.0, V3, ALU.add, ALU.add))
            link(V.tensor_copy(S2, V3))
            eng.sem_clear(fu["dve"])
            with eng.Fori(0, NEXP) as e:
                n[0] = 0
                link(V.tensor_copy(IT, T2[:, bass.ds(e, 1)]))
                link(V.tensor_copy(IS, S2[:, bass.ds(e, 1)]))
                eng.sem_clear(fu["dve"])
                V.memset(DC[:, 0:1], 0.0).then_inc(fu["load"], 1)
                V.memset(DC[:, 1:2], 0.0).then_inc(fu["idx"], 1)
                take(eng, "xt", 1)
                V.tensor_copy(XTT[0][:, :].rearrange("p (k n) -> p k n", k=4)[:, :, 0:M2],
                              PS[:, 0, :].rearrange("p (k n) -> p k n", k=4)[:, :, 0:M2]).then_inc(fu["xc"], 1)
                take(eng, "down", 1)
                V.tensor_copy(YS[0][0:M2, :], PS[0:M2, 4, :]).then_inc(fu["yc"], 1)
                take(eng, "sc", 1)
            V.memset(DC[:, 1:2], 0.0).then_inc(fu["end"], 1)

        def full_pool(eng):
            with eng.Fori(0, NEXP):
                take(eng, "idx", 1)
                G.indirect_dma_start(out=XG[0][0:M2, :], out_offset=None, in_=xx_d[:, :],
                                     in_offset=bass.IndirectOffsetOnAxis(ap=IT, axis=0)).then_inc(fu["xg"], 16)
                eng.drain().then_inc(fu["row"], 1)
                take(eng, "yc", 1)
                G.indirect_dma_start(out=y_d[:, :], out_offset=bass.IndirectOffsetOnAxis(ap=IS, axis=0),
                                     in_=YS[0][0:M2, :], in_offset=None, bounds_check=2 * N - 1,
                                     oob_is_err=False).then_inc(fu["ys"], 16)
                eng.drain().then_inc(fu["sc"], 1)

        def full_sp(eng):
            with eng.Fori(0, NEXP) as e:
                take(eng, "load", 1)
                eng.dma_start(EX[:, :], we_in[bass.ds(e, 1), :, :].rearrange("a p n -> (a p) n")).then_inc(fu["w"], 16)
            take(eng, "end", 1)

        def full_act(eng):
            with eng.Fori(0, NEXP):
                take(eng, "gelu", 1)
                A.activation(HT[:, 0, 0:2 * M2], PS[:, 2, 0:2 * M2], ACT.Gelu).then_inc(fu["hid"], 1)

        def full_pe(eng):
            take(eng, "tab", 1)
            for j in range(20):
                last = mm(PS[0:M2, 0, 0:NEXP], L2[:, j, :], R2[:, j, :], start=(j == 0), stop=(j == 19))
            last.then_inc(fu["up"], 1)
            with eng.Fori(0, NEXP):
                take(eng, "row", 1)
                for k in range(4):
                    last = nc.tensor.transpose(PS[:, 0, 128 * k:128 * k + M2], XG[0][0:M2, 128 * k:128 * k + 128],
                                               IDN[0:M2, 0:M2])
                last.then_inc(fu["xt"], 1)
                take(eng, "xc", 1)
                take(eng, "w", 16)
                for f2 in range(2):
                    for k in range(4):
                        last = mm(PS[:, 2, M2 * f2:M2 * f2 + M2], EX[:, 256 * k + 128 * f2:256 * k + 128 * f2 + 128],
                                  XTT[0][:, 128 * k:128 * k + M2], start=(k == 0), stop=(k == 3))
                last.then_inc(fu["gelu"], 1)
                take(eng, "hid", 1)
                for f2 in range(2):
                    last = mm(PS[0:M2, 4, :], HT[:, 0, M2 * f2:M2 * f2 + M2],
                              EX[:, 1024 + 512 * f2:1024 + 512 * f2 + 512], start=(f2 == 0), stop=(f2 == 1))
                last.then_inc(fu["down"], 1)

        for eng, body in (("sp", full_sp), ("dve", full_dve), ("act", full_act), ("pool", full_pool), ("pe", full_pe)):
            pr.raw(eng, full(body), after=[t_full, st2["y", 31], *[t_ys[r] for r in range(32 - NY, 32)]])

        YL = RH[:, 0:10240].rearrange("p (i a d) -> p i a d", i=NT, a=2)
        yv = y_d.rearrange("(t a) d -> t a d", a=2)
        t_out = []
        lastp = st2["y", 31]
        for i in range(NT):
            n = rows(i)
            t = dma("sp", f"yl{i}", YL[0:n, i, :, :], yv[128 * i:128 * i + n, :, :],
                    after=[*[t_ys[r] for r in range(32 - NY, 32)], lastp])
            a1 = put("dve", V.tensor_tensor, YL[0:n, i, 0, :], YL[0:n, i, 0, :], YL[0:n, i, 1, :], ALU.add, after=[t])
            a1 = put("dve", V.scalar_tensor_tensor, YL[0:n, i, 0, :], YL[0:n, i, 0, :], 0.5, XA[0:n, i, :], ALU.mult,
                     ALU.add, after=[a1])
            t_out.append(dma("act", "out", out[128 * i:128 * i + n, :], YL[0:n, i, 0, :], after=[a1]))
        pr.raw("act", lambda e: None, after=[t_out[-1], *t_xns[-6:], *t_xxs[-4:], t_yz[-1]])

        block = ctx.enter_context(nc.Block())
        block.sync(lambda eng: pr.replay("sp", eng))
        block.gpsimd(lambda eng: pr.replay("pool", eng))
        block.scalar(lambda eng: pr.replay("act", eng))
        block.vector(lambda eng: pr.replay("dve", eng))
        block.tensor(lambda eng: pr.replay("pe", eng))


def constants(np):
    c = np.zeros((128, 743), np.float32)
    p = np.arange(128)
    c[:, 0:128] = np.eye(128)
    c[:, 128:256] = p[:, None] < p[None, :]
    c[:, 256:512] = np.arange(256)[None, :]
    c[:, 512:640] = (p[:, None] // 64) == (p[None, :] // 64)
    c[:, 670] = p < 32
    for q in range(128):
        for r in range(4):
            c[q, 671 + 8 * r + 2 * r + q // 64] = 1
    for i in range(NT):
        c[:, 640 + i] = (128 * i + p) >= N
        for k in range(2):
            v = 2 * (128 * i + p) + k + 1
            c[:, 650 + 2 * i + k] = v
            c[:, 703 + 2 * i + k] = v // 16 * 16
            c[:, 723 + 2 * i + k] = v % 16
    return c


def kernel(**inputs):
    import numpy as np
    import concourse.bacc as _bacc
    from concourse import mybir as _mybir
    from concourse.bass_utils import run_bass_kernel_spmd as _run

    g = {k: np.asarray(v) for k, v in inputs.items()}

    def edges(a, mode):
        a = np.pad(a, (0, NG * GE - NE), mode=mode)
        return np.ascontiguousarray(a.reshape(NG, GE))

    def cols(a):
        return a.reshape(-1, 128).T

    vec = np.concatenate([cols(g["L0_gnn_b1"]), cols(g["L0_gnn_g1"]), cols(g["L0_gnn_be1"]), cols(g["L0_gnn_b2"]),
                          cols(g["L0_gnn_g2"]), cols(g["L0_gnn_be2"]), cols(g["L0_mix_bq"]),
                          np.broadcast_to(g["L0_gnn_eps"].reshape(1, 1), (128, 1))], axis=1)
    brow = np.concatenate([np.broadcast_to(g[k][None, :], (128, D)) for k in ("L0_mix_bk", "L0_mix_bv", "L0_mix_bp")],
                          axis=1)
    we = np.concatenate([
        g["L0_ffn_W1"].reshape(NEXP, 4, 128, 256).transpose(0, 2, 1, 3).reshape(NEXP, 128, 1024),
        g["L0_ffn_W2"].reshape(NEXP, 2, 128, 512).transpose(0, 2, 1, 3).reshape(NEXP, 128, 1024)], axis=2)
    arrays = {
        "x": g["x"], "src": edges(g["src"], "constant"), "dst": edges(g["dst"], "edge"),
        "w1g": g["L0_gnn_W1"], "w2g": g["L0_gnn_W2"],
        "wqkvp": np.stack([g["L0_mix_Wk"], g["L0_mix_Wv"], g["L0_mix_Wq"], g["L0_mix_Wp"]]),
        "hp": g["L0_ffn_hash_proj"].transpose(1, 0, 2).reshape(D, 256),
        "vec": vec, "brow": brow, "cst": constants(np), "we": we,
    }
    nc = _bacc.Bacc("TRN2", target_bir_lowering=False, num_devices=1)
    ins, args = {}, []
    for name, a in arrays.items():
        a = np.ascontiguousarray(a)
        ins[f"in_{name}"] = a
        args.append(nc.dram_tensor(f"in_{name}", a.shape, _mybir.dt.from_np(a.dtype), kind="ExternalInput").ap())
    out = nc.dram_tensor("out_0", (N, D), _mybir.dt.float32, kind="ExternalOutput").ap()
    gnn_mix_moe(nc, *args, out)
    r = _run(nc, [ins], core_ids=[0])
    return r.results[0]["out_0"]
```
